# Optimizing a Trainium2 kernel written in Bass

```python
import numpy as np
import jax
import jax.numpy as jnp

def _softmax(x, axis=-1):
    return jax.nn.softmax(x, axis=axis)

def _gelu(x):
    return jax.nn.gelu(x, approximate=True)

def _silu(x):
    return jax.nn.silu(x)

def _sigmoid(x):
    return jax.nn.sigmoid(x)

def _layernorm(x, axis=-1, eps=1e-05):
    m = jnp.mean(x, axis=axis, keepdims=True)
    v = jnp.var(x, axis=axis, keepdims=True)
    return (x - m) / jnp.sqrt(v + eps)

def _scatter_add(tgt, idx, src, axis=0):
    return tgt.at[idx].add(src)

def _segment_sum(src, seg, n):
    return jax.ops.segment_sum(src, seg, n)
kernel_name = 'mk_sandwich_d1_jaxref_r8_7c907a'

def setup_inputs(seed: int=0):
    np.random.seed(seed)
    _w = jnp.asarray

    def _L0_attn_setup():
        import jax, jax.numpy as jnp
        import numpy as np
        B, N, C = (32, 64, 128)
        H = 16
        D = C // H
        MAX_SEQ = 64
        BASE = 10000.0

        def _rope_tables(n, d):
            position = jnp.arange(n, dtype=jnp.float32)[:, None]
            div_term = jnp.exp(jnp.arange(0, d, 2, dtype=jnp.float32) * (-np.log(BASE) / d))
            ang = position * div_term
            return (jnp.sin(ang), jnp.cos(ang))

        def _apply_rope(x, sin, cos):
            x1 = x[..., ::2]
            x2 = x[..., 1::2]
            out = jnp.stack([x1 * cos - x2 * sin, x1 * sin + x2 * cos], axis=-1)
            return out.reshape(*x.shape[:-1], -1)
        key = jax.random.key(seed)
        k1, k2, k3, k4, k5 = jax.random.split(key, 5)
        s = 0.02
        return {'x': jax.random.normal(k1, (B, N, C), dtype=jnp.float32), 'w_qkv': jax.random.normal(k2, (3 * C, C), dtype=jnp.float32) * s, 'b_qkv': jax.random.normal(k3, (3 * C,), dtype=jnp.float32) * s, 'w_lepe': jax.random.normal(k4, (C, 1, 3), dtype=jnp.float32) * s, 'b_lepe': jax.random.normal(k5, (C,), dtype=jnp.float32) * s}
    _L0_attn_in = _L0_attn_setup()

    def _L0_ffn_setup():
        import jax, jax.numpy as jnp
        import numpy as np
        E = 8
        TOP_K = 2
        ROUTE_SCALE = 1.0
        ALPHA = 1.702
        LIMIT = 7.0
        D = 128
        F = 128
        B, S = (2, 128)

        def swiglu(h):
            g = jnp.minimum(h[..., ::2], LIMIT)
            l = jnp.clip(h[..., 1::2], -LIMIT, LIMIT)
            return g * jax.nn.sigmoid(ALPHA * g) * (l + 1.0)
        if __name__ == '__main__':
            out = reference(**setup_inputs())
            print(out.shape, out.dtype)
        key = jax.random.key(seed)
        ks = jax.random.split(key, 16)
        sd = 1.0 / np.sqrt(D)
        sf = 1.0 / np.sqrt(F)
        return {'x': jax.random.normal(ks[0], (B, S, D), jnp.float32), 'gate_w': jax.random.normal(ks[1], (E, D), jnp.float32) * sd, 'gate_b': jax.random.normal(ks[2], (E,), jnp.float32) * 0.01, 'w1': jax.random.normal(ks[3], (E, 2 * F, D), jnp.float32) * sd, 'b1': jax.random.normal(ks[4], (E, 2 * F), jnp.float32) * 0.01, 'w3': jax.random.normal(ks[5], (E, 2 * F, D), jnp.float32) * sd, 'b3': jax.random.normal(ks[6], (E, 2 * F), jnp.float32) * 0.01, 'w2': jax.random.normal(ks[7], (E, D, F), jnp.float32) * sf, 'b2': jax.random.normal(ks[8], (E, D), jnp.float32) * 0.01, 'sw1': jax.random.normal(ks[9], (2 * F, D), jnp.float32) * sd, 'sb1': jax.random.normal(ks[10], (2 * F,), jnp.float32) * 0.01, 'sw3': jax.random.normal(ks[11], (2 * F, D), jnp.float32) * sd, 'sb3': jax.random.normal(ks[12], (2 * F,), jnp.float32) * 0.01, 'sw2': jax.random.normal(ks[13], (D, F), jnp.float32) * sf, 'sb2': jax.random.normal(ks[14], (D,), jnp.float32) * 0.01}
    _L0_ffn_in = _L0_ffn_setup()
    _d = {'L0_attn_x': _L0_attn_in['x'], 'L0_attn_w_qkv': _L0_attn_in['w_qkv'], 'L0_attn_b_qkv': _L0_attn_in['b_qkv'], 'L0_attn_w_lepe': _L0_attn_in['w_lepe'], 'L0_attn_b_lepe': _L0_attn_in['b_lepe'], 'L0_ffn_gate_w': _L0_ffn_in['gate_w'], 'L0_ffn_gate_b': _L0_ffn_in['gate_b'], 'L0_ffn_w1': _L0_ffn_in['w1'], 'L0_ffn_b1': _L0_ffn_in['b1'], 'L0_ffn_w3': _L0_ffn_in['w3'], 'L0_ffn_b3': _L0_ffn_in['b3'], 'L0_ffn_w2': _L0_ffn_in['w2'], 'L0_ffn_b2': _L0_ffn_in['b2'], 'L0_ffn_sw1': _L0_ffn_in['sw1'], 'L0_ffn_sb1': _L0_ffn_in['sb1'], 'L0_ffn_sw3': _L0_ffn_in['sw3'], 'L0_ffn_sb3': _L0_ffn_in['sb3'], 'L0_ffn_sw2': _L0_ffn_in['sw2'], 'L0_ffn_sb2': _L0_ffn_in['sb2']}
    _x0 = _d['L0_attn_x']
    _d['L0_attn_x'] = jax.random.normal(jax.random.fold_in(jax.random.key(seed), 1), (16, 512, 128), dtype=_x0.dtype)
    del _x0
    return _d

def reference(L0_attn_x, L0_attn_w_qkv, L0_attn_b_qkv, L0_attn_w_lepe, L0_attn_b_lepe, L0_ffn_gate_w, L0_ffn_gate_b, L0_ffn_w1, L0_ffn_b1, L0_ffn_w3, L0_ffn_b3, L0_ffn_w2, L0_ffn_b2, L0_ffn_sw1, L0_ffn_sb1, L0_ffn_sw3, L0_ffn_sb3, L0_ffn_sw2, L0_ffn_sb2):

    def _L0_attn_ref(x, w_qkv, b_qkv, w_lepe, b_lepe):
        import jax, jax.numpy as jnp
        import numpy as np
        B, N, C = (32, 64, 128)
        H = 16
        D = C // H
        MAX_SEQ = 64
        BASE = 10000.0

        def _rope_tables(n, d):
            position = jnp.arange(n, dtype=jnp.float32)[:, None]
            div_term = jnp.exp(jnp.arange(0, d, 2, dtype=jnp.float32) * (-np.log(BASE) / d))
            ang = position * div_term
            return (jnp.sin(ang), jnp.cos(ang))

        def _apply_rope(x, sin, cos):
            x1 = x[..., ::2]
            x2 = x[..., 1::2]
            out = jnp.stack([x1 * cos - x2 * sin, x1 * sin + x2 * cos], axis=-1)
            return out.reshape(*x.shape[:-1], -1)
        b, n, c = x.shape
        scale = 1.0 / np.sqrt(D)
        sin, cos = _rope_tables(n, D)
        qkv = (x @ w_qkv.T + b_qkv).reshape(b, n, 3, H, D).transpose(2, 0, 3, 1, 4)
        q, k, v = (qkv[0], qkv[1], qkv[2])
        q = jax.nn.elu(q) + 1.0
        k = jax.nn.elu(k) + 1.0
        q = _apply_rope(q, sin, cos)
        k = _apply_rope(k, sin, cos)
        attn = jnp.einsum('bhnd,bhmd->bhnm', q, k) * scale
        attn = jax.nn.softmax(attn, axis=-1)
        attn_out = jnp.einsum('bhnm,bhmd->bhnd', attn, v)
        attn_out = attn_out.transpose(0, 2, 1, 3).reshape(b, n, c)
        v_conv = v.transpose(0, 2, 1, 3).reshape(b, n, c).transpose(0, 2, 1)
        lepe = jax.lax.conv_general_dilated(v_conv, w_lepe, window_strides=(1,), padding=((1, 1),), dimension_numbers=('NCH', 'OIH', 'NCH'), feature_group_count=c) + b_lepe[None, :, None]
        lepe = lepe.transpose(0, 2, 1)
        return attn_out + lepe

    def _L0_ffn_ref(x, gate_w, gate_b, w1, b1, w3, b3, w2, b2, sw1, sb1, sw3, sb3, sw2, sb2):
        import jax, jax.numpy as jnp
        import numpy as np
        E = 8
        TOP_K = 2
        ROUTE_SCALE = 1.0
        ALPHA = 1.702
        LIMIT = 7.0
        D = 128
        F = 128
        B, S = (2, 128)

        def swiglu(h):
            g = jnp.minimum(h[..., ::2], LIMIT)
            l = jnp.clip(h[..., 1::2], -LIMIT, LIMIT)
            return g * jax.nn.sigmoid(ALPHA * g) * (l + 1.0)
        if __name__ == '__main__':
            out = reference(**setup_inputs())
            print(out.shape, out.dtype)
        inp_shape = x.shape
        xt = x.reshape(-1, D)
        logits = xt @ gate_w.T
        scores = jax.nn.softmax(logits.astype(jnp.float32), axis=-1)
        biased = scores + gate_b.astype(jnp.float32)
        idx = jax.lax.top_k(biased, TOP_K)[1]
        weights = (jnp.take_along_axis(scores, idx, axis=-1) * ROUTE_SCALE).astype(x.dtype)
        cw = jnp.sum(jax.nn.one_hot(idx, E, dtype=x.dtype) * weights[..., None], axis=1)
        h1 = jnp.einsum('td,efd->etf', xt, w1) + b1[:, None, :]
        h3 = jnp.einsum('td,efd->etf', xt, w3) + b3[:, None, :]
        a = swiglu(h1 * h3)
        y = jnp.einsum('etf,edf->etd', a, w2) + b2[:, None, :]
        routed = jnp.einsum('te,etd->td', cw, y)
        sh = swiglu((xt @ sw1.T + sb1) * (xt @ sw3.T + sb3))
        shared = sh @ sw2.T + sb2
        return (routed + shared).reshape(inp_shape)
    x = L0_attn_x
    x = x + _layernorm(_L0_attn_ref(_layernorm(x, axis=-1), L0_attn_w_qkv, L0_attn_b_qkv, L0_attn_w_lepe, L0_attn_b_lepe), axis=-1)
    x = x + _layernorm(_L0_ffn_ref(_layernorm(x, axis=-1), L0_ffn_gate_w, L0_ffn_gate_b, L0_ffn_w1, L0_ffn_b1, L0_ffn_w3, L0_ffn_b3, L0_ffn_w2, L0_ffn_b2, L0_ffn_sw1, L0_ffn_sb1, L0_ffn_sw3, L0_ffn_sb3, L0_ffn_sw2, L0_ffn_sb2), axis=-1)
    return x

_drawn_inputs = setup_inputs


def setup_inputs(seed=0):
    import zlib

    import numpy as np

    out = dict(_drawn_inputs(seed))
    spreads = {}
    factors = {'L0_ffn_b1': 8.0,
     'L0_ffn_b3': 8.0,
     'L0_ffn_b2': 22.67,
     'L0_ffn_sb1': 8.0,
     'L0_ffn_sb3': 8.0,
     'L0_ffn_sb2': 8.0}
    for name, (base, spread) in spreads.items():
        noise = np.random.default_rng([zlib.crc32(name.encode()), seed]).standard_normal(out[name].shape)
        drawn = base * np.exp(spread * noise) if base else spread * noise
        out[name] = jnp.asarray(drawn.astype(out[name].dtype))
    for name, factor in factors.items():
        out[name] = (out[name] * factor).astype(out[name].dtype)
    return out
```

```python
import concourse.bass as bass
from concourse import mybir
from contextlib import ExitStack

F32 = mybir.dt.float32
F32R = mybir.dt.float32r
BF16 = mybir.dt.bfloat16
I32 = mybir.dt.int32
U32 = mybir.dt.uint32
ALU = mybir.AluOpType
ACT = mybir.ActivationFunctionType
AX = mybir.AxisListType

P = 128
B, N, C = 16, 512, 128
H, D = 16, 8
QC = N // P
NE, TOPK, F = 8, 2, 128
EXP_ALL = NE + 1
ALPHA, LIMIT, EPS = 1.702, 7.0, 1e-5
SCALE = 1.0 / (D ** 0.5)

PARTS = 3
ROWS_QK = PARTS * PARTS * D
ROWS_ALL = ROWS_QK + PARTS
QPARTS = 2 * PARTS - 1
HALF = H // 2
HG = 4
VW = 32
FIRST = 3
SLOTS = H


class Batch:

    def __init__(self, i, c):
        self.i, self.c = i, c

    def __add__(self, k):
        return Batch(self.i, self.c + k)

    def number(self):
        return self.c if isinstance(self.i, int) else self.i * 2 + self.c

    @property
    def par(self):
        return self.c % 2

    @property
    def live(self):
        return not isinstance(self.i, int) or 0 <= self.c < B

    def done(self, per, extra=0):
        if isinstance(self.i, int):
            return self.c * per + extra
        return self.i * (2 * per) + (self.c * per + extra)

    def done_par(self, per):
        return (self.i + (self.c // 2 + 1)) * per


def due(count):
    return not isinstance(count, int) or count > 0


def attention(nc, x_in, wqkvT, chan, bv, rope_cos, rope_sin, perm, ident, X, load_weights):
    nc.disable_value_cache = True
    es = ExitStack()
    with es:
        def sb(name, shape, dt):
            return es.enter_context(nc.sbuf_tensor(name, shape, dt))

        def sem(name):
            return es.enter_context(nc.semaphore(name))

        WQKV = sb("WQKV", [P, 3 * C], F32)
        PERM = sb("PERM", [P, P], F32)
        IDF = sb("IDF", [P, P], F32)
        IDB = sb("IDB", [P, P], BF16)
        CHAN = sb("CHAN", [P, 7], F32)
        BP1 = sb("BP1", [P, 2], F32)
        BV = sb("BV", [P, C], F32)
        COS = sb("COS", [P, N], F32)
        SIN = sb("SIN", [P, N], F32)
        NHALF = sb("NHALF", [P, QC], F32)
        ST0 = sb("ST0", [P, QC, 6], F32)
        MV0 = sb("MV0", [P, QC, 2], F32)
        VE0 = sb("VE0", [P, QC], F32)
        RS0 = sb("RS0", [P, QC], F32)
        XN = sb("XN", [P, QC, C], F32)
        ST1 = sb("ST1", [P, QC, 6], F32)
        MV1 = sb("MV1", [P, QC, 2], F32)
        VE1 = sb("VE1", [P, QC], F32)
        RS1 = sb("RS1", [P, QC], F32)
        Y = sb("Y", [P, 2, QC, C], F32)
        Z = sb("Z", [P, QC, C], F32)
        REC = sb("REC", [P, QC, HG], F32)
        MX = sb("MX", [P, QC, H], F32)
        MP = sb("MP", [P, 2, QC, PARTS, HALF], BF16)
        MR = sb("MR", [P, 2, QC, HALF], F32)
        XT = sb("XT", [P, 2, N], F32)
        EXQ = sb("EXQ", [P, 2, N], F32)
        EL = sb("EL", [P, 2, N], F32)
        ROT = sb("ROT", [P, 2, N], F32)
        RES = sb("RES", [P, 2, N], F32)
        PT = sb("PT", [P, 2, PARTS, N], BF16)
        VT = sb("VT", [P, N + 2], F32)
        LP = sb("LP", [P, 2, N], F32)
        MT = sb("MT", [PARTS * HALF, 2, N], BF16)
        QS = [sb(f"QS{i}", [P, H, N], BF16) for i in range(2)]
        KS = [sb(f"KS{i}", [P, H, N], BF16) for i in range(2)]
        V = [sb(f"V{i}", [P, QC, H, VW], F32) for i in range(2)]
        PR = sb("PR", [P, 2, HG, N], F32)
        OT = sb("OT", [P, 2, N], F32)

        psST = [es.enter_context(nc.psum_tensor(f"psST{i}", [P, N], F32)) for i in range(2)]
        psS = [es.enter_context(nc.psum_tensor(f"psS{i}", [P, N], F32)) for i in range(2)]
        psPV = [es.enter_context(nc.psum_tensor(f"psPV{i}", [P, N], F32)) for i in range(2)]
        psM = [es.enter_context(nc.psum_tensor(f"psM{i}", [P, N], F32)) for i in range(2)]

        SCR = [nc.dram_tensor(f"scratch_parts{w}", [2, H, QPARTS, D, N], BF16, kind="Internal").ap() for w in range(2)]
        SCM = nc.dram_tensor("scratch_max", [2, 2, PARTS * HALF, N], BF16, kind="Internal").ap()

        consts = sem("consts_loaded")
        passed = sem("passed")
        zeros_set, ones_set, lead = sem("zeros_set"), sem("ones_set"), sem("constants_set")
        x_loaded = [sem(f"x_loaded{i}") for i in range(2)]
        stats0, aggr0, eps0, rstd0, xn_ready = (sem(s) for s in ("stats0", "aggr0", "eps0", "rstd0", "xn_ready"))
        xT_psum, xT_ready = sem("xT_psum"), sem("xT_ready")
        qk_psum = [sem(f"qk_psum{w}") for w in range(2)]
        qk_exp = [sem(f"qk_exp{w}") for w in range(2)]
        qk_min = [sem(f"qk_min{w}") for w in range(2)]
        qk_elu = [sem(f"qk_elu{w}") for w in range(2)]
        rot_psum = [sem(f"rot_psum{w}") for w in range(2)]
        rot_cos = [sem(f"rot_cos{w}") for w in range(2)]
        rot_sin = [sem(f"rot_sin{w}") for w in range(2)]
        rot_sum = [sem(f"rot_sum{w}") for w in range(2)]
        part1 = [sem(f"part1_{w}") for w in range(2)]
        resid = [sem(f"resid{w}") for w in range(2)]
        part2 = [sem(f"part2_{w}") for w in range(2)]
        part3 = [sem(f"part3_{w}") for w in range(2)]
        parts_stored = [sem(f"parts_stored{w}") for w in range(2)]
        stacked = [[sem(f"stacked{p}{h}") for h in range(2)] for p in range(2)]
        s_psum = sem("s_psum")
        s_max = sem("s_max")
        mx_step = [sem(f"max_split_step{h}") for h in range(2)]
        mT_psum = sem("mT_psum")
        mT_ready = sem("mT_ready")
        m_stored = sem("m_stored")
        m_stacked = [[sem(f"m_stacked{p}{h}") for h in range(2)] for p in range(2)]
        st_psum = sem("st_psum")
        st_exp = sem("st_exp")
        pv_done = sem("pv_done")
        ot_ready = sem("ot_ready")
        oT_psum = sem("oT_psum")
        recip = sem("recip")
        o_norm = sem("o_norm")
        v_psum, v_ready = sem("v_psum"), sem("v_ready")
        vT_psum, vT_ready = sem("vT_psum"), sem("vT_ready")
        lepe_mid, lepe_left, lepe_ready = sem("lepe_mid"), sem("lepe_left"), sem("lepe_ready")
        lepeT_psum, y_ready = sem("lepeT_psum"), sem("y_ready")
        stats1, aggr1, eps1, rstd1, z_ready, x1_ready = (
            sem(s) for s in ("stats1", "aggr1", "eps1", "rstd1", "z_ready", "x1_ready"))

        NCONST = 7
        LOADS = 3 * 16 * 2
        MISC = ["xT", "mT1", "q", "k", "O3", "Rq", "Rk", "O0", "lepeT", "mT0", "O1", "V", "vT", "O2"]

        def misc_bank(use):
            return psM[MISC.index(use) % 2]

        READER = {"xT": (2, xT_ready, 1, 1), "mT1": (0, mT_ready, 2, 2), "q": (2, qk_elu[0], 1, 1),
                  "O3": (-1, o_norm, 4, 4), "k": (2, qk_elu[1], 1, 1), "Rq": (2, rot_sin[0], 1, 1),
                  "Rk": (2, rot_sin[1], 1, 1), "O0": (0, o_norm, 4, 1), "lepeT": (-1, y_ready, 1, 1),
                  "mT0": (1, mT_ready, 2, 1), "O1": (0, o_norm, 4, 2), "V": (1, v_ready, 1, 1),
                  "vT": (1, vT_ready, 1, 1), "O2": (0, o_norm, 4, 3)}

        def misc_freed(pe, t, use):
            n = MISC.index(use)
            for back in range(2, 2 * len(MISC), 2):
                turn, m = divmod(n - back, len(MISC))
                of, reader, per, mine = READER[MISC[m]]
                b = t + turn + of
                if b.live:
                    pe.wait_ge(reader, b.done(per, mine))
                    return

        def everywhere(emit):
            def loop(eng):
                for c in range(-3, FIRST):
                    emit(Batch(0, c))
                with eng.Fori(0, (B - 3 - FIRST) // 2) as i:
                    emit(Batch(i, FIRST))
                    emit(Batch(i, FIRST + 1))
                for c in range(B - 3, B + 1):
                    emit(Batch(0, c))
            return loop

        block = es.enter_context(nc.Block())

        @block.sync
        def _(sp):
            def load_x(b):
                if due(before := (b + (-2)).done_par(16)):
                    sp.wait_ge(x_loaded[b.par], before)
                sp.dma_start(X[:, bass.ds(b.number() * QC, QC), :],
                             x_in[bass.ds(b.number() * QC, QC)].rearrange("q p c -> p q c")).then_inc(x_loaded[b.par], 16)

            def iteration(t):
                if (t + 3).live:
                    load_x(t + 3)
                b = t + 1
                if t.live:
                    send_max(t, 1)
                if b.live:
                    send_max(b, 0)
                b2 = t + 2
                if b2.live:
                    for w in range(2):
                        for a in range(PARTS if w else QPARTS):
                            if a == 0:
                                sp.wait_ge(part3[w], b2.done(1, 1))
                                for hf in range(2):
                                    if due(before := (b2 + (-2)).done_par(LOADS)):
                                        sp.wait_ge(stacked[b2.par][hf], before)
                            sp.dma_start(SCR[w][b2.par, :, a], PT[:, w, a % PARTS, :]).then_inc(parts_stored[w], 16)
                    stack(t, b2, 0)
                    stack(t, b2, 1)

            def stack(t, b, hf):
                sp.wait_ge(lead, 3)
                for w in range(2):
                    sp.wait_ge(parts_stored[w], b.done(16 * (PARTS if w else QPARTS), 16 * (PARTS if w else QPARTS)))
                if t.live:
                    sp.wait_ge(st_psum, t.done(64, 32 * (hf + 1)))
                for w, S in enumerate((QS, KS)):
                    for r in range(PARTS):
                        first = 0 if w else r
                        sp.dma_start(S[b.par][24 * r:24 * r + 24, HALF * hf:HALF * hf + HALF, :],
                                     SCR[w][b.par, HALF * hf:HALF * hf + HALF, first:first + PARTS].rearrange(
                                         "h a d n -> (a d) h n")).then_inc(stacked[b.par][hf], 16)

            def send_max(b, hf):
                sp.wait_ge(mT_ready, b.done(2, hf + 1))
                sp.dma_start(SCM[b.par, hf], MT[:, hf, :]).then_inc(m_stored, 16)
                sp.wait_ge(m_stored, b.done(32, 16 * (hf + 1)))
                sp.dma_start(QS[b.par][ROWS_QK:ROWS_ALL, HALF * hf:HALF * hf + HALF, :],
                             SCM[b.par, hf].rearrange("(a h) n -> a h n", a=PARTS)).then_inc(m_stacked[b.par][hf], 16)

            everywhere(iteration)(sp)

        @block.tensor
        def _(pe):
            pe.wait_ge(consts, 16 * NCONST)
            pe.wait_ge(lead, 3)

            def scores_t(t, h, kc, k):
                if kc == 0 and h % HALF == 0:
                    hf = h // HALF
                    pe.wait_ge(stacked[t.par][hf], t.done_par(LOADS))
                    pe.wait_ge(m_stacked[t.par][hf], t.done_par(16))
                if due(before := t.done(64, k - 1)):
                    pe.wait_ge(st_exp, before)
                nc.tensor.matmul(psST[k % 2][:], KS[t.par][0:ROWS_ALL, h, kc * P:(kc + 1) * P],
                                 QS[t.par][0:ROWS_ALL, h, :], start=True, stop=True).then_inc(st_psum, 1)

            def scores(b, h, qc, k):
                if qc == 0 and h % HALF == 0:
                    pe.wait_ge(stacked[b.par][h // HALF], b.done_par(LOADS))
                if due(before := b.done(64, k - 1)):
                    pe.wait_ge(s_max, before)
                nc.tensor.matmul(psS[k % 2][:], QS[b.par][0:ROWS_QK, h, qc * P:(qc + 1) * P],
                                 KS[b.par][0:ROWS_QK, h, :], start=True, stop=True).then_inc(s_psum, 1)

            def values(b, s):
                g, kc = divmod(s, QC)
                if s == 0:
                    pe.wait_ge(v_ready, b.done(1, 1))
                if kc == 0:
                    if due(before := b.done(4, g - 1)):
                        pe.wait_ge(ot_ready, before)
                pe.wait_ge(st_exp, b.done(64, 4 * s + 4))
                for j in range(HG):
                    last = nc.tensor.matmul(psPV[g % 2][VW * j:VW * j + VW, :], V[b.par][:, kc, HG * g + j, :],
                                            PR[:, s % 2, j, :], start=(kc == 0), stop=(kc == QC - 1))
                last.then_inc(pv_done, 1)

            def out_transposes(b, g, use):
                pe.wait_ge(ot_ready, b.done(4, g + 1))
                m = misc_bank(use)
                for qc in range(QC):
                    last = nc.tensor.transpose(m[:, qc * P:(qc + 1) * P], OT[:, g % 2, qc * P:(qc + 1) * P], IDF[:])
                last.then_inc(oT_psum, 1)

            def misc(t, s):
                nxt, prep, prev = t + 1, t + 2, t + (-1)
                if s == 0 and prep.live:
                    misc_freed(pe, t, "xT")
                    pe.wait_ge(xn_ready, prep.done(1, 1))
                    m = misc_bank("xT")
                    for qc in range(QC):
                        last = nc.tensor.transpose(m[:, qc * P:(qc + 1) * P], XN[:, qc, :], IDF[:])
                    last.then_inc(xT_psum, 1)
                if s == 1 and t.live:
                    misc_freed(pe, t, "mT1")
                    max_transposes(t, 1, "mT1")
                if s == 2 and prep.live:
                    misc_freed(pe, t, "q")
                    project(prep, 0, "q")
                if s == 3 and prep.live:
                    misc_freed(pe, t, "k")
                    project(prep, 1, "k")
                if s == 4 and prev.live:
                    misc_freed(pe, t, "O3")
                    out_transposes(prev, 3, "O3")
                if s in (5, 6) and prep.live:
                    w = s - 5
                    use = ("Rq", "Rk")[w]
                    misc_freed(pe, t, use)
                    pe.wait_ge(qk_elu[w], prep.done(1, 1))
                    nc.tensor.matmul(misc_bank(use)[:], PERM[:], EL[:, w, :], start=True, stop=True).then_inc(rot_psum[w], 1)
                if s == 7 and t.live:
                    misc_freed(pe, t, "O0")
                    out_transposes(t, 0, "O0")
                if s == 8 and prev.live:
                    misc_freed(pe, t, "lepeT")
                    pe.wait_ge(lepe_ready, prev.done(1, 1))
                    m = misc_bank("lepeT")
                    for qc in range(QC):
                        last = nc.tensor.transpose(m[:, qc * P:(qc + 1) * P], LP[:, prev.par, qc * P:(qc + 1) * P], IDF[:])
                    last.then_inc(lepeT_psum, 1)
                if s == 9 and nxt.live:
                    misc_freed(pe, t, "mT0")
                    max_transposes(nxt, 0, "mT0")
                if s == 10 and t.live:
                    misc_freed(pe, t, "O1")
                    out_transposes(t, 1, "O1")
                if s == 11 and nxt.live:
                    misc_freed(pe, t, "V")
                    pe.wait_ge(xT_ready, nxt.done(1, 1))
                    m = misc_bank("V")
                    for kc in range(QC):
                        last = nc.tensor.matmul(m[:, kc * P:(kc + 1) * P], XT[:, nxt.par, kc * P:(kc + 1) * P],
                                                WQKV[:, 2 * C:3 * C], start=True, stop=True)
                    last.then_inc(v_psum, 1)
                if s == 12 and nxt.live:
                    misc_freed(pe, t, "vT")
                    nc.tensor.matmul(misc_bank("vT")[:], WQKV[:, 2 * C:3 * C], XT[:, nxt.par, :],
                                     start=True, stop=True).then_inc(vT_psum, 1)
                if s == 14 and t.live:
                    misc_freed(pe, t, "O2")
                    out_transposes(t, 2, "O2")

            def max_transposes(b, hf, use):
                pe.wait_ge(mx_step[hf], b.done(5, 5))
                m = misc_bank(use)[0:PARTS * HALF, 0:N // 2].bitcast(BF16)
                for qc in range(QC):
                    last = nc.tensor.transpose(m[:, qc * P:(qc + 1) * P],
                                               MP[:, hf, qc, :, :].rearrange("p a h -> p (a h)"), IDB[:])
                last.then_inc(mT_psum, 1)

            def project(b, w, use):
                pe.wait_ge(xT_ready, b.done(1, 1))
                nc.tensor.matmul(misc_bank(use)[:], WQKV[:, w * C:(w + 1) * C], XT[:, b.par, :],
                                 start=True, stop=True).then_inc(qk_psum[w], 1)

            def iteration(t):
                nxt, prev = t + 1, t + (-1)
                for s in range(SLOTS):
                    g, kc = divmod(s, QC)
                    for j in range(HG):
                        if t.live:
                            scores_t(t, HG * g + j, kc, 4 * s + j)
                        if nxt.live:
                            scores(nxt, s, j, 4 * s + j)
                        if j == 1:
                            if s == 0 and prev.live:
                                values(prev, SLOTS - 1)
                            if s > 0 and t.live:
                                values(t, s - 1)
                    misc(t, s)

            everywhere(iteration)(pe)

        @block.scalar
        def _(act):
            for dst, src in ((IDF[:], ident), (WQKV[:], wqkvT), (CHAN[:], chan), (PERM[:], perm),
                             (COS[:], rope_cos), (SIN[:], rope_sin), (BV[:], bv.unsqueeze(0).to_broadcast([P, C]))):
                act.dma_start(dst, src).then_inc(consts, 16)
            load_weights(act)
            act.wait_ge(consts, 16 * NCONST)
            act.wait_ge(lead, 3)

            def extra(t, s):
                nxt, prep, prev = t + 1, t + 2, t + (-1)
                if s in (1, 5, 9, 13):
                    b, g = (prev, 3) if s == 1 else (t, s // 4 - 1)
                    if b.live:
                        act.wait_ge(pv_done, b.done(16, 4 * g + 4))
                        if due(before := b.done(4, g - 1)):
                            act.wait_ge(oT_psum, before)
                        nc.scalar.activation(OT[:, g % 2, :], psPV[g % 2][:], ACT.Copy).then_inc(ot_ready, 1)
                if s == 1 and prep.live:
                    act.wait_ge(xT_psum, prep.done(1, 1))
                    if due(before := (prep + (-2)).done(1, 1)):
                        act.wait_ge(vT_psum, before)
                    nc.scalar.activation(XT[:, prep.par, :], misc_bank("xT")[:], ACT.Copy).then_inc(xT_ready, 1)
                if s == 2 and t.live:
                    copy_max(t, 1, "mT1")
                if s in (3, 4) and prep.live:
                    w = s - 3
                    act.wait_ge(qk_psum[w], prep.done(1, 1))
                    if due(before := prep.done(1, 0)):
                        act.wait_ge(qk_elu[w], before)
                    nc.scalar.activation(EXQ[:, w, :], misc_bank("qk"[w])[:], ACT.Exp,
                                         bias=CHAN[:, w:w + 1]).then_inc(qk_exp[w], 1)
                if s in (8, 9) and prep.live:
                    w = s - 8
                    act.wait_ge(rot_sum[w], prep.done(1, 1))
                    if due(before := prep.done(16 * (PARTS if w else QPARTS), 0)):
                        act.wait_ge(parts_stored[w], before)
                    nc.scalar.activation(PT[:, w, 0, :], ROT[:, w, :], ACT.Copy).then_inc(part1[w], 1)
                if s in (10, 11) and prep.live:
                    w = s - 10
                    act.wait_ge(resid[w], prep.done(1, 1))
                    nc.scalar.activation(PT[:, w, 1, :], RES[:, w, :], ACT.Copy).then_inc(part2[w], 1)
                if s == 10 and nxt.live:
                    copy_max(nxt, 0, "mT0")
                if s == 13 and nxt.live:
                    act.wait_ge(vT_psum, nxt.done(1, 1))
                    if due(before := nxt.done(1, 0)):
                        act.wait_ge(lepe_ready, before)
                    nc.scalar.activation(VT[:, 1:N + 1], misc_bank("vT")[:], ACT.Identity,
                                         bias=CHAN[:, 2:3]).then_inc(vT_ready, 1)
                if s == 14 and nxt.live:
                    act.wait_ge(vT_ready, nxt.done(1, 1))
                    if due(before := (nxt + (-2)).done(1, 1)):
                        act.wait_ge(lepeT_psum, before)
                    nc.scalar.activation(LP[:, nxt.par, :], VT[:, 1:N + 1], ACT.Identity,
                                         bias=CHAN[:, 6:7], scale=CHAN[:, 4:5]).then_inc(lepe_mid, 1)

            def copy_max(b, hf, use):
                act.wait_ge(mT_psum, b.done(2, hf + 1))
                if due(before := b.done(32, 16 * (hf + 1) - 32)):
                    act.wait_ge(m_stored, before)
                nc.scalar.activation(MT[:, hf, :], misc_bank(use)[0:PARTS * HALF, 0:N // 2].bitcast(BF16),
                                     ACT.Copy).then_inc(mT_ready, 1)

            def iteration(t):
                for s in range(SLOTS):
                    for j in range(HG):
                        if t.live:
                            k = 4 * s + j
                            act.wait_ge(st_psum, t.done(64, k + 1))
                            if j == 0:
                                if due(before := t.done(16, s - 1)):
                                    act.wait_ge(pv_done, before)
                            nc.scalar.activation(PR[:, s % 2, j, :], psST[k % 2][:], ACT.Exp,
                                                 scale=SCALE).then_inc(st_exp, 1)
                    extra(t, s)

            everywhere(iteration)(act)

        @block.vector
        def _(dve):
            nc.vector.memset(VT[:], 0.0)
            for p in range(2):
                last = nc.vector.memset(V[p][:], 0.0)
            last.then_inc(zeros_set, 1)
            dve.wait_ge(zeros_set, 1)
            for p in range(2):
                last = nc.vector.memset(V[p][:, :, :, D:D + 1], 1.0)
            last.then_inc(lead, 1)
            dve.wait_ge(consts, 16 * NCONST)
            nc.vector.tensor_copy(IDB[:], IDF[:])
            nc.vector.tensor_scalar(BP1[:], CHAN[:, 0:2], 1.0, None, ALU.add).then_inc(lead, 1)
            dve.wait_ge(lead, 3)

            def elu(b, w):
                dve.wait_ge(qk_exp[w], b.done(1, 1))
                nc.vector.tensor_scalar(EXQ[:, w, :], EXQ[:, w, :], 1.0, None, ALU.min).then_inc(qk_min[w], 1)
                dve.wait_ge(qk_min[w], b.done(1, 1))
                if due(before := b.done(1, 0)):
                    dve.wait_ge(rot_cos[w], before)
                if due(before := b.done(1, 0)):
                    dve.wait_ge(rot_psum[w], before)
                nc.vector.scalar_tensor_tensor(out=EL[:, w, :], in0=misc_bank("qk"[w])[:], scalar=BP1[:, w:w + 1],
                                               in1=EXQ[:, w, :], op0=ALU.add, op1=ALU.max).then_inc(qk_elu[w], 1)

            def normalise(b, g, use):
                m = misc_bank(use)[:].rearrange("p (q j v) -> p q j v", q=QC, j=HG)
                dve.wait_ge(oT_psum, b.done(4, g + 1))
                if due(before := b.done(4, g)):
                    dve.wait_ge(o_norm, before)
                nc.vector.reciprocal(REC[:], m[:, :, :, D]).then_inc(recip, 1)
                dve.wait_ge(recip, b.done(4, g + 1))
                if g == 0:
                    if due(before := b.done(1, -1)):
                        dve.wait_ge(z_ready, before)
                y = Y[:, b.par, :, g * HG * D:(g + 1) * HG * D].rearrange("p q (j d) -> p q j d", j=HG)
                nc.vector.tensor_tensor(y, m[:, :, :, 0:D], REC[:].unsqueeze(3).to_broadcast([P, QC, HG, D]),
                                        ALU.mult).then_inc(o_norm, 1)

            def extra(t, s, j):
                nxt, prep, prev, far = t + 1, t + 2, t + (-1), t + 3
                if s in (4, 5) and j == 1 and prep.live:
                    elu(prep, s - 4)
                if s == 5 and j == 3 and prev.live:
                    normalise(prev, 3, "O3")
                if s in (6, 7) and j == 1 and prep.live:
                    w = s - 6
                    dve.wait_ge(rot_psum[w], prep.done(1, 1))
                    if due(before := prep.done(1, 0)):
                        dve.wait_ge(part3[w], before)
                    nc.vector.tensor_tensor(RES[:, w, :], misc_bank(("Rq", "Rk")[w])[:], SIN[:],
                                            ALU.mult).then_inc(rot_sin[w], 1)
                if s == 8 and j == 1 and t.live:
                    normalise(t, 0, "O0")
                if s == 9 and j == 1 and prev.live:
                    dve.wait_ge(lepeT_psum, prev.done(1, 1))
                    dve.wait_ge(o_norm, prev.done(4, 4))
                    nc.vector.tensor_tensor(Y[:, prev.par], misc_bank("lepeT")[:].rearrange("p (q c) -> p q c", q=QC),
                                            Y[:, prev.par],
                                            ALU.add).then_inc(y_ready, 1)
                if s == 11 and j == 1 and t.live:
                    normalise(t, 1, "O1")
                if s == 12 and j == 3 and nxt.live:
                    dve.wait_ge(v_psum, nxt.done(1, 1))
                    if due(before := (nxt + (-1)).done(16, 0)):
                        dve.wait_ge(pv_done, before)
                    nc.vector.tensor_tensor(
                        V[nxt.par][:, :, :, 0:D],
                        misc_bank("V")[:].rearrange("p (q h d) -> p q h d", q=QC, h=H),
                        BV[:].rearrange("p (h d) -> p h d", h=H).unsqueeze(1).to_broadcast([P, QC, H, D]),
                        ALU.add).then_inc(v_ready, 1)
                if s == 15 and j == 2 and nxt.live:
                    dve.wait_ge(lepe_mid, nxt.done(1, 1))
                    nc.vector.scalar_tensor_tensor(out=LP[:, nxt.par, :], in0=VT[:, 0:N], scalar=CHAN[:, 3:4],
                                                   in1=LP[:, nxt.par, :], op0=ALU.mult, op1=ALU.add).then_inc(lepe_left, 1)
                if s == 0 and j == 1 and t.live:
                    dve.wait_ge(lepe_left, t.done(1, 1))
                    nc.vector.scalar_tensor_tensor(out=LP[:, t.par, :], in0=VT[:, 2:N + 2], scalar=CHAN[:, 5:6],
                                                   in1=LP[:, t.par, :], op0=ALU.mult, op1=ALU.add).then_inc(lepe_ready, 1)
                if s == 15 and j == 1 and t.live:
                    normalise(t, 2, "O2")
                if s == 9 and j == 3 and prev.live:
                    dve.wait_ge(y_ready, prev.done(1, 1))
                    for qc in range(QC):
                        last = nc.vector.bn_stats(ST1[:, qc, :], Y[:, prev.par, qc, :])
                    last.then_inc(stats1, 1)
                if s == 10 and j == 1 and prev.live:
                    dve.wait_ge(stats1, prev.done(1, 1))
                    dve.sem_inc(passed, 1)
                    for qc in range(QC):
                        last = nc.vector.bn_aggr(MV1[:, qc, :], ST1[:, qc, :])
                    last.then_inc(aggr1, 1)
                if s == 12 and j == 1 and prev.live:
                    dve.wait_ge(rstd1, prev.done(1, 1))
                    if due(before := prev.done(1, 0)):
                        dve.wait_ge(x1_ready, before)
                    for qc in range(QC):
                        last = nc.vector.tensor_scalar(Z[:, qc, :], Y[:, prev.par, qc, :], MV1[:, qc, 0:1], RS1[:, qc:qc + 1],
                                                       ALU.subtract, ALU.mult)
                    last.then_inc(z_ready, 1)
                if s == 13 and j == 1 and far.live:
                    dve.wait_ge(x_loaded[far.par], far.done_par(16))
                    for qc in range(QC):
                        last = nc.vector.bn_stats(ST0[:, qc, :], X[:, far.number() * QC + qc, :])
                    last.then_inc(stats0, 1)
                if s == 13 and j == 3 and far.live:
                    dve.wait_ge(stats0, far.done(1, 1))
                    dve.sem_inc(passed, 1)
                    for qc in range(QC):
                        last = nc.vector.bn_aggr(MV0[:, qc, :], ST0[:, qc, :])
                    last.then_inc(aggr0, 1)
                if s == 15 and j == 0 and far.live:
                    dve.wait_ge(rstd0, far.done(1, 1))
                    if due(before := far.done(1, 0)):
                        dve.wait_ge(xT_psum, before)
                    for qc in range(QC):
                        last = nc.vector.tensor_scalar(XN[:, qc, :], X[:, far.number() * QC + qc, :], MV0[:, qc, 0:1],
                                                       RS0[:, qc:qc + 1], ALU.subtract, ALU.mult)
                    last.then_inc(xn_ready, 1)

            def iteration(t):
                nxt = t + 1
                for s in range(SLOTS):
                    for j in range(HG):
                        if nxt.live:
                            k = 4 * s + j
                            dve.wait_ge(s_psum, nxt.done(64, k + 1))
                            if s % HALF == 0 and j == 0:
                                if due(before := nxt.done(5, 0)):
                                    dve.wait_ge(mx_step[s // HALF], before)
                            nc.vector.tensor_reduce(out=MX[:, j, s:s + 1], in_=psS[k % 2][:], axis=AX.X,
                                                    op=ALU.max).then_inc(s_max, 1)
                        extra(t, s, j)

            everywhere(iteration)(dve)

        @block.gpsimd
        def _(pool):
            for p in range(2):
                nc.gpsimd.memset(KS[p][64:96, :, :], 1.0).then_inc(ones_set, 1)
                pool.wait_ge(ones_set, p + 1)
            nc.gpsimd.memset(NHALF[:], -0.5).then_inc(lead, 1)
            pool.wait_ge(consts, 16 * NCONST)
            pool.wait_ge(lead, 3)

            def split_max(b, hf):
                m = MX[:, :, HALF * hf:HALF * hf + HALF]
                n = [MP[:, hf, :, a, :] for a in range(PARTS)]
                r = MR[:, hf]
                pool.wait_ge(s_max, b.done(64, 32 * (hf + 1)))
                if due(before := b.done(2, hf - 1)):
                    pool.wait_ge(mT_psum, before)
                pool.sem_inc(passed, 1)
                step = mx_step[hf]
                nc.gpsimd.tensor_scalar(n[0], m, -1.0, 0.0, ALU.mult, ALU.add).then_inc(step, 1)
                pool.wait_ge(step, b.done(5, 1))
                nc.gpsimd.tensor_tensor(r, m, n[0], ALU.add).then_inc(step, 1)
                pool.wait_ge(step, b.done(5, 2))
                pool.sem_inc(passed, 1)
                nc.gpsimd.tensor_scalar(n[1], r, -1.0, 0.0, ALU.mult, ALU.add).then_inc(step, 1)
                pool.wait_ge(step, b.done(5, 3))
                nc.gpsimd.tensor_tensor(r, r, n[1], ALU.add).then_inc(step, 1)
                pool.wait_ge(step, b.done(5, 4))
                pool.sem_inc(passed, 1)
                nc.gpsimd.tensor_scalar(n[2], r, -1.0, 0.0, ALU.mult, ALU.add).then_inc(step, 1)

            def rsqrt(b, MV, VE, RS, aggr, eps, rstd, free):
                pool.wait_ge(aggr, b.done(1, 1))
                pool.sem_inc(passed, 1)
                nc.gpsimd.tensor_scalar(VE[:], MV[:, :, 1], 1.0, EPS, ALU.mult, ALU.add).then_inc(eps, 1)
                pool.wait_ge(eps, b.done(1, 1))
                if due(before := b.done(1, 0)):
                    pool.wait_ge(free, before)
                nc.gpsimd.tensor_tensor(RS[:], VE[:], NHALF[:], ALU.pow).then_inc(rstd, 1)

            def iteration(t):
                nxt, prep, prev, far = t + 1, t + 2, t + (-1), t + 3
                if t.live:
                    split_max(t, 1)
                if prep.live:
                    for w in range(2):
                        pool.wait_ge(qk_elu[w], prep.done(1, 1))
                        if due(before := prep.done(1, 0)):
                            pool.wait_ge(resid[w], before)
                        nc.gpsimd.tensor_tensor(ROT[:, w, :], EL[:, w, :], COS[:], ALU.mult).then_inc(rot_cos[w], 1)
                    for w in range(2):
                        pool.wait_ge(rot_cos[w], prep.done(1, 1))
                        pool.wait_ge(rot_sin[w], prep.done(1, 1))
                        nc.gpsimd.tensor_tensor(ROT[:, w, :], ROT[:, w, :], RES[:, w, :], ALU.add).then_inc(rot_sum[w], 1)
                if nxt.live:
                    split_max(nxt, 0)
                for w in range(2):
                    if prep.live:
                        pool.wait_ge(part1[w], prep.done(1, 1))
                        nc.gpsimd.tensor_tensor(RES[:, w, :], ROT[:, w, :], PT[:, w, 0, :], ALU.subtract).then_inc(resid[w], 1)
                    if w == 0 and prev.live:
                        rsqrt(prev, MV1, VE1, RS1, aggr1, eps1, rstd1, z_ready)
                if prep.live:
                    for w in range(2):
                        pool.wait_ge(part2[w], prep.done(1, 1))
                        nc.gpsimd.tensor_tensor(PT[:, w, 2, :], RES[:, w, :], PT[:, w, 1, :], ALU.subtract).then_inc(part3[w], 1)
                if prev.live:
                    pool.wait_ge(z_ready, prev.done(1, 1))
                    x = X[:, bass.ds(prev.number() * QC, QC), :]
                    nc.gpsimd.tensor_tensor(x, x, Z[:], ALU.add).then_inc(x1_ready, 1)
                if far.live:
                    rsqrt(far, MV0, VE0, RS0, aggr0, eps0, rstd0, xn_ready)

            everywhere(iteration)(pool)


def experts(nc, gate_wT, gate_b, W1, W3, W2, weights, HB, B2, ident, X, out):
    es = ExitStack()
    with es:
        def sb(name, shape, dt):
            return es.enter_context(nc.sbuf_tensor(name, shape, dt))

        def sem(name):
            return es.enter_context(nc.semaphore(name))

        WH = [sb(f"WH{m}", [P, EXP_ALL, 2, F], F32R) for m in range(2)]
        WL = [sb(f"WL{m}", [P, EXP_ALL, 2, F], F32R) for m in range(2)]
        GH = sb("GH", [P, NE], F32R)
        GL = sb("GL", [P, NE], F32R)
        GW = sb("GW", [P, NE], F32)
        GB = sb("GB", [P, NE], F32)
        IDF = sb("IDFB", [P, P], F32)
        IOTA = sb("IOTA", [P, NE], F32)
        BIAS = sb("BIAS", [P, 2, 2, EXP_ALL], F32)
        BD = sb("BD", [EXP_ALL, C], F32)
        NHALF = sb("NHALFB", [P, QC], F32)

        ST2 = sb("ST2", [P, QC, 6], F32)
        MV2 = sb("MV2", [P, QC, 2], F32)
        VE2 = sb("VE2", [P, QC], F32)
        RS2 = sb("RS2", [P, QC], F32)
        ST3 = sb("ST3", [P, QC, 6], F32)
        MV3 = sb("MV3", [P, QC, 2], F32)
        VE3 = sb("VE3", [P, QC], F32)
        RS3 = sb("RS3", [P, QC], F32)
        XN = sb("XNB", [P, QC, C], F32)
        XH = sb("XH", [P, 2, N], F32R)
        XL = sb("XL", [P, 2, N], F32R)
        GM = sb("GM", [P, QC, 1], F32)
        GE = sb("GE", [P, QC, NE], F32)
        GS = sb("GS", [P, QC, 1], F32)
        GR = sb("GR", [P, QC, 1], F32)
        SC = sb("SC", [P, QC, NE], F32)
        BI = sb("BI", [P, QC, NE], F32)
        TOP = sb("TOP", [P, QC, 8], F32)
        IDX = sb("IDX", [P, QC, 8], U32)
        IDXF = sb("IDXF", [P, QC, TOPK], F32)
        PICK = sb("PICK", [P, TOPK, QC, NE], F32)
        CW = sb("CW", [P, 2, QC, EXP_ALL], F32)
        CWT = sb("CWT", [EXP_ALL, 2, N], F32)
        A1 = sb("A1", [P, 2, 2, N], F32)
        G = sb("G", [P, 2, N], F32)
        L = sb("L", [P, 2, N], F32)
        TH = sb("TH", [P, 2, N], F32)
        GT = sb("GT", [P, 2, N], F32)
        HA = sb("HA", [P, 2, N], F32)
        ACC = sb("ACC", [P, QC, C], F32)
        Z = sb("ZB", [P, QC, C], F32)
        OUT = sb("OUT", [P, 2, QC, C], F32)

        RING = 6
        psH = [es.enter_context(nc.psum_tensor(f"psH{i}", [P, N], F32)) for i in range(RING)]
        psY = es.enter_context(nc.psum_tensor("psY", [P, N], F32))
        psX = es.enter_context(nc.psum_tensor("psX", [P, N], F32))

        consts, ready = sem("constsB_loaded"), sem("weights_split")
        passed = sem("passedB")
        iota_done, wh_ready = sem("iota_done"), sem("weights_high")
        stats2, aggr2, eps2, rstd2, xn_ready = (sem(s) for s in ("stats2", "aggr2", "eps2", "rstd2", "xn2_ready"))
        stats3, aggr3, eps3, rstd3, z_ready = (sem(s) for s in ("stats3", "aggr3", "eps3", "rstd3", "z3_ready"))
        xT_psum, xh_ready, xl_ready = sem("xT2_psum"), sem("xh_ready"), sem("xl_ready")
        logits_psum, logits_read = sem("logits_psum"), sem("logits_read")
        gate_step = sem("gate_step")
        gate_exp = sem("gate_exp")
        biased = sem("biased")
        cwT_psum, cwT_ready = sem("cwT_psum"), sem("cwT_ready")
        h1_psum, h3_psum = sem("h1_psum"), sem("h3_psum")
        a1_ready, gl_ready = sem("a1_ready"), sem("gl_ready")
        g_clip, l_clip = sem("g_clipped"), sem("l_clipped")
        tanh_done, l_plus = sem("tanh_done"), sem("l_plus")
        gate_done, ha_ready = sem("gate_done"), sem("ha_ready")
        y_psum, y_added = sem("y_psum"), sem("y_added")
        x2_ready = sem("x2_ready")
        stored = [sem(f"stored{i}") for i in range(2)]
        NCONST = 5
        GATE_STEPS = 12

        def everywhere(emit):
            def loop(eng):
                for c in range(-1, FIRST):
                    emit(Batch(0, c))
                with eng.Fori(0, (B - 1 - FIRST) // 2) as i:
                    emit(Batch(i, FIRST))
                    emit(Batch(i, FIRST + 1))
                for c in (B - 1, B):
                    emit(Batch(0, c))
            return loop

        block = es.enter_context(nc.Block())

        @block.sync
        def _(sp):
            for dst, src in ((GW[:], gate_wT), (IDF[:], ident), (BIAS[:], HB), (BD[:], B2),
                             (GB[:], gate_b.unsqueeze(0).to_broadcast([P, NE]))):
                sp.dma_start(dst, src).then_inc(consts, 16)

            def iteration(t):
                b = t + (-1)
                if b.live:
                    sp.wait_ge(x2_ready, b.done(1, 1))
                    sp.dma_start(out[bass.ds(b.number() * QC, QC)].rearrange("q p c -> p q c"),
                                 OUT[:, b.par]).then_inc(stored[b.par], 16)

            everywhere(iteration)(sp)
            for p in range(2):
                sp.wait_ge(stored[p], 16 * (B // 2))

        @block.tensor
        def _(pe):
            pe.wait_ge(consts, 16 * NCONST)
            pe.wait_ge(ready, 2)

            def hidden(b, e, u):
                m, gl = u % 2, u // 2 % 2
                if u == 0:
                    pe.wait_ge(xh_ready, b.done(1, 1))
                    pe.wait_ge(xl_ready, b.done(1, 1))
                v = u - RING
                if due(before := b.done(2 * EXP_ALL, v // 4 * 2 + v % 4 // 2 + 1)):
                    pe.wait_ge(gl_ready if m else a1_ready, before)
                ps = psH[u % RING]
                nc.tensor.matmul(ps[:], WH[m][:, e, gl, :], XH[:, b.par, :], start=True, stop=False)
                nc.tensor.matmul(ps[:], WH[m][:, e, gl, :], XL[:, b.par, :], start=False, stop=False)
                nc.tensor.matmul(ps[:], WL[m][:, e, gl, :], XH[:, b.par, :], start=False,
                                 stop=True).then_inc(h3_psum if m else h1_psum, 1)

            def down(b, e):
                pe.wait_ge(ha_ready, b.done(EXP_ALL, e + 1))
                if due(before := b.done(EXP_ALL, e)):
                    pe.wait_ge(y_added, before)
                shared = e == NE
                if shared:
                    pe.wait_ge(cwT_ready, b.done(1, 1))
                for qc in range(QC):
                    last = nc.tensor.matmul(psY[:, qc * P:(qc + 1) * P], HA[:, (b.par + e) % 2, qc * P:(qc + 1) * P],
                                            W2[:, e, :], start=True, stop=not shared)
                    if shared:
                        last = nc.tensor.matmul(psY[:, qc * P:(qc + 1) * P], CWT[:, b.par, qc * P:(qc + 1) * P],
                                                BD[:], start=False, stop=True)
                last.then_inc(y_psum, 1)

            def prepare(b, s):
                if s == 2:
                    pe.wait_ge(xn_ready, b.done(1, 1))
                    if due(before := b.done(1, 0)):
                        pe.wait_ge(cwT_ready, before)
                    for qc in range(QC):
                        last = nc.tensor.transpose(psX[:, qc * P:(qc + 1) * P], XN[:, qc, :], IDF[:])
                    last.then_inc(xT_psum, 1)
                if s == 3:
                    pe.wait_ge(xh_ready, b.done(1, 1))
                    pe.wait_ge(xl_ready, b.done(1, 1))
                    for qc in range(QC):
                        o = psX[:, qc * NE:(qc + 1) * NE]
                        for n, (xx, ww) in enumerate(((XH, GH), (XL, GH), (XH, GL))):
                            last = nc.tensor.matmul(o, xx[:, b.par, qc * P:(qc + 1) * P], ww[:],
                                                    start=(n == 0), stop=(n == 2))
                    last.then_inc(logits_psum, 1)
                if s == 7:
                    pe.wait_ge(gate_step, b.done(GATE_STEPS, GATE_STEPS))
                    for qc in range(QC):
                        last = nc.tensor.transpose(psX[0:EXP_ALL, qc * P:(qc + 1) * P], CW[:, b.par, qc, :], IDF[:])
                    last.then_inc(cwT_psum, 1)

            def iteration(t):
                nxt = t + 1
                prev = t + (-1)
                for e in range(EXP_ALL):
                    for u in range(4):
                        if t.live:
                            hidden(t, e, 4 * e + u)
                        if u == 1 and e < 2 and prev.live:
                            down(prev, NE - 1 + e)
                        if u == 1 and e >= 2 and t.live:
                            down(t, e - 2)
                    if nxt.live:
                        prepare(nxt, e)

            everywhere(iteration)(pe)

        @block.scalar
        def _(act):
            act.wait_ge(consts, 16 * NCONST)
            act.wait_ge(weights, 16 * 3)
            for m, W in enumerate((W1, W3)):
                nc.scalar.activation(WH[m][:], W[:].rearrange("p e (f g) -> p e g f", g=2), ACT.Copy)
            last = nc.scalar.activation(GH[:], GW[:], ACT.Copy)
            last.then_inc(wh_ready, 1)

            def prepare(b, s):
                if s == 2:
                    act.wait_ge(xT_psum, b.done(1, 1))
                    if due(before := b.done(2 * EXP_ALL, -2 * EXP_ALL)):
                        act.wait_ge(h3_psum, before)
                    nc.scalar.activation(XH[:, b.par, :], psX[:], ACT.Copy).then_inc(xh_ready, 1)
                if s == 4:
                    act.wait_ge(gate_step, b.done(GATE_STEPS, 2))
                    nc.scalar.activation(GE[:], GE[:], ACT.Exp).then_inc(gate_exp, 1)
                if s == 8:
                    act.wait_ge(cwT_psum, b.done(1, 1))
                    if due(before := b.done(EXP_ALL, -EXP_ALL)):
                        act.wait_ge(y_psum, before)
                    nc.scalar.activation(CWT[:, b.par, :], psX[0:EXP_ALL, :], ACT.Copy).then_inc(cwT_ready, 1)

            def hidden(b, e):
                for gl in range(2):
                    k = 2 * e + gl
                    act.wait_ge(h1_psum, b.done(2 * EXP_ALL, k + 1))
                    if due(before := b.done(2 * EXP_ALL, k - 3)):
                        act.wait_ge(gl_ready, before)
                    nc.scalar.activation(A1[:, (b.par + e) % 2, gl, :], psH[4 * e % RING if gl == 0 else (4 * e + 2) % RING][:],
                                         ACT.Identity, bias=BIAS[:, 0, gl, e:e + 1]).then_inc(a1_ready, 1)

            def gates(b, e):
                act.wait_ge(g_clip, b.done(EXP_ALL, e + 1))
                if due(before := b.done(EXP_ALL, e - 1)):
                    act.wait_ge(gate_done, before)
                nc.scalar.activation(TH[:, (b.par + e) % 2, :], G[:, (b.par + e) % 2, :], ACT.Tanh, scale=ALPHA / 2).then_inc(tanh_done, 1)
                act.wait_ge(l_clip, b.done(EXP_ALL, e + 1))
                nc.scalar.activation(L[:, (b.par + e) % 2, :], L[:, (b.par + e) % 2, :], ACT.Identity, bias=1.0).then_inc(l_plus, 1)

            def iteration(t):
                nxt = t + 1
                for e in range(EXP_ALL):
                    if t.live:
                        hidden(t, e)
                        if e > 0:
                            gates(t, e - 1)
                    if nxt.live:
                        prepare(nxt, e)
                if t.live:
                    gates(t, NE)

            everywhere(iteration)(act)

        @block.vector
        def _(dve):
            nc.vector.memset(NHALF[:], -0.5)
            last = nc.vector.memset(CW[:], 1.0)
            last.then_inc(ready, 1)
            dve.wait_ge(consts, 16 * NCONST)
            dve.wait_ge(iota_done, 1)
            dve.wait_ge(wh_ready, 1)
            for m, W in enumerate((W1, W3)):
                nc.vector.tensor_tensor(WL[m][:], W[:].rearrange("p e (f g) -> p e g f", g=2), WH[m][:].bitcast(F32),
                                        ALU.subtract)
            nc.vector.tensor_tensor(GL[:], GW[:], GH[:].bitcast(F32), ALU.subtract)
            nc.vector.tensor_scalar(W2[:], W2[:], 0.5, None, ALU.mult).then_inc(ready, 1)

            def prepare(b, s):
                def step(n):
                    dve.wait_ge(gate_step, b.done(GATE_STEPS, n))
                if s == 0:
                    for qc in range(QC):
                        last = nc.vector.bn_stats(ST2[:, qc, :], X[:, b.number() * QC + qc, :])
                    last.then_inc(stats2, 1)
                    dve.wait_ge(stats2, b.done(1, 1))
                    dve.sem_inc(passed, 1)
                    for qc in range(QC):
                        last = nc.vector.bn_aggr(MV2[:, qc, :], ST2[:, qc, :])
                    last.then_inc(aggr2, 1)
                if s == 1:
                    dve.wait_ge(rstd2, b.done(1, 1))
                    for qc in range(QC):
                        last = nc.vector.tensor_scalar(XN[:, qc, :], X[:, b.number() * QC + qc, :], MV2[:, qc, 0:1],
                                                       RS2[:, qc:qc + 1], ALU.subtract, ALU.mult)
                    last.then_inc(xn_ready, 1)
                if s == 2:
                    dve.wait_ge(xh_ready, b.done(1, 1))
                    nc.vector.tensor_tensor(XL[:, b.par, :], psX[:], XH[:, b.par, :].bitcast(F32),
                                            ALU.subtract).then_inc(xl_ready, 1)
                if s == 3:
                    dve.wait_ge(logits_psum, b.done(1, 1))
                    lg = psX[:, 0:QC * NE].rearrange("p (q e) -> p q e", q=QC)
                    nc.vector.tensor_reduce(out=GM[:], in_=lg, axis=AX.X, op=ALU.max).then_inc(gate_step, 1)
                    step(1)
                    nc.vector.tensor_tensor(GE[:], lg, GM[:].to_broadcast([P, QC, NE]), ALU.subtract).then_inc(gate_step, 1)
                if s == 4:
                    dve.wait_ge(gate_exp, b.done(1, 1))
                    nc.vector.tensor_reduce(out=GS[:], in_=GE[:], axis=AX.X, op=ALU.add).then_inc(gate_step, 1)
                    step(3)
                    nc.vector.reciprocal(GR[:], GS[:]).then_inc(gate_step, 1)
                    step(4)
                    nc.vector.tensor_tensor(SC[:], GE[:], GR[:].to_broadcast([P, QC, NE]), ALU.mult).then_inc(gate_step, 1)
                if s == 5:
                    step(5)
                    nc.vector.tensor_tensor(BI[:], SC[:], GB[:].unsqueeze(1).to_broadcast([P, QC, NE]),
                                            ALU.add).then_inc(gate_step, 1)
                    dve.wait_ge(gate_step, b.done(GATE_STEPS, 6))
                    dve.sem_inc(passed, 1)
                    for qc in range(QC):
                        last = nc.vector.max(out=TOP[:, qc, :], in_=BI[:, qc, :])
                    last.then_inc(gate_step, 1)
                    dve.wait_ge(gate_step, b.done(GATE_STEPS, 7))
                    dve.sem_inc(passed, 1)
                    for qc in range(QC):
                        last = nc.vector.max_index(out=IDX[:, qc, :], in_max=TOP[:, qc, :], in_values=BI[:, qc, :])
                    last.then_inc(gate_step, 1)
                if s == 6:
                    step(8)
                    nc.vector.tensor_copy(IDXF[:], IDX[:, :, 0:TOPK]).then_inc(gate_step, 1)
                    step(9)
                    for k in range(TOPK):
                        last = nc.vector.tensor_tensor(PICK[:, k], IOTA[:].unsqueeze(1).to_broadcast([P, QC, NE]),
                                                       IDXF[:, :, k:k + 1].to_broadcast([P, QC, NE]), ALU.is_equal)
                    last.then_inc(gate_step, 1)
                    step(10)
                    nc.vector.tensor_tensor(PICK[:, 0], PICK[:, 0], PICK[:, 1], ALU.add).then_inc(gate_step, 1)
                    step(11)
                    if due(before := b.done(EXP_ALL, -EXP_ALL)):
                        dve.wait_ge(y_added, before)
                    nc.vector.tensor_tensor(CW[:, b.par, :, 0:NE], PICK[:, 0], SC[:], ALU.mult).then_inc(gate_step, 1)

            def products(b, e):
                for gl, T in enumerate((G, L)):
                    k = 2 * e + gl
                    dve.wait_ge(h3_psum, b.done(2 * EXP_ALL, k + 1))
                    dve.wait_ge(a1_ready, b.done(2 * EXP_ALL, k + 1))
                    if due(before := b.done(EXP_ALL, e - 1)):
                        dve.wait_ge(gate_done if gl == 0 else ha_ready, before)
                    nc.vector.scalar_tensor_tensor(out=T[:, (b.par + e) % 2, :], in0=psH[(4 * e + 2 * gl + 1) % RING][:],
                                                   scalar=BIAS[:, 1, gl, e:e + 1], in1=A1[:, (b.par + e) % 2, gl, :],
                                                   op0=ALU.add, op1=ALU.mult).then_inc(gl_ready, 1)
                dve.wait_ge(gl_ready, b.done(2 * EXP_ALL, 2 * e + 1))
                nc.vector.tensor_scalar(G[:, (b.par + e) % 2, :], G[:, (b.par + e) % 2, :], LIMIT, None, ALU.min).then_inc(g_clip, 1)
                dve.wait_ge(gl_ready, b.done(2 * EXP_ALL, 2 * e + 2))
                nc.vector.tensor_scalar(L[:, (b.par + e) % 2, :], L[:, (b.par + e) % 2, :], LIMIT, -LIMIT, ALU.min, ALU.max).then_inc(l_clip, 1)

            def gated(b, e):
                dve.wait_ge(tanh_done, b.done(EXP_ALL, e + 1))
                if due(before := b.done(EXP_ALL, e - 1)):
                    dve.wait_ge(ha_ready, before)
                nc.vector.scalar_tensor_tensor(out=GT[:, (b.par + e) % 2, :], in0=TH[:, (b.par + e) % 2, :], scalar=1.0, in1=G[:, (b.par + e) % 2, :],
                                               op0=ALU.add, op1=ALU.mult).then_inc(gate_done, 1)

            def add(b, e):
                dve.wait_ge(y_psum, b.done(EXP_ALL, e + 1))
                y = psY[:].rearrange("p (q c) -> p q c", q=QC)
                if e == 0:
                    dve.wait_ge(gate_step, b.done(GATE_STEPS, GATE_STEPS))
                    if due(before := b.done(1, 0)):
                        dve.wait_ge(z_ready, before)
                else:
                    if due(before := b.done(EXP_ALL, e)):
                        dve.wait_ge(y_added, before)
                if e == NE:
                    nc.vector.tensor_tensor(ACC[:], y, ACC[:], ALU.add).then_inc(y_added, 1)
                    return
                for qc in range(QC):
                    w = CW[:, b.par, qc, e:e + 1]
                    if e == 0:
                        last = nc.vector.tensor_scalar(ACC[:, qc, :], y[:, qc, :], w, None, ALU.mult)
                    else:
                        last = nc.vector.scalar_tensor_tensor(out=ACC[:, qc, :], in0=y[:, qc, :], scalar=w,
                                                              in1=ACC[:, qc, :], op0=ALU.mult, op1=ALU.add)
                last.then_inc(y_added, 1)

            def finish(b, s):
                if s == 1:
                    dve.wait_ge(y_added, b.done(EXP_ALL, EXP_ALL))
                    for qc in range(QC):
                        last = nc.vector.bn_stats(ST3[:, qc, :], ACC[:, qc, :])
                    last.then_inc(stats3, 1)
                    dve.wait_ge(stats3, b.done(1, 1))
                    dve.sem_inc(passed, 1)
                    for qc in range(QC):
                        last = nc.vector.bn_aggr(MV3[:, qc, :], ST3[:, qc, :])
                    last.then_inc(aggr3, 1)
                if s == 2:
                    dve.wait_ge(rstd3, b.done(1, 1))
                    if due(before := b.done(1, 0)):
                        dve.wait_ge(x2_ready, before)
                    for qc in range(QC):
                        last = nc.vector.tensor_scalar(Z[:, qc, :], ACC[:, qc, :], MV3[:, qc, 0:1], RS3[:, qc:qc + 1],
                                                       ALU.subtract, ALU.mult)
                    last.then_inc(z_ready, 1)

            def iteration(t):
                nxt, prev = t + 1, t + (-1)
                for e in range(EXP_ALL):
                    if t.live:
                        products(t, e)
                    if e == 0 and prev.live:
                        gated(prev, NE)
                    if t.live and e > 0:
                        gated(t, e - 1)
                    if prev.live:
                        if e < 2:
                            add(prev, NE - 1 + e)
                        finish(prev, e)
                    if t.live and e > 1:
                        add(t, e - 2)
                    if nxt.live:
                        prepare(nxt, e)

            everywhere(iteration)(dve)

        @block.gpsimd
        def _(pool):
            nc.gpsimd.iota(IOTA[:], pattern=[[1, NE]], base=0, channel_multiplier=0,
                           allow_small_or_imprecise_dtypes=True).then_inc(iota_done, 1)
            pool.wait_ge(ready, 1)

            def rsqrt(b, MV, VE, RS, aggr, eps, rstd, free):
                pool.wait_ge(aggr, b.done(1, 1))
                pool.sem_inc(passed, 1)
                nc.gpsimd.tensor_scalar(VE[:], MV[:, :, 1], 1.0, EPS, ALU.mult, ALU.add).then_inc(eps, 1)
                pool.wait_ge(eps, b.done(1, 1))
                if due(before := b.done(1, 0)):
                    pool.wait_ge(free, before)
                nc.gpsimd.tensor_tensor(RS[:], VE[:], NHALF[:], ALU.pow).then_inc(rstd, 1)

            def act_out(b, e):
                pool.wait_ge(gate_done, b.done(EXP_ALL, e + 1))
                pool.wait_ge(l_plus, b.done(EXP_ALL, e + 1))
                if due(before := b.done(EXP_ALL, e - 1)):
                    pool.wait_ge(y_psum, before)
                nc.gpsimd.tensor_tensor(HA[:, (b.par + e) % 2, :], GT[:, (b.par + e) % 2, :], L[:, (b.par + e) % 2, :], ALU.mult).then_inc(ha_ready, 1)

            def iteration(t):
                nxt, prev = t + 1, t + (-1)
                for e in range(EXP_ALL):
                    if e == 0 and prev.live:
                        act_out(prev, NE)
                    if t.live and e > 0:
                        act_out(t, e - 1)
                    if e == 0 and nxt.live:
                        rsqrt(nxt, MV2, VE2, RS2, aggr2, eps2, rstd2, xn_ready)
                    if e == 1 and prev.live:
                        rsqrt(prev, MV3, VE3, RS3, aggr3, eps3, rstd3, z_ready)
                    if e == 3 and prev.live:
                        pool.wait_ge(z_ready, prev.done(1, 1))
                        if due(before := (prev + (-2)).done_par(16)):
                            pool.wait_ge(stored[prev.par], before)
                        nc.gpsimd.tensor_tensor(OUT[:, prev.par], X[:, bass.ds(prev.number() * QC, QC), :], Z[:],
                                                ALU.add).then_inc(x2_ready, 1)

            everywhere(iteration)(pool)


def build(nc, x, wqkvT, chan, bv, cos, sin, perm, ident, gate_wT, gate_b, w1T, w3T, w2T, hb, b2, out):
    ctx = ExitStack()
    with ctx:
        def sb(name, shape):
            return ctx.enter_context(nc.sbuf_tensor(name, shape, F32))

        X = sb("X", [P, B * QC, C])
        W1 = sb("W1", [P, EXP_ALL, 2 * F])
        W3 = sb("W3", [P, EXP_ALL, 2 * F])
        W2 = sb("W2", [P, EXP_ALL, C])
        weights = ctx.enter_context(nc.semaphore("weights_loaded"))

        def load_weights(eng):
            for dst, src in ((W1, w1T), (W3, w3T), (W2, w2T)):
                eng.dma_start(dst[:], src).then_inc(weights, 16)

        attention(nc, x, wqkvT, chan, bv, cos, sin, perm, ident, X, load_weights)
        experts(nc, gate_wT, gate_b, W1, W3, W2, weights, hb, b2, ident, X, out)


def host_constants():
    import numpy as np
    div = np.exp(np.arange(0, D, 2, dtype=np.float32) * np.float32(-np.log(10000.0) / D)).astype(np.float32)
    angle = (np.arange(N, dtype=np.float32)[:, None] * div).astype(np.float32)
    freq = (np.arange(C) % D) // 2
    cos = np.cos(angle.astype(np.float64)).astype(np.float32).T[freq]
    sin = np.sin(angle.astype(np.float64)).astype(np.float32).T[freq]
    perm = np.zeros((C, C), np.float32)
    for j in range(0, C, 2):
        perm[j + 1, j] = -1.0
        perm[j, j + 1] = 1.0
    return dict(cos=cos, sin=sin, perm=perm, ident=np.eye(P, dtype=np.float32))


_INPUTS = ("x", "wqkvT", "chan", "bv", "cos", "sin", "perm", "ident", "gate_wT", "gate_b", "w1T", "w3T", "w2T", "hb", "b2")


def kernel(**inputs):
    import numpy as np
    import concourse.bacc as bacc
    from concourse.bass_utils import run_bass_kernel_spmd

    a = {k: np.asarray(v) for k, v in inputs.items()}
    stack = lambda routed, shared: np.concatenate([a["L0_ffn_" + routed], a["L0_ffn_" + shared][None]])
    both = lambda m: stack("b" + m, "sb" + m).reshape(EXP_ALL, F, 2)
    laid = dict(
        x=a["L0_attn_x"].reshape(B * QC, P, C),
        wqkvT=a["L0_attn_w_qkv"].T,
        chan=np.concatenate([a["L0_attn_b_qkv"].reshape(3, C).T, a["L0_attn_w_lepe"][:, 0, :],
                             a["L0_attn_b_lepe"][:, None]], 1),
        bv=a["L0_attn_b_qkv"][2 * C:],
        gate_wT=a["L0_ffn_gate_w"].T,
        gate_b=a["L0_ffn_gate_b"],
        w1T=stack("w1", "sw1").transpose(2, 0, 1),
        w3T=stack("w3", "sw3").transpose(2, 0, 1),
        w2T=stack("w2", "sw2").transpose(2, 0, 1),
        hb=np.stack([both("1"), both("3")]).transpose(2, 0, 3, 1),
        b2=stack("b2", "sb2"),
        **host_constants(),
    )
    nc = bacc.Bacc("TRN2", target_bir_lowering=False, num_devices=1)
    arrays, args = {}, []
    for name in _INPUTS:
        v = np.ascontiguousarray(laid[name])
        arrays["in_" + name] = v
        args.append(nc.dram_tensor("in_" + name, v.shape, mybir.dt.from_np(v.dtype), kind="ExternalInput").ap())
    args.append(nc.dram_tensor("out_0", (B * QC, P, C), F32, kind="ExternalOutput").ap())
    build(nc, *args)
    r = run_bass_kernel_spmd(nc, [arrays], core_ids=[0])
    return r.results[0]["out_0"].reshape(B, N, C)
```

```python
import concourse.bass as bass
from concourse import mybir
from contextlib import ExitStack

F32 = mybir.dt.float32
F32R = mybir.dt.float32r
BF16 = mybir.dt.bfloat16
I32 = mybir.dt.int32
U32 = mybir.dt.uint32
ALU = mybir.AluOpType
ACT = mybir.ActivationFunctionType
AX = mybir.AxisListType

P = 128
B, N, C = 16, 512, 128
H, D = 16, 8
QC = N // P
NE, TOPK, F = 8, 2, 128
EXP_ALL = NE + 1
ALPHA, LIMIT, EPS = 1.702, 7.0, 1e-5
SCALE = 1.0 / (D ** 0.5)

PARTS = 3
ROWS_QK = PARTS * PARTS * D
ROWS_ALL = ROWS_QK + PARTS
QPARTS = 2 * PARTS - 1
HALF = H // 2
HG = 4
VW = 32
FIRST = 3
S_BANKS = 3
TILES = H * QC
SLOTS = H


class Batch:

    def __init__(self, i, c):
        self.i, self.c = i, c

    def __add__(self, k):
        return Batch(self.i, self.c + k)

    def number(self):
        return self.c if isinstance(self.i, int) else self.i * 2 + self.c

    @property
    def par(self):
        return self.c % 2

    @property
    def live(self):
        return not isinstance(self.i, int) or 0 <= self.c < B

    def done(self, per, extra=0):
        if isinstance(self.i, int):
            return self.c * per + extra
        return self.i * (2 * per) + (self.c * per + extra)

    def done_par(self, per):
        return (self.i + (self.c // 2 + 1)) * per


def due(count):
    return not isinstance(count, int) or count > 0


def attention(nc, x_in, wqkvT, chan, bv, rope_cos, rope_sin, perm, ident, X, load_weights):
    nc.disable_value_cache = True
    es = ExitStack()
    with es:
        def sb(name, shape, dt):
            return es.enter_context(nc.sbuf_tensor(name, shape, dt))

        def sem(name):
            return es.enter_context(nc.semaphore(name))

        WQKV = sb("WQKV", [P, 3 * C], F32)
        PERM = sb("PERM", [P, P], F32)
        IDF = sb("IDF", [P, P], F32)
        IDB = sb("IDB", [P, P], BF16)
        CHAN = sb("CHAN", [P, 7], F32)
        BP1 = sb("BP1", [P, 2], F32)
        BV = sb("BV", [P, C], F32)
        COS = sb("COS", [P, N], F32)
        SIN = sb("SIN", [P, N], F32)
        NHALF = sb("NHALF", [P, QC], F32)
        ST0 = sb("ST0", [P, QC, 6], F32)
        MV0 = sb("MV0", [P, QC, 2], F32)
        VE0 = sb("VE0", [P, QC], F32)
        RS0 = sb("RS0", [P, QC], F32)
        XN = sb("XN", [P, QC, C], F32)
        ST1 = sb("ST1", [P, QC, 6], F32)
        MV1 = sb("MV1", [P, QC, 2], F32)
        VE1 = sb("VE1", [P, QC], F32)
        RS1 = sb("RS1", [P, QC], F32)
        SH1 = sb("SH1", [P, QC], F32)
        Y = sb("Y", [P, 2, QC, C], F32)
        Z = sb("Z", [P, QC, C], F32)
        REC = sb("REC", [P, QC, HG], F32)
        MX = sb("MX", [P, QC, H], F32)
        MP = sb("MP", [P, 2, QC, PARTS, HALF], BF16)
        MR = sb("MR", [P, 2, QC, HALF], F32)
        XT = sb("XT", [P, 2, N], F32)
        EXQ = sb("EXQ", [P, 2, N], F32)
        EL = sb("EL", [P, 2, N], F32)
        ROT = sb("ROT", [P, 2, N], F32)
        RES = sb("RES", [P, 2, N], F32)
        PT = sb("PT", [P, 2, PARTS, N], BF16)
        VT = sb("VT", [P, N + 2], F32)
        TAP = sb("TAP", [P, N], F32)
        LP = sb("LP", [P, 2, N], F32)
        MT = sb("MT", [PARTS * HALF, 2, N], BF16)
        QS = [sb(f"QS{i}", [P, H, N], BF16) for i in range(2)]
        KS = [sb(f"KS{i}", [P, H, N], BF16) for i in range(2)]
        V = [sb(f"V{i}", [P, QC, H, VW], F32) for i in range(2)]
        PR = sb("PR", [P, 2, HG, N], F32)
        OT = sb("OT", [P, 2, N], F32)

        psST = [es.enter_context(nc.psum_tensor(f"psST{i}", [P, N], F32)) for i in range(2)]
        psS = [es.enter_context(nc.psum_tensor(f"psS{i}", [P, N], F32)) for i in range(S_BANKS)]
        psPV = es.enter_context(nc.psum_tensor("psPV", [P, N], F32))
        psM = [es.enter_context(nc.psum_tensor(f"psM{i}", [P, N], F32)) for i in range(2)]

        SCR = [nc.dram_tensor(f"scratch_parts{w}", [2, H, QPARTS, D, N], BF16, kind="Internal").ap() for w in range(2)]
        SCM = nc.dram_tensor("scratch_max", [2, 2, PARTS * HALF, N], BF16, kind="Internal").ap()

        consts = sem("consts_loaded")
        passed = sem("passed")
        zeros_set, ones_set, lead = sem("zeros_set"), sem("ones_set"), sem("constants_set")
        x_loaded = [sem(f"x_loaded{i}") for i in range(2)]
        stats0, aggr0, eps0, rstd0, xn_ready = (sem(s) for s in ("stats0", "aggr0", "eps0", "rstd0", "xn_ready"))
        xT_psum, xT_ready = sem("xT_psum"), sem("xT_ready")
        qk_psum = [sem(f"qk_psum{w}") for w in range(2)]
        qk_exp = [sem(f"qk_exp{w}") for w in range(2)]
        qk_min = [sem(f"qk_min{w}") for w in range(2)]
        qk_elu = [sem(f"qk_elu{w}") for w in range(2)]
        rot_psum = [sem(f"rot_psum{w}") for w in range(2)]
        rot_cos = [sem(f"rot_cos{w}") for w in range(2)]
        rot_sin = [sem(f"rot_sin{w}") for w in range(2)]
        rot_sum = [sem(f"rot_sum{w}") for w in range(2)]
        part1 = [sem(f"part1_{w}") for w in range(2)]
        resid = [sem(f"resid{w}") for w in range(2)]
        part2 = [sem(f"part2_{w}") for w in range(2)]
        part3 = [sem(f"part3_{w}") for w in range(2)]
        parts_stored = [sem(f"parts_stored{w}") for w in range(2)]
        stacked = [[sem(f"stacked{p}{h}") for h in range(2)] for p in range(2)]
        s_psum = sem("s_psum")
        s_max = sem("s_max")
        mx_step = [sem(f"max_split_step{h}") for h in range(2)]
        mT_psum = sem("mT_psum")
        mT_ready = sem("mT_ready")
        m_stored = sem("m_stored")
        m_stacked = [[sem(f"m_stacked{p}{h}") for h in range(2)] for p in range(2)]
        st_psum = sem("st_psum")
        st_exp = sem("st_exp")
        pv_done = sem("pv_done")
        ot_ready = sem("ot_ready")
        oT_psum = sem("oT_psum")
        recip = sem("recip")
        o_norm = sem("o_norm")
        v_psum, v_ready = sem("v_psum"), sem("v_ready")
        vT_psum, vT_ready = sem("vT_psum"), sem("vT_ready")
        lepe_mid = sem("lepe_mid")
        tap_ready, tap_added = sem("tap_ready"), sem("tap_added")
        lepeT_psum, y_ready = sem("lepeT_psum"), sem("y_ready")
        stats1, aggr1, eps1, rstd1, shift1, z_ready, x1_ready = (
            sem(s) for s in ("stats1", "aggr1", "eps1", "rstd1", "shift1", "z_ready", "x1_ready"))

        NCONST = 7
        LOADS = 3 * 16 * 2
        MISC = ["xT", "mT1", "q", "k", "O3", "Rq", "Rk", "O0", "lepeT", "mT0", "O1", "V", "vT", "O2"]

        def misc_bank(use):
            return psM[MISC.index(use) % 2]

        READER = {"xT": (2, xT_ready, 1, 1), "mT1": (0, mT_ready, 2, 2), "q": (2, qk_elu[0], 1, 1),
                  "O3": (-1, o_norm, 4, 4), "k": (2, qk_elu[1], 1, 1), "Rq": (2, rot_sin[0], 1, 1),
                  "Rk": (2, rot_sin[1], 1, 1), "O0": (0, o_norm, 4, 1), "lepeT": (-1, y_ready, 1, 1),
                  "mT0": (1, mT_ready, 2, 1), "O1": (0, o_norm, 4, 2), "V": (1, v_ready, 1, 1),
                  "vT": (1, vT_ready, 1, 1), "O2": (0, o_norm, 4, 3)}

        def misc_freed(pe, t, use):
            n = MISC.index(use)
            for back in range(2, 2 * len(MISC), 2):
                turn, m = divmod(n - back, len(MISC))
                of, reader, per, mine = READER[MISC[m]]
                b = t + turn + of
                if b.live:
                    pe.wait_ge(reader, b.done(per, mine))
                    return

        def s_bank(k):
            return psS[1 if k == TILES - 1 else k % S_BANKS]

        def s_before(k):
            return {0: -4, 1: -1, 2: -2, TILES - 1: TILES - 3}.get(k, k - S_BANKS)

        def everywhere(emit):
            def loop(eng):
                for c in range(-3, FIRST):
                    emit(Batch(0, c))
                with eng.Fori(0, (B - 3 - FIRST) // 2) as i:
                    emit(Batch(i, FIRST))
                    emit(Batch(i, FIRST + 1))
                for c in range(B - 3, B + 1):
                    emit(Batch(0, c))
            return loop

        block = es.enter_context(nc.Block())

        @block.sync
        def _(sp):
            def load_x(b):
                if due(before := (b + (-2)).done_par(16)):
                    sp.wait_ge(x_loaded[b.par], before)
                sp.dma_start(X[:, bass.ds(b.number() * QC, QC), :],
                             x_in[bass.ds(b.number() * QC, QC)].rearrange("q p c -> p q c")).then_inc(x_loaded[b.par], 16)

            def iteration(t):
                if (t + 3).live:
                    load_x(t + 3)
                b = t + 1
                if t.live:
                    send_max(t, 1)
                if b.live:
                    send_max(b, 0)
                b2 = t + 2
                if b2.live:
                    for w in range(2):
                        for a in range(PARTS if w else QPARTS):
                            if a == 0:
                                sp.wait_ge(part3[w], b2.done(1, 1))
                                for hf in range(2):
                                    if due(before := (b2 + (-2)).done_par(LOADS)):
                                        sp.wait_ge(stacked[b2.par][hf], before)
                            sp.dma_start(SCR[w][b2.par, :, a], PT[:, w, a % PARTS, :]).then_inc(parts_stored[w], 16)
                    stack(t, b2, 0)
                    stack(t, b2, 1)

            def stack(t, b, hf):
                sp.wait_ge(lead, 3)
                for w in range(2):
                    sp.wait_ge(parts_stored[w], b.done(16 * (PARTS if w else QPARTS), 16 * (PARTS if w else QPARTS)))
                if t.live:
                    sp.wait_ge(st_psum, t.done(64, 32 * (hf + 1)))
                for w, S in enumerate((QS, KS)):
                    for r in range(PARTS):
                        first = 0 if w else r
                        sp.dma_start(S[b.par][24 * r:24 * r + 24, HALF * hf:HALF * hf + HALF, :],
                                     SCR[w][b.par, HALF * hf:HALF * hf + HALF, first:first + PARTS].rearrange(
                                         "h a d n -> (a d) h n")).then_inc(stacked[b.par][hf], 16)

            def send_max(b, hf):
                sp.wait_ge(mT_ready, b.done(2, hf + 1))
                sp.dma_start(SCM[b.par, hf], MT[:, hf, :]).then_inc(m_stored, 16)
                sp.wait_ge(m_stored, b.done(32, 16 * (hf + 1)))
                sp.dma_start(QS[b.par][ROWS_QK:ROWS_ALL, HALF * hf:HALF * hf + HALF, :],
                             SCM[b.par, hf].rearrange("(a h) n -> a h n", a=PARTS)).then_inc(m_stacked[b.par][hf], 16)

            everywhere(iteration)(sp)

        @block.tensor
        def _(pe):
            pe.wait_ge(consts, 16 * NCONST)
            pe.wait_ge(lead, 3)

            def scores_t(t, h, kc, k):
                if kc == 0 and h % HALF == 0:
                    hf = h // HALF
                    pe.wait_ge(stacked[t.par][hf], t.done_par(LOADS))
                    pe.wait_ge(m_stacked[t.par][hf], t.done_par(16))
                if due(before := t.done(64, k - 1)):
                    pe.wait_ge(st_exp, before)
                nc.tensor.matmul(psST[k % 2][:], KS[t.par][0:ROWS_ALL, h, kc * P:(kc + 1) * P],
                                 QS[t.par][0:ROWS_ALL, h, :], start=True, stop=True).then_inc(st_psum, 1)

            def scores(b, h, qc, k):
                if qc == 0 and h % HALF == 0:
                    pe.wait_ge(stacked[b.par][h // HALF], b.done_par(LOADS))
                if due(before := b.done(TILES, s_before(k) + 1)):
                    pe.wait_ge(s_max, before)
                nc.tensor.matmul(s_bank(k)[:], QS[b.par][0:ROWS_QK, h, qc * P:(qc + 1) * P],
                                 KS[b.par][0:ROWS_QK, h, :], start=True, stop=True).then_inc(s_psum, 1)

            def values(b, s):
                g, kc = divmod(s, QC)
                if s == 0:
                    pe.wait_ge(v_ready, b.done(1, 1))
                if kc == 0:
                    if due(before := b.done(4, g)):
                        pe.wait_ge(ot_ready, before)
                pe.wait_ge(st_exp, b.done(64, 4 * s + 4))
                for j in range(HG):
                    last = nc.tensor.matmul(psPV[VW * j:VW * j + VW, :], V[b.par][:, kc, HG * g + j, :],
                                            PR[:, s % 2, j, :], start=(kc == 0), stop=(kc == QC - 1))
                last.then_inc(pv_done, 1)

            def out_transposes(b, g, use):
                pe.wait_ge(ot_ready, b.done(4, g + 1))
                m = misc_bank(use)
                for qc in range(QC):
                    last = nc.tensor.transpose(m[:, qc * P:(qc + 1) * P], OT[:, g % 2, qc * P:(qc + 1) * P], IDF[:])
                last.then_inc(oT_psum, 1)

            def misc(t, s):
                nxt, prep, prev = t + 1, t + 2, t + (-1)
                if s == 0 and prep.live:
                    misc_freed(pe, t, "xT")
                    pe.wait_ge(xn_ready, prep.done(1, 1))
                    m = misc_bank("xT")
                    for qc in range(QC):
                        last = nc.tensor.transpose(m[:, qc * P:(qc + 1) * P], XN[:, qc, :], IDF[:])
                    last.then_inc(xT_psum, 1)
                if s == 1 and t.live:
                    misc_freed(pe, t, "mT1")
                    max_transposes(t, 1, "mT1")
                if s == 2 and prep.live:
                    misc_freed(pe, t, "q")
                    project(prep, 0, "q")
                if s == 3 and prep.live:
                    misc_freed(pe, t, "k")
                    project(prep, 1, "k")
                if s == 4 and prev.live:
                    misc_freed(pe, t, "O3")
                    out_transposes(prev, 3, "O3")
                if s in (5, 6) and prep.live:
                    w = s - 5
                    use = ("Rq", "Rk")[w]
                    misc_freed(pe, t, use)
                    pe.wait_ge(qk_elu[w], prep.done(1, 1))
                    nc.tensor.matmul(misc_bank(use)[:], PERM[:], EL[:, w, :], start=True, stop=True).then_inc(rot_psum[w], 1)
                if s == 7 and t.live:
                    misc_freed(pe, t, "O0")
                    out_transposes(t, 0, "O0")
                if s == 8 and prev.live:
                    misc_freed(pe, t, "lepeT")
                    pe.wait_ge(tap_added, prev.done(2, 2))
                    m = misc_bank("lepeT")
                    for qc in range(QC):
                        last = nc.tensor.transpose(m[:, qc * P:(qc + 1) * P], LP[:, prev.par, qc * P:(qc + 1) * P], IDF[:])
                    last.then_inc(lepeT_psum, 1)
                if s == 9 and nxt.live:
                    misc_freed(pe, t, "mT0")
                    max_transposes(nxt, 0, "mT0")
                if s == 10 and t.live:
                    misc_freed(pe, t, "O1")
                    out_transposes(t, 1, "O1")
                if s == 11 and nxt.live:
                    misc_freed(pe, t, "V")
                    pe.wait_ge(xT_ready, nxt.done(1, 1))
                    m = misc_bank("V")
                    for kc in range(QC):
                        last = nc.tensor.matmul(m[:, kc * P:(kc + 1) * P], XT[:, nxt.par, kc * P:(kc + 1) * P],
                                                WQKV[:, 2 * C:3 * C], start=True, stop=True)
                    last.then_inc(v_psum, 1)
                if s == 12 and nxt.live:
                    misc_freed(pe, t, "vT")
                    nc.tensor.matmul(misc_bank("vT")[:], WQKV[:, 2 * C:3 * C], XT[:, nxt.par, :],
                                     start=True, stop=True).then_inc(vT_psum, 1)
                if s == 14 and t.live:
                    misc_freed(pe, t, "O2")
                    out_transposes(t, 2, "O2")

            def max_transposes(b, hf, use):
                pe.wait_ge(mx_step[hf], b.done(5, 5))
                m = misc_bank(use)[0:PARTS * HALF, 0:N // 2].bitcast(BF16)
                for qc in range(QC):
                    last = nc.tensor.transpose(m[:, qc * P:(qc + 1) * P],
                                               MP[:, hf, qc, :, :].rearrange("p a h -> p (a h)"), IDB[:])
                last.then_inc(mT_psum, 1)

            def project(b, w, use):
                pe.wait_ge(xT_ready, b.done(1, 1))
                nc.tensor.matmul(misc_bank(use)[:], WQKV[:, w * C:(w + 1) * C], XT[:, b.par, :],
                                 start=True, stop=True).then_inc(qk_psum[w], 1)

            def iteration(t):
                nxt, prev = t + 1, t + (-1)
                for s in range(SLOTS):
                    g, kc = divmod(s, QC)
                    for j in range(HG):
                        if t.live:
                            scores_t(t, HG * g + j, kc, 4 * s + j)
                        if nxt.live:
                            scores(nxt, s, j, 4 * s + j)
                        if j == 1:
                            if s == 0 and prev.live:
                                values(prev, SLOTS - 1)
                            if s > 0 and t.live:
                                values(t, s - 1)
                    misc(t, s)

            everywhere(iteration)(pe)

        @block.scalar
        def _(act):
            for dst, src in ((IDF[:], ident), (WQKV[:], wqkvT), (CHAN[:], chan), (PERM[:], perm),
                             (COS[:], rope_cos), (SIN[:], rope_sin), (BV[:], bv.unsqueeze(0).to_broadcast([P, C]))):
                act.dma_start(dst, src).then_inc(consts, 16)
            load_weights(act)
            act.wait_ge(consts, 16 * NCONST)
            act.wait_ge(lead, 3)

            def extra(t, s):
                nxt, prep, prev = t + 1, t + 2, t + (-1)
                if s in (0, 4, 8, 12):
                    b, g = (prev, 3) if s == 0 else (t, s // 4 - 1)
                    if b.live:
                        act.wait_ge(pv_done, b.done(16, 4 * g + 4))
                        if due(before := b.done(4, g - 1)):
                            act.wait_ge(oT_psum, before)
                        nc.scalar.activation(OT[:, g % 2, :], psPV[:], ACT.Copy).then_inc(ot_ready, 1)
                if s == 1 and prep.live:
                    act.wait_ge(xT_psum, prep.done(1, 1))
                    if due(before := (prep + (-2)).done(1, 1)):
                        act.wait_ge(vT_psum, before)
                    nc.scalar.activation(XT[:, prep.par, :], misc_bank("xT")[:], ACT.Copy).then_inc(xT_ready, 1)
                if s == 2 and t.live:
                    copy_max(t, 1, "mT1")
                if s in (3, 4) and prep.live:
                    w = s - 3
                    act.wait_ge(qk_psum[w], prep.done(1, 1))
                    if due(before := prep.done(1, 0)):
                        act.wait_ge(qk_elu[w], before)
                    nc.scalar.activation(EXQ[:, w, :], misc_bank("qk"[w])[:], ACT.Exp,
                                         bias=CHAN[:, w:w + 1]).then_inc(qk_exp[w], 1)
                if s in (8, 9) and prep.live:
                    w = s - 8
                    act.wait_ge(rot_sum[w], prep.done(1, 1))
                    if due(before := prep.done(16 * (PARTS if w else QPARTS), 0)):
                        act.wait_ge(parts_stored[w], before)
                    nc.scalar.activation(PT[:, w, 0, :], ROT[:, w, :], ACT.Copy).then_inc(part1[w], 1)
                if s in (10, 11) and prep.live:
                    w = s - 10
                    act.wait_ge(resid[w], prep.done(1, 1))
                    nc.scalar.activation(PT[:, w, 1, :], RES[:, w, :], ACT.Copy).then_inc(part2[w], 1)
                if s == 10 and nxt.live:
                    copy_max(nxt, 0, "mT0")
                if s == 13 and nxt.live:
                    act.wait_ge(vT_psum, nxt.done(1, 1))
                    if due(before := nxt.done(2, 0)):
                        act.wait_ge(tap_added, before)
                    nc.scalar.activation(VT[:, 1:N + 1], misc_bank("vT")[:], ACT.Identity,
                                         bias=CHAN[:, 2:3]).then_inc(vT_ready, 1)
                if s == 14 and nxt.live:
                    act.wait_ge(vT_ready, nxt.done(1, 1))
                    if due(before := (nxt + (-2)).done(1, 1)):
                        act.wait_ge(lepeT_psum, before)
                    nc.scalar.activation(LP[:, nxt.par, :], VT[:, 1:N + 1], ACT.Identity,
                                         bias=CHAN[:, 6:7], scale=CHAN[:, 4:5]).then_inc(lepe_mid, 1)

            def copy_max(b, hf, use):
                act.wait_ge(mT_psum, b.done(2, hf + 1))
                if due(before := b.done(32, 16 * (hf + 1) - 32)):
                    act.wait_ge(m_stored, before)
                nc.scalar.activation(MT[:, hf, :], misc_bank(use)[0:PARTS * HALF, 0:N // 2].bitcast(BF16),
                                     ACT.Copy).then_inc(mT_ready, 1)

            def iteration(t):
                for s in range(SLOTS):
                    for j in range(HG):
                        if t.live:
                            k = 4 * s + j
                            act.wait_ge(st_psum, t.done(64, k + 1))
                            if j == 0:
                                if due(before := t.done(16, s - 1)):
                                    act.wait_ge(pv_done, before)
                            nc.scalar.activation(PR[:, s % 2, j, :], psST[k % 2][:], ACT.Exp,
                                                 scale=SCALE).then_inc(st_exp, 1)
                    extra(t, s)

            everywhere(iteration)(act)

        @block.vector
        def _(dve):
            nc.vector.memset(VT[:], 0.0)
            for p in range(2):
                last = nc.vector.memset(V[p][:], 0.0)
            last.then_inc(zeros_set, 1)
            dve.wait_ge(zeros_set, 1)
            for p in range(2):
                last = nc.vector.memset(V[p][:, :, :, D:D + 1], 1.0)
            last.then_inc(lead, 1)
            dve.wait_ge(consts, 16 * NCONST)
            nc.vector.tensor_copy(IDB[:], IDF[:])
            nc.vector.tensor_scalar(BP1[:], CHAN[:, 0:2], 1.0, None, ALU.add).then_inc(lead, 1)
            dve.wait_ge(lead, 3)

            def elu(b, w):
                dve.wait_ge(qk_exp[w], b.done(1, 1))
                nc.vector.tensor_scalar(EXQ[:, w, :], EXQ[:, w, :], 1.0, None, ALU.min).then_inc(qk_min[w], 1)
                dve.wait_ge(qk_min[w], b.done(1, 1))
                if due(before := b.done(1, 0)):
                    dve.wait_ge(rot_cos[w], before)
                if due(before := b.done(1, 0)):
                    dve.wait_ge(rot_psum[w], before)
                nc.vector.scalar_tensor_tensor(out=EL[:, w, :], in0=misc_bank("qk"[w])[:], scalar=BP1[:, w:w + 1],
                                               in1=EXQ[:, w, :], op0=ALU.add, op1=ALU.max).then_inc(qk_elu[w], 1)

            def normalise(b, g, use):
                m = misc_bank(use)[:].rearrange("p (q j v) -> p q j v", q=QC, j=HG)
                dve.wait_ge(oT_psum, b.done(4, g + 1))
                if due(before := b.done(4, g)):
                    dve.wait_ge(o_norm, before)
                nc.vector.reciprocal(REC[:], m[:, :, :, D]).then_inc(recip, 1)
                dve.wait_ge(recip, b.done(4, g + 1))
                if g == 0:
                    if due(before := b.done(1, -1)):
                        dve.wait_ge(z_ready, before)
                y = Y[:, b.par, :, g * HG * D:(g + 1) * HG * D].rearrange("p q (j d) -> p q j d", j=HG)
                nc.vector.tensor_tensor(y, m[:, :, :, 0:D], REC[:].unsqueeze(3).to_broadcast([P, QC, HG, D]),
                                        ALU.mult).then_inc(o_norm, 1)

            def extra(t, s, j):
                nxt, prep, prev, far = t + 1, t + 2, t + (-1), t + 3
                if s in (4, 5) and j == 1 and prep.live:
                    elu(prep, s - 4)
                if s == 5 and j == 3 and prev.live:
                    normalise(prev, 3, "O3")
                if s in (6, 7) and j == 1 and prep.live:
                    w = s - 6
                    dve.wait_ge(rot_psum[w], prep.done(1, 1))
                    if due(before := prep.done(1, 0)):
                        dve.wait_ge(part3[w], before)
                    nc.vector.tensor_tensor(RES[:, w, :], misc_bank(("Rq", "Rk")[w])[:], SIN[:],
                                            ALU.mult).then_inc(rot_sin[w], 1)
                if s == 8 and j == 1 and t.live:
                    normalise(t, 0, "O0")
                if s == 9 and j == 1 and prev.live:
                    dve.wait_ge(lepeT_psum, prev.done(1, 1))
                    dve.wait_ge(o_norm, prev.done(4, 4))
                    nc.vector.tensor_tensor(Y[:, prev.par], misc_bank("lepeT")[:].rearrange("p (q c) -> p q c", q=QC),
                                            Y[:, prev.par],
                                            ALU.add).then_inc(y_ready, 1)
                if s == 11 and j == 1 and t.live:
                    normalise(t, 1, "O1")
                if s == 12 and j == 3 and nxt.live:
                    dve.wait_ge(v_psum, nxt.done(1, 1))
                    if due(before := (nxt + (-1)).done(16, 0)):
                        dve.wait_ge(pv_done, before)
                    nc.vector.tensor_tensor(
                        V[nxt.par][:, :, :, 0:D],
                        misc_bank("V")[:].rearrange("p (q h d) -> p q h d", q=QC, h=H),
                        BV[:].rearrange("p (h d) -> p h d", h=H).unsqueeze(1).to_broadcast([P, QC, H, D]),
                        ALU.add).then_inc(v_ready, 1)
                if s == 15 and j == 1 and t.live:
                    normalise(t, 2, "O2")
                if s == 10 and j == 1 and prev.live:
                    dve.wait_ge(y_ready, prev.done(1, 1))
                    for qc in range(QC):
                        last = nc.vector.bn_stats(ST1[:, qc, :], Y[:, prev.par, qc, :])
                    last.then_inc(stats1, 1)
                if s == 11 and j == 3 and prev.live:
                    dve.wait_ge(stats1, prev.done(1, 1))
                    if due(before := prev.done(1, 0)):
                        dve.wait_ge(z_ready, before)
                    dve.sem_inc(passed, 1)
                    for qc in range(QC):
                        last = nc.vector.bn_aggr(MV1[:, qc, :], ST1[:, qc, :])
                    last.then_inc(aggr1, 1)
                if s == 2 and j == 1 and far.live:
                    dve.wait_ge(x_loaded[far.par], far.done_par(16))
                    for qc in range(QC):
                        last = nc.vector.bn_stats(ST0[:, qc, :], X[:, far.number() * QC + qc, :])
                    last.then_inc(stats0, 1)
                if s == 3 and j == 2 and far.live:
                    dve.wait_ge(stats0, far.done(1, 1))
                    dve.sem_inc(passed, 1)
                    for qc in range(QC):
                        last = nc.vector.bn_aggr(MV0[:, qc, :], ST0[:, qc, :])
                    last.then_inc(aggr0, 1)
                if s == 13 and j == 2 and far.live:
                    dve.wait_ge(rstd0, far.done(1, 1))
                    if due(before := far.done(1, 0)):
                        dve.wait_ge(xT_psum, before)
                    for qc in range(QC):
                        last = nc.vector.tensor_scalar(XN[:, qc, :], X[:, far.number() * QC + qc, :], MV0[:, qc, 0:1],
                                                       RS0[:, qc:qc + 1], ALU.subtract, ALU.mult)
                    last.then_inc(xn_ready, 1)

            def iteration(t):
                nxt = t + 1
                for s in range(SLOTS):
                    for j in range(HG):
                        if nxt.live:
                            k = 4 * s + j
                            dve.wait_ge(s_psum, nxt.done(64, k + 1))
                            if s % HALF == 0 and j == 0:
                                if due(before := nxt.done(5, 0)):
                                    dve.wait_ge(mx_step[s // HALF], before)
                            nc.vector.tensor_reduce(out=MX[:, j, s:s + 1], in_=s_bank(k)[:], axis=AX.X,
                                                    op=ALU.max).then_inc(s_max, 1)
                        extra(t, s, j)

            everywhere(iteration)(dve)

        @block.gpsimd
        def _(pool):
            for p in range(2):
                nc.gpsimd.memset(KS[p][64:96, :, :], 1.0).then_inc(ones_set, 1)
                pool.wait_ge(ones_set, p + 1)
            nc.gpsimd.memset(NHALF[:], -0.5).then_inc(lead, 1)
            pool.wait_ge(consts, 16 * NCONST)
            pool.wait_ge(lead, 3)

            def split_max(b, hf):
                m = MX[:, :, HALF * hf:HALF * hf + HALF]
                n = [MP[:, hf, :, a, :] for a in range(PARTS)]
                r = MR[:, hf]
                pool.wait_ge(s_max, b.done(64, 32 * (hf + 1)))
                if due(before := b.done(2, hf - 1)):
                    pool.wait_ge(mT_psum, before)
                pool.sem_inc(passed, 1)
                step = mx_step[hf]
                nc.gpsimd.tensor_scalar(n[0], m, -1.0, 0.0, ALU.mult, ALU.add).then_inc(step, 1)
                pool.wait_ge(step, b.done(5, 1))
                nc.gpsimd.tensor_tensor(r, m, n[0], ALU.add).then_inc(step, 1)
                pool.wait_ge(step, b.done(5, 2))
                pool.sem_inc(passed, 1)
                nc.gpsimd.tensor_scalar(n[1], r, -1.0, 0.0, ALU.mult, ALU.add).then_inc(step, 1)
                pool.wait_ge(step, b.done(5, 3))
                nc.gpsimd.tensor_tensor(r, r, n[1], ALU.add).then_inc(step, 1)
                pool.wait_ge(step, b.done(5, 4))
                pool.sem_inc(passed, 1)
                nc.gpsimd.tensor_scalar(n[2], r, -1.0, 0.0, ALU.mult, ALU.add).then_inc(step, 1)

            def rsqrt(b, MV, VE, RS, aggr, eps, rstd, free):
                pool.wait_ge(aggr, b.done(1, 1))
                pool.sem_inc(passed, 1)
                nc.gpsimd.tensor_scalar(VE[:], MV[:, :, 1], 1.0, EPS, ALU.mult, ALU.add).then_inc(eps, 1)
                pool.wait_ge(eps, b.done(1, 1))
                if due(before := b.done(1, 0)):
                    pool.wait_ge(free, before)
                nc.gpsimd.tensor_tensor(RS[:], VE[:], NHALF[:], ALU.pow).then_inc(rstd, 1)

            def lepe(b):
                pool.wait_ge(lepe_mid, b.done(1, 1))
                for tap, (first, w) in enumerate(((0, 3), (2, 5))):
                    if due(before := b.done(2, tap)):
                        pool.wait_ge(tap_added, before)
                    pool.sem_inc(passed, 1)
                    nc.gpsimd.tensor_scalar(TAP[:], VT[:, first:first + N], CHAN[:, w:w + 1], 0.0, ALU.mult,
                                            ALU.add).then_inc(tap_ready, 1)
                    pool.wait_ge(tap_ready, b.done(2, tap + 1))
                    nc.gpsimd.tensor_tensor(LP[:, b.par, :], LP[:, b.par, :], TAP[:], ALU.add).then_inc(tap_added, 1)

            def iteration(t):
                nxt, prep, prev, far = t + 1, t + 2, t + (-1), t + 3
                if t.live:
                    split_max(t, 1)
                if far.live:
                    rsqrt(far, MV0, VE0, RS0, aggr0, eps0, rstd0, xn_ready)
                if t.live:
                    lepe(t)
                if prep.live:
                    for w in range(2):
                        pool.wait_ge(qk_elu[w], prep.done(1, 1))
                        if due(before := prep.done(1, 0)):
                            pool.wait_ge(resid[w], before)
                        nc.gpsimd.tensor_tensor(ROT[:, w, :], EL[:, w, :], COS[:], ALU.mult).then_inc(rot_cos[w], 1)
                    for w in range(2):
                        pool.wait_ge(rot_cos[w], prep.done(1, 1))
                        pool.wait_ge(rot_sin[w], prep.done(1, 1))
                        nc.gpsimd.tensor_tensor(ROT[:, w, :], ROT[:, w, :], RES[:, w, :], ALU.add).then_inc(rot_sum[w], 1)
                if nxt.live:
                    split_max(nxt, 0)
                for w in range(2):
                    if prep.live:
                        pool.wait_ge(part1[w], prep.done(1, 1))
                        nc.gpsimd.tensor_tensor(RES[:, w, :], ROT[:, w, :], PT[:, w, 0, :], ALU.subtract).then_inc(resid[w], 1)
                if prep.live:
                    for w in range(2):
                        pool.wait_ge(part2[w], prep.done(1, 1))
                        nc.gpsimd.tensor_tensor(PT[:, w, 2, :], RES[:, w, :], PT[:, w, 1, :], ALU.subtract).then_inc(part3[w], 1)
                if prev.live:
                    rsqrt(prev, MV1, VE1, RS1, aggr1, eps1, rstd1, z_ready)
                    pool.wait_ge(rstd1, prev.done(1, 1))
                    nc.gpsimd.tensor_tensor(SH1[:], MV1[:, :, 0], RS1[:], ALU.mult).then_inc(shift1, 1)
                    pool.wait_ge(shift1, prev.done(2, 1))
                    pool.sem_inc(passed, 1)
                    nc.gpsimd.tensor_scalar(SH1[:], SH1[:], -1.0, 0.0, ALU.mult, ALU.add).then_inc(shift1, 1)
                    pool.wait_ge(shift1, prev.done(2, 2))
                    if due(before := prev.done(1, 0)):
                        pool.wait_ge(x1_ready, before)
                    pool.wait_ge(y_ready, prev.done(1, 1))
                    pool.sem_inc(passed, 1)
                    for qc in range(QC):
                        last = nc.gpsimd.tensor_scalar(Z[:, qc, :], Y[:, prev.par, qc, :], RS1[:, qc:qc + 1],
                                                       SH1[:, qc:qc + 1], ALU.mult, ALU.add)
                    last.then_inc(z_ready, 1)
                    pool.wait_ge(z_ready, prev.done(1, 1))
                    x = X[:, bass.ds(prev.number() * QC, QC), :]
                    nc.gpsimd.tensor_tensor(x, x, Z[:], ALU.add).then_inc(x1_ready, 1)

            everywhere(iteration)(pool)


def experts(nc, gate_wT, gate_b, W1, W3, W2, weights, HB, B2, ident, X, out):
    es = ExitStack()
    with es:
        def sb(name, shape, dt):
            return es.enter_context(nc.sbuf_tensor(name, shape, dt))

        def sem(name):
            return es.enter_context(nc.semaphore(name))

        LAG = 3
        HA_BUFS = 3
        WH = [sb(f"WH{m}", [P, EXP_ALL, 2, F], F32R) for m in range(2)]
        WL = [sb(f"WL{m}", [P, EXP_ALL, 2, F], F32R) for m in range(2)]
        GH = sb("GH", [P, NE], F32R)
        GL = sb("GL", [P, NE], F32R)
        GW = sb("GW", [P, NE], F32)
        GB = sb("GB", [P, NE], F32)
        IDF = sb("IDFB", [P, P], F32)
        IOTA = sb("IOTA", [P, NE], F32)
        BIAS = sb("BIAS", [P, 2, 2, EXP_ALL], F32)
        BD = sb("BD", [EXP_ALL, C], F32)
        NHALF = sb("NHALFB", [P, QC], F32)

        ST2 = sb("ST2", [P, QC, 6], F32)
        MV2 = sb("MV2", [P, QC, 2], F32)
        VE2 = sb("VE2", [P, QC], F32)
        RS2 = sb("RS2", [P, QC], F32)
        ST3 = sb("ST3", [P, QC, 6], F32)
        MV3 = sb("MV3", [P, QC, 2], F32)
        VE3 = sb("VE3", [P, QC], F32)
        RS3 = sb("RS3", [P, QC], F32)
        XN = sb("XNB", [P, QC, C], F32)
        XH = sb("XH", [P, 2, N], F32R)
        XL = sb("XL", [P, 2, N], F32R)
        GM = sb("GM", [P, QC, 1], F32)
        GE = sb("GE", [P, QC, NE], F32)
        GS = sb("GS", [P, QC, 1], F32)
        GR = sb("GR", [P, QC, 1], F32)
        SC = sb("SC", [P, QC, NE], F32)
        BI = sb("BI", [P, QC, NE], F32)
        TOP = sb("TOP", [P, QC, 8], F32)
        IDX = sb("IDX", [P, QC, 8], U32)
        IDXF = sb("IDXF", [P, QC, TOPK], F32)
        PICK = sb("PICK", [P, TOPK, QC, NE], F32)
        CW = sb("CW", [P, 2, QC, EXP_ALL], F32)
        CWT = sb("CWT", [EXP_ALL, 2, N], F32)
        A1 = sb("A1", [P, 2, 2, N], F32)
        G = sb("G", [P, 2, N], F32)
        L = sb("L", [P, 2, N], F32)
        TH = sb("TH", [P, 2, N], F32)
        GT = sb("GT", [P, 2, N], F32)
        HA = sb("HA", [P, HA_BUFS, N], F32)
        YW = sb("YW", [P, 2, QC, C], F32)
        ACC = sb("ACC", [P, 2, QC, C], F32)
        Z = sb("ZB", [P, QC, C], F32)
        OUT = sb("OUT", [P, 2, QC, C], F32)

        RING = 6
        psH = [es.enter_context(nc.psum_tensor(f"psH{i}", [P, N], F32)) for i in range(RING)]
        psY = es.enter_context(nc.psum_tensor("psY", [P, N], F32))
        psX = es.enter_context(nc.psum_tensor("psX", [P, N], F32))

        consts, ready = sem("constsB_loaded"), sem("gate_split")
        split = sem("weights_split")
        passed = sem("passedB")
        iota_done, wh_ready = sem("iota_done"), sem("weights_high")
        stats2, aggr2, eps2, rstd2, xn_ready = (sem(s) for s in ("stats2", "aggr2", "eps2", "rstd2", "xn2_ready"))
        stats3, aggr3, eps3, rstd3, z_ready = (sem(s) for s in ("stats3", "aggr3", "eps3", "rstd3", "z3_ready"))
        xT_psum, xh_ready, xl_ready = sem("xT2_psum"), sem("xh_ready"), sem("xl_ready")
        logits_psum, logits_read = sem("logits_psum"), sem("logits_read")
        gate_step = sem("gate_step")
        gate_exp = sem("gate_exp")
        biased = sem("biased")
        cwT_psum, cwT_ready = sem("cwT_psum"), sem("cwT_ready")
        h1_psum, h3_psum = sem("h1_psum"), sem("h3_psum")
        a1_ready, gl_ready = sem("a1_ready"), sem("gl_ready")
        g_clip, l_clip = sem("g_clipped"), sem("l_clipped")
        tanh_done, l_plus = sem("tanh_done"), sem("l_plus")
        gate_done, ha_ready = sem("gate_done"), sem("ha_ready")
        y_psum, y_read = sem("y_psum"), sem("y_read")
        summed = sem("summed")
        x2_ready = sem("x2_ready")
        stored = [sem(f"stored{i}") for i in range(2)]
        NCONST = 5
        GATE_STEPS = 12
        SUMS = NE - 1

        def everywhere(emit):
            def loop(eng):
                for c in range(-1, FIRST):
                    emit(Batch(0, c))
                with eng.Fori(0, (B - 1 - FIRST) // 2) as i:
                    emit(Batch(i, FIRST))
                    emit(Batch(i, FIRST + 1))
                for c in (B - 1, B):
                    emit(Batch(0, c))
            return loop

        block = es.enter_context(nc.Block())

        @block.sync
        def _(sp):
            for dst, src in ((GW[:], gate_wT), (IDF[:], ident), (BIAS[:], HB), (BD[:], B2),
                             (GB[:], gate_b.unsqueeze(0).to_broadcast([P, NE]))):
                sp.dma_start(dst, src).then_inc(consts, 16)

            def iteration(t):
                b = t + (-1)
                if b.live:
                    sp.wait_ge(x2_ready, b.done(1, 1))
                    sp.dma_start(out[bass.ds(b.number() * QC, QC)].rearrange("q p c -> p q c"),
                                 OUT[:, b.par]).then_inc(stored[b.par], 16)

            everywhere(iteration)(sp)
            for p in range(2):
                sp.wait_ge(stored[p], 16 * (B // 2))

        @block.tensor
        def _(pe):
            pe.wait_ge(consts, 16 * NCONST)
            pe.wait_ge(ready, 2)

            def hidden(b, e, u):
                m, gl = u % 2, u // 2 % 2
                if isinstance(b.i, int) and b.c == 0 and u % 4 == 0:
                    pe.wait_ge(split, e + 1)
                if u == 0:
                    pe.wait_ge(xh_ready, b.done(1, 1))
                    pe.wait_ge(xl_ready, b.done(1, 1))
                v = u - RING
                if due(before := b.done(2 * EXP_ALL, v // 4 * 2 + v % 4 // 2 + 1)):
                    pe.wait_ge(gl_ready if m else a1_ready, before)
                ps = psH[u % RING]
                nc.tensor.matmul(ps[:], WH[m][:, e, gl, :], XH[:, b.par, :], start=True, stop=False)
                nc.tensor.matmul(ps[:], WH[m][:, e, gl, :], XL[:, b.par, :], start=False, stop=False)
                nc.tensor.matmul(ps[:], WL[m][:, e, gl, :], XH[:, b.par, :], start=False,
                                 stop=True).then_inc(h3_psum if m else h1_psum, 1)

            def down(b, e):
                pe.wait_ge(ha_ready, b.done(EXP_ALL, e + 1))
                if due(before := b.done(EXP_ALL, e)):
                    pe.wait_ge(y_read, before)
                shared = e == NE
                if shared:
                    pe.wait_ge(cwT_ready, b.done(1, 1))
                for qc in range(QC):
                    last = nc.tensor.matmul(psY[:, qc * P:(qc + 1) * P], HA[:, e % HA_BUFS, qc * P:(qc + 1) * P],
                                            W2[:, e, :], start=True, stop=not shared)
                    if shared:
                        last = nc.tensor.matmul(psY[:, qc * P:(qc + 1) * P], CWT[:, b.par, qc * P:(qc + 1) * P],
                                                BD[:], start=False, stop=True)
                last.then_inc(y_psum, 1)

            def prepare(b, s):
                if s == 2:
                    pe.wait_ge(xn_ready, b.done(1, 1))
                    if due(before := b.done(1, 0)):
                        pe.wait_ge(cwT_ready, before)
                    for qc in range(QC):
                        last = nc.tensor.transpose(psX[:, qc * P:(qc + 1) * P], XN[:, qc, :], IDF[:])
                    last.then_inc(xT_psum, 1)
                if s == 4:
                    pe.wait_ge(xh_ready, b.done(1, 1))
                    pe.wait_ge(xl_ready, b.done(1, 1))
                    for qc in range(QC):
                        o = psX[:, qc * NE:(qc + 1) * NE]
                        for n, (xx, ww) in enumerate(((XH, GH), (XL, GH), (XH, GL))):
                            last = nc.tensor.matmul(o, xx[:, b.par, qc * P:(qc + 1) * P], ww[:],
                                                    start=(n == 0), stop=(n == 2))
                    last.then_inc(logits_psum, 1)
                if s == EXP_ALL:
                    pe.wait_ge(gate_step, b.done(GATE_STEPS, GATE_STEPS))
                    for qc in range(QC):
                        last = nc.tensor.transpose(psX[0:EXP_ALL, qc * P:(qc + 1) * P], CW[:, b.par, qc, :], IDF[:])
                    last.then_inc(cwT_psum, 1)

            def iteration(t):
                nxt = t + 1
                prev = t + (-1)
                for e in range(EXP_ALL):
                    for u in range(4):
                        if t.live:
                            hidden(t, e, 4 * e + u)
                        if u == 1 and e < LAG and prev.live:
                            down(prev, EXP_ALL - LAG + e)
                        if u == 1 and e >= LAG and t.live:
                            down(t, e - LAG)
                    if e == 0 and t.live:
                        prepare(t, EXP_ALL)
                    if nxt.live:
                        prepare(nxt, e)

            everywhere(iteration)(pe)

        @block.scalar
        def _(act):
            act.wait_ge(consts, 16 * NCONST)
            act.wait_ge(weights, 16 * 3)
            nc.scalar.activation(GH[:], GW[:], ACT.Copy).then_inc(wh_ready, 1)

            def prepare(b, s):
                if s == 2:
                    act.wait_ge(xT_psum, b.done(1, 1))
                    if due(before := b.done(2 * EXP_ALL, -2 * EXP_ALL)):
                        act.wait_ge(h3_psum, before)
                    nc.scalar.activation(XH[:, b.par, :], psX[:], ACT.Copy).then_inc(xh_ready, 1)
                if s == 5:
                    act.wait_ge(gate_step, b.done(GATE_STEPS, 2))
                    nc.scalar.activation(GE[:], GE[:], ACT.Exp).then_inc(gate_exp, 1)
                if s == EXP_ALL:
                    act.wait_ge(cwT_psum, b.done(1, 1))
                    if due(before := b.done(EXP_ALL, -EXP_ALL)):
                        act.wait_ge(y_psum, before)
                    nc.scalar.activation(CWT[:, b.par, :], psX[0:EXP_ALL, :], ACT.Copy).then_inc(cwT_ready, 1)

            def hidden(b, e, gl):
                k = 2 * e + gl
                act.wait_ge(h1_psum, b.done(2 * EXP_ALL, k + 1))
                if due(before := b.done(2 * EXP_ALL, k - 3)):
                    act.wait_ge(gl_ready, before)
                nc.scalar.activation(A1[:, (b.par + e) % 2, gl, :], psH[(4 * e + 2 * gl) % RING][:],
                                     ACT.Identity, bias=BIAS[:, 0, gl, e:e + 1]).then_inc(a1_ready, 1)

            def gates(b, e, gl):
                if gl == 0:
                    act.wait_ge(g_clip, b.done(EXP_ALL, e + 1))
                    if due(before := b.done(EXP_ALL, e - 1)):
                        act.wait_ge(gate_done, before)
                    nc.scalar.activation(TH[:, (b.par + e) % 2, :], G[:, (b.par + e) % 2, :], ACT.Tanh,
                                         scale=ALPHA / 2).then_inc(tanh_done, 1)
                else:
                    act.wait_ge(l_clip, b.done(EXP_ALL, e + 1))
                    nc.scalar.activation(L[:, (b.par + e) % 2, :], L[:, (b.par + e) % 2, :], ACT.Identity,
                                         bias=1.0).then_inc(l_plus, 1)

            def weigh(b, e):
                act.wait_ge(y_psum, b.done(EXP_ALL, e + 1))
                if e == 0:
                    act.wait_ge(gate_step, b.done(GATE_STEPS, GATE_STEPS))
                    if due(before := b.done(1, -1)):
                        act.wait_ge(z_ready, before)
                else:
                    if due(before := b.done(SUMS, max(e - 2, 0))):
                        act.wait_ge(summed, before)
                for qc in range(QC):
                    to = ACC[:, b.par, qc, :] if e == 0 else YW[:, e % 2, qc, :]
                    last = nc.scalar.activation(to, psY[:, qc * C:(qc + 1) * C], ACT.Copy, scale=CW[:, b.par, qc, e:e + 1])
                last.then_inc(y_read, 1)

            def iteration(t):
                nxt, prev = t + 1, t + (-1)
                for e in range(EXP_ALL):
                    if not t.live and nxt.live:
                        for m, W in enumerate((W1, W3)):
                            last = nc.scalar.activation(WH[m][:, e], W[:, e].rearrange("p (f g) -> p g f", g=2), ACT.Copy)
                        last.then_inc(wh_ready, 1)
                    if t.live:
                        hidden(t, e, 0)
                        if e > 0:
                            gates(t, e - 1, 0)
                    if e < LAG - 1 and prev.live:
                        weigh(prev, EXP_ALL - LAG + e)
                    if e >= LAG and t.live:
                        weigh(t, e - LAG)
                    if t.live:
                        hidden(t, e, 1)
                        if e > 0:
                            gates(t, e - 1, 1)
                    if e == 0 and t.live:
                        prepare(t, EXP_ALL)
                    if nxt.live:
                        prepare(nxt, e)
                if t.live:
                    gates(t, NE, 0)
                    gates(t, NE, 1)

            everywhere(iteration)(act)

        @block.vector
        def _(dve):
            nc.vector.memset(NHALF[:], -0.5)
            last = nc.vector.memset(CW[:], 1.0)
            last.then_inc(ready, 1)
            dve.wait_ge(consts, 16 * NCONST)
            dve.wait_ge(iota_done, 1)
            dve.wait_ge(wh_ready, 1)
            nc.vector.tensor_tensor(GL[:], GW[:], GH[:].bitcast(F32), ALU.subtract).then_inc(ready, 1)

            def split_weights(e):
                dve.wait_ge(wh_ready, 2 + e)
                for m, W in enumerate((W1, W3)):
                    nc.vector.tensor_tensor(WL[m][:, e], W[:, e].rearrange("p (f g) -> p g f", g=2),
                                            WH[m][:, e].bitcast(F32), ALU.subtract)
                nc.vector.tensor_scalar(W2[:, e], W2[:, e], 0.5, None, ALU.mult).then_inc(split, 1)

            def prepare(b, s):
                def step(n):
                    dve.wait_ge(gate_step, b.done(GATE_STEPS, n))
                if s == (0, 0):
                    for qc in range(QC):
                        last = nc.vector.bn_stats(ST2[:, qc, :], X[:, b.number() * QC + qc, :])
                    last.then_inc(stats2, 1)
                if s == (0, 2):
                    dve.wait_ge(stats2, b.done(1, 1))
                    dve.sem_inc(passed, 1)
                    for qc in range(QC):
                        last = nc.vector.bn_aggr(MV2[:, qc, :], ST2[:, qc, :])
                    last.then_inc(aggr2, 1)
                if s == (1, 4):
                    dve.wait_ge(rstd2, b.done(1, 1))
                    for qc in range(QC):
                        last = nc.vector.tensor_scalar(XN[:, qc, :], X[:, b.number() * QC + qc, :], MV2[:, qc, 0:1],
                                                       RS2[:, qc:qc + 1], ALU.subtract, ALU.mult)
                    last.then_inc(xn_ready, 1)
                if s == (3, 1):
                    dve.wait_ge(xh_ready, b.done(1, 1))
                    nc.vector.tensor_tensor(XL[:, b.par, :], psX[:], XH[:, b.par, :].bitcast(F32),
                                            ALU.subtract).then_inc(xl_ready, 1)
                lg = psX[:, 0:QC * NE].rearrange("p (q e) -> p q e", q=QC)
                if s == (4, 3):
                    dve.wait_ge(logits_psum, b.done(1, 1))
                    nc.vector.tensor_reduce(out=GM[:], in_=lg, axis=AX.X, op=ALU.max).then_inc(gate_step, 1)
                if s == (4, 4):
                    step(1)
                    nc.vector.tensor_tensor(GE[:], lg, GM[:].to_broadcast([P, QC, NE]), ALU.subtract).then_inc(gate_step, 1)
                if s == (5, 3):
                    dve.wait_ge(gate_exp, b.done(1, 1))
                    nc.vector.tensor_reduce(out=GS[:], in_=GE[:], axis=AX.X, op=ALU.add).then_inc(gate_step, 1)
                if s == (5, 4):
                    step(3)
                    nc.vector.reciprocal(GR[:], GS[:]).then_inc(gate_step, 1)
                if s == (6, 0):
                    step(4)
                    nc.vector.tensor_tensor(SC[:], GE[:], GR[:].to_broadcast([P, QC, NE]), ALU.mult).then_inc(gate_step, 1)
                if s == (6, 1):
                    step(5)
                    nc.vector.tensor_tensor(BI[:], SC[:], GB[:].unsqueeze(1).to_broadcast([P, QC, NE]),
                                            ALU.add).then_inc(gate_step, 1)
                if s == (6, 2):
                    dve.wait_ge(gate_step, b.done(GATE_STEPS, 6))
                    dve.sem_inc(passed, 1)
                    for qc in range(QC):
                        last = nc.vector.max(out=TOP[:, qc, :], in_=BI[:, qc, :])
                    last.then_inc(gate_step, 1)
                if s == (6, 3):
                    dve.wait_ge(gate_step, b.done(GATE_STEPS, 7))
                    dve.sem_inc(passed, 1)
                    for qc in range(QC):
                        last = nc.vector.max_index(out=IDX[:, qc, :], in_max=TOP[:, qc, :], in_values=BI[:, qc, :])
                    last.then_inc(gate_step, 1)
                if s == (6, 4):
                    step(8)
                    nc.vector.tensor_copy(IDXF[:], IDX[:, :, 0:TOPK]).then_inc(gate_step, 1)
                if s == (7, 0):
                    step(9)
                    for k in range(TOPK):
                        last = nc.vector.tensor_tensor(PICK[:, k], IOTA[:].unsqueeze(1).to_broadcast([P, QC, NE]),
                                                       IDXF[:, :, k:k + 1].to_broadcast([P, QC, NE]), ALU.is_equal)
                    last.then_inc(gate_step, 1)
                if s == (7, 1):
                    step(10)
                    nc.vector.tensor_tensor(PICK[:, 0], PICK[:, 0], PICK[:, 1], ALU.add).then_inc(gate_step, 1)
                if s == (7, 2):
                    step(11)
                    if due(before := b.done(EXP_ALL, -EXP_ALL)):
                        dve.wait_ge(y_read, before)
                    nc.vector.tensor_tensor(CW[:, b.par, :, 0:NE], PICK[:, 0], SC[:], ALU.mult).then_inc(gate_step, 1)

            def products(b, e, gl):
                T = (G, L)[gl]
                k = 2 * e + gl
                dve.wait_ge(h3_psum, b.done(2 * EXP_ALL, k + 1))
                dve.wait_ge(a1_ready, b.done(2 * EXP_ALL, k + 1))
                if due(before := b.done(EXP_ALL, e - 1)):
                    dve.wait_ge(gate_done if gl == 0 else ha_ready, before)
                nc.vector.scalar_tensor_tensor(out=T[:, (b.par + e) % 2, :], in0=psH[(4 * e + 2 * gl + 1) % RING][:],
                                               scalar=BIAS[:, 1, gl, e:e + 1], in1=A1[:, (b.par + e) % 2, gl, :],
                                               op0=ALU.add, op1=ALU.mult).then_inc(gl_ready, 1)

            def clip(b, e, gl):
                dve.wait_ge(gl_ready, b.done(2 * EXP_ALL, 2 * e + gl + 1))
                if gl == 0:
                    nc.vector.tensor_scalar(G[:, (b.par + e) % 2, :], G[:, (b.par + e) % 2, :], LIMIT, None,
                                            ALU.min).then_inc(g_clip, 1)
                else:
                    nc.vector.tensor_scalar(L[:, (b.par + e) % 2, :], L[:, (b.par + e) % 2, :], LIMIT, -LIMIT,
                                            ALU.min, ALU.max).then_inc(l_clip, 1)

            def gated(b, e):
                dve.wait_ge(tanh_done, b.done(EXP_ALL, e + 1))
                if due(before := b.done(EXP_ALL, e - 1)):
                    dve.wait_ge(ha_ready, before)
                nc.vector.scalar_tensor_tensor(out=GT[:, (b.par + e) % 2, :], in0=TH[:, (b.par + e) % 2, :], scalar=1.0, in1=G[:, (b.par + e) % 2, :],
                                               op0=ALU.add, op1=ALU.mult).then_inc(gate_done, 1)

            def complete(b):
                dve.wait_ge(y_psum, b.done(EXP_ALL, EXP_ALL))
                dve.wait_ge(summed, b.done(SUMS, SUMS))
                nc.vector.tensor_tensor(ACC[:, b.par], psY[:].rearrange("p (q c) -> p q c", q=QC), ACC[:, b.par],
                                        ALU.add).then_inc(y_read, 1)

            def finish(b, s):
                if s == (2, 3):
                    dve.wait_ge(y_read, b.done(EXP_ALL, EXP_ALL))
                    for qc in range(QC):
                        last = nc.vector.bn_stats(ST3[:, qc, :], ACC[:, b.par, qc, :])
                    last.then_inc(stats3, 1)
                if s == (3, 0):
                    dve.wait_ge(stats3, b.done(1, 1))
                    dve.sem_inc(passed, 1)
                    for qc in range(QC):
                        last = nc.vector.bn_aggr(MV3[:, qc, :], ST3[:, qc, :])
                    last.then_inc(aggr3, 1)
                if s == (4, 2):
                    dve.wait_ge(rstd3, b.done(1, 1))
                    if due(before := b.done(1, 0)):
                        dve.wait_ge(x2_ready, before)
                    for qc in range(QC):
                        last = nc.vector.tensor_scalar(Z[:, qc, :], ACC[:, b.par, qc, :], MV3[:, qc, 0:1],
                                                       RS3[:, qc:qc + 1], ALU.subtract, ALU.mult)
                    last.then_inc(z_ready, 1)

            def iteration(t):
                nxt, prev = t + 1, t + (-1)
                for e in range(EXP_ALL):
                    if not t.live and nxt.live:
                        split_weights(e)
                    for k in range(6):
                        if k == 0 and t.live:
                            products(t, e, 0)
                        if k == 1 and e == LAG - 1 and prev.live:
                            complete(prev)
                        if k == 2 and t.live:
                            clip(t, e, 0)
                        if k == 3 and t.live:
                            products(t, e, 1)
                        if k == 4 and e == 0 and prev.live:
                            gated(prev, NE)
                        if k == 4 and t.live and e > 0:
                            gated(t, e - 1)
                        if k == 5 and t.live:
                            clip(t, e, 1)
                        if prev.live:
                            finish(prev, (e, k))
                        if nxt.live:
                            prepare(nxt, (e, k))

            everywhere(iteration)(dve)

        @block.gpsimd
        def _(pool):
            nc.gpsimd.iota(IOTA[:], pattern=[[1, NE]], base=0, channel_multiplier=0,
                           allow_small_or_imprecise_dtypes=True).then_inc(iota_done, 1)
            pool.wait_ge(ready, 1)

            def rsqrt(b, MV, VE, RS, aggr, eps, rstd, free):
                pool.wait_ge(aggr, b.done(1, 1))
                pool.sem_inc(passed, 1)
                nc.gpsimd.tensor_scalar(VE[:], MV[:, :, 1], 1.0, EPS, ALU.mult, ALU.add).then_inc(eps, 1)
                pool.wait_ge(eps, b.done(1, 1))
                if due(before := b.done(1, 0)):
                    pool.wait_ge(free, before)
                nc.gpsimd.tensor_tensor(RS[:], VE[:], NHALF[:], ALU.pow).then_inc(rstd, 1)

            def add(b, e):
                pool.wait_ge(y_read, b.done(EXP_ALL, e + 1))
                if due(before := b.done(SUMS, e - 1)):
                    pool.wait_ge(summed, before)
                nc.gpsimd.tensor_tensor(ACC[:, b.par], ACC[:, b.par], YW[:, e % 2], ALU.add).then_inc(summed, 1)

            def act_out(b, e):
                pool.wait_ge(gate_done, b.done(EXP_ALL, e + 1))
                pool.wait_ge(l_plus, b.done(EXP_ALL, e + 1))
                if due(before := b.done(EXP_ALL, e + 1 - HA_BUFS)):
                    pool.wait_ge(y_psum, before)
                nc.gpsimd.tensor_tensor(HA[:, e % HA_BUFS, :], GT[:, (b.par + e) % 2, :], L[:, (b.par + e) % 2, :], ALU.mult).then_inc(ha_ready, 1)

            def iteration(t):
                nxt, prev = t + 1, t + (-1)
                for e in range(EXP_ALL):
                    if e == 0 and prev.live:
                        act_out(prev, NE)
                    if t.live and e > 0:
                        act_out(t, e - 1)
                    if e < LAG - 1 and prev.live:
                        add(prev, EXP_ALL - LAG + e)
                    if e > LAG and t.live:
                        add(t, e - LAG)
                    if e == 0 and nxt.live:
                        rsqrt(nxt, MV2, VE2, RS2, aggr2, eps2, rstd2, xn_ready)
                    if e == 3 and prev.live:
                        rsqrt(prev, MV3, VE3, RS3, aggr3, eps3, rstd3, z_ready)
                    if e == 5 and prev.live:
                        pool.wait_ge(z_ready, prev.done(1, 1))
                        if due(before := (prev + (-2)).done_par(16)):
                            pool.wait_ge(stored[prev.par], before)
                        nc.gpsimd.tensor_tensor(OUT[:, prev.par], X[:, bass.ds(prev.number() * QC, QC), :], Z[:],
                                                ALU.add).then_inc(x2_ready, 1)

            everywhere(iteration)(pool)


def build(nc, x, wqkvT, chan, bv, cos, sin, perm, ident, gate_wT, gate_b, w1T, w3T, w2T, hb, b2, out):
    ctx = ExitStack()
    with ctx:
        def sb(name, shape):
            return ctx.enter_context(nc.sbuf_tensor(name, shape, F32))

        X = sb("X", [P, B * QC, C])
        W1 = sb("W1", [P, EXP_ALL, 2 * F])
        W3 = sb("W3", [P, EXP_ALL, 2 * F])
        W2 = sb("W2", [P, EXP_ALL, C])
        weights = ctx.enter_context(nc.semaphore("weights_loaded"))

        def load_weights(eng):
            for dst, src in ((W1, w1T), (W3, w3T), (W2, w2T)):
                eng.dma_start(dst[:], src).then_inc(weights, 16)

        attention(nc, x, wqkvT, chan, bv, cos, sin, perm, ident, X, load_weights)
        experts(nc, gate_wT, gate_b, W1, W3, W2, weights, hb, b2, ident, X, out)


def host_constants():
    import numpy as np
    div = np.exp(np.arange(0, D, 2, dtype=np.float32) * np.float32(-np.log(10000.0) / D)).astype(np.float32)
    angle = (np.arange(N, dtype=np.float32)[:, None] * div).astype(np.float32)
    freq = (np.arange(C) % D) // 2
    cos = np.cos(angle.astype(np.float64)).astype(np.float32).T[freq]
    sin = np.sin(angle.astype(np.float64)).astype(np.float32).T[freq]
    perm = np.zeros((C, C), np.float32)
    for j in range(0, C, 2):
        perm[j + 1, j] = -1.0
        perm[j, j + 1] = 1.0
    return dict(cos=cos, sin=sin, perm=perm, ident=np.eye(P, dtype=np.float32))


_INPUTS = ("x", "wqkvT", "chan", "bv", "cos", "sin", "perm", "ident", "gate_wT", "gate_b", "w1T", "w3T", "w2T", "hb", "b2")


def kernel(**inputs):
    import numpy as np
    import concourse.bacc as bacc
    from concourse.bass_utils import run_bass_kernel_spmd

    a = {k: np.asarray(v) for k, v in inputs.items()}
    stack = lambda routed, shared: np.concatenate([a["L0_ffn_" + routed], a["L0_ffn_" + shared][None]])
    both = lambda m: stack("b" + m, "sb" + m).reshape(EXP_ALL, F, 2)
    laid = dict(
        x=a["L0_attn_x"].reshape(B * QC, P, C),
        wqkvT=a["L0_attn_w_qkv"].T,
        chan=np.concatenate([a["L0_attn_b_qkv"].reshape(3, C).T, a["L0_attn_w_lepe"][:, 0, :],
                             a["L0_attn_b_lepe"][:, None]], 1),
        bv=a["L0_attn_b_qkv"][2 * C:],
        gate_wT=a["L0_ffn_gate_w"].T,
        gate_b=a["L0_ffn_gate_b"],
        w1T=stack("w1", "sw1").transpose(2, 0, 1),
        w3T=stack("w3", "sw3").transpose(2, 0, 1),
        w2T=stack("w2", "sw2").transpose(2, 0, 1),
        hb=np.stack([both("1"), both("3")]).transpose(2, 0, 3, 1),
        b2=stack("b2", "sb2"),
        **host_constants(),
    )
    nc = bacc.Bacc("TRN2", target_bir_lowering=False, num_devices=1)
    arrays, args = {}, []
    for name in _INPUTS:
        v = np.ascontiguousarray(laid[name])
        arrays["in_" + name] = v
        args.append(nc.dram_tensor("in_" + name, v.shape, mybir.dt.from_np(v.dtype), kind="ExternalInput").ap())
    args.append(nc.dram_tensor("out_0", (B * QC, P, C), F32, kind="ExternalOutput").ap())
    build(nc, *args)
    r = run_bass_kernel_spmd(nc, [arrays], core_ids=[0])
    return r.results[0]["out_0"].reshape(B, N, C)
```

```python
import concourse.bass as bass
from concourse import mybir
from contextlib import ExitStack

F32 = mybir.dt.float32
F32R = mybir.dt.float32r
BF16 = mybir.dt.bfloat16
U32 = mybir.dt.uint32
U16 = mybir.dt.uint16
ALU = mybir.AluOpType
ACT = mybir.ActivationFunctionType
AX = mybir.AxisListType

P = 128
B, N, C = 16, 512, 128
H, D = 16, 8
QC = N // P
NE, TOPK, F = 8, 2, 128
EXP_ALL = NE + 1
WEIGHTS = 9
BIAS_LOW = 32
ALPHA, LIMIT, EPS = 1.702, 7.0, 1e-5
SCALE = 1.0 / (D ** 0.5)

PARTS = 3
ROWS_QK = PARTS * PARTS * D
ROWS_ALL = ROWS_QK + PARTS
QPARTS = 2 * PARTS - 1
HALF = H // 2
HG = 4
VW = 32
FIRST = 3
ST_BANKS, S_BANKS = 2, 3
TILES = H * QC
SLOTS = H


class Batch:

    def __init__(self, i, c):
        self.i, self.c = i, c

    def __add__(self, k):
        return Batch(self.i, self.c + k)

    def number(self):
        return self.c if isinstance(self.i, int) else self.i * 2 + self.c

    @property
    def par(self):
        return self.c % 2

    @property
    def live(self):
        return not isinstance(self.i, int) or 0 <= self.c < B

    def done(self, per, extra=0):
        if isinstance(self.i, int):
            return self.c * per + extra
        return self.i * (2 * per) + (self.c * per + extra)

    def done_par(self, per):
        return (self.i + (self.c // 2 + 1)) * per


def due(count):
    return not isinstance(count, int) or count > 0


def attention(nc, x_in, wqkvT, chan, ones, rope_cos, rope_sin, perm, ident, X, IDF, BD, load_weights):
    nc.disable_value_cache = True
    es = ExitStack()
    with es:
        def sb(name, shape, dt):
            return es.enter_context(nc.sbuf_tensor(name, shape, dt))

        def sem(name):
            return es.enter_context(nc.semaphore(name))

        WQKV = sb("WQKV", [P, 3 * C], F32)
        PERM = sb("PERM", [P, P], F32)
        IDB = sb("IDB", [P, P], BF16)
        CHAN = sb("CHAN", [P, 7], F32)
        BP1 = sb("BP1", [P, 2], F32)
        COS = sb("COS", [P, N], F32)
        SIN = sb("SIN", [P, N], F32)
        NHALF = sb("NHALF", [P, QC], F32)
        ST0 = sb("ST0", [P, QC, 6], F32)
        MV0 = sb("MV0", [P, QC, 2], F32)
        VE0 = sb("VE0", [P, QC], F32)
        RS0 = sb("RS0", [P, QC], F32)
        XN = sb("XN", [P, QC, C], F32)
        ST1 = sb("ST1", [P, QC, 6], F32)
        MV1 = sb("MV1", [P, QC, 2], F32)
        VE1 = sb("VE1", [P, QC], F32)
        RS1 = sb("RS1", [P, QC], F32)
        SH1 = sb("SH1", [P, QC], F32)
        Y = sb("Y", [P, 2, QC, C], F32)
        Z = sb("Z", [P, QC, C], F32)
        REC = sb("REC", [P, QC, HG], F32)
        MX = sb("MX", [P, QC, H], F32)
        MP = sb("MP", [P, 2, QC, PARTS, HALF], BF16)
        MR = sb("MR", [P, 2, QC, HALF], F32)
        XT = sb("XT", [P, 2, N], F32)
        EXQ = sb("EXQ", [P, 2, N], F32)
        EL = sb("EL", [P, 2, N], F32)
        ROT = sb("ROT", [P, 2, N], F32)
        RES = sb("RES", [P, 2, N], F32)
        PT = sb("PT", [P, 2, PARTS, N], BF16)
        VT = sb("VT", [P, N + 2], F32)
        TAP = sb("TAP", [P, N], F32)
        LP = sb("LP", [P, 2, N], F32)
        MT = sb("MT", [PARTS * HALF, 2, N], BF16)
        QS = [sb(f"QS{i}", [P, H, N], BF16) for i in range(2)]
        KS = [sb(f"KS{i}", [P, H, N], BF16) for i in range(2)]
        V = [sb(f"V{i}", [P, QC, H, VW], F32) for i in range(2)]
        PR = sb("PR", [P, 2, HG, N], F32)
        OT = sb("OT", [P, 2, N], F32)

        psST = [es.enter_context(nc.psum_tensor(f"psST{i}", [P, N], F32)) for i in range(ST_BANKS)]
        psS = [es.enter_context(nc.psum_tensor(f"psS{i}", [P, N], F32)) for i in range(S_BANKS)]
        psPV = es.enter_context(nc.psum_tensor("psPV", [P, N], F32))
        psM = [es.enter_context(nc.psum_tensor(f"psM{i}", [P, N], F32)) for i in range(2)]

        SCR = [nc.dram_tensor(f"scratch_parts{w}", [2, H, QPARTS, D, N], BF16, kind="Internal").ap() for w in range(2)]
        SCM = nc.dram_tensor("scratch_max", [2, 2, PARTS * HALF, N], BF16, kind="Internal").ap()

        consts = sem("consts_loaded")
        passed = sem("passed")
        half_set, zeros_set, ones_set, lead = sem("half_set"), sem("zeros_set"), sem("ones_set"), sem("constants_set")
        x_loaded = [sem(f"x_loaded{i}") for i in range(2)]
        stats0, aggr0, eps0, rstd0, xn_ready = (sem(s) for s in ("stats0", "aggr0", "eps0", "rstd0", "xn_ready"))
        xT_psum, xT_ready = sem("xT_psum"), sem("xT_ready")
        qk_psum = [sem(f"qk_psum{w}") for w in range(2)]
        qk_exp = [sem(f"qk_exp{w}") for w in range(2)]
        qk_min = [sem(f"qk_min{w}") for w in range(2)]
        qk_elu = [sem(f"qk_elu{w}") for w in range(2)]
        rot_psum = [sem(f"rot_psum{w}") for w in range(2)]
        rot_cos = [sem(f"rot_cos{w}") for w in range(2)]
        rot_sin = [sem(f"rot_sin{w}") for w in range(2)]
        rot_sum = [sem(f"rot_sum{w}") for w in range(2)]
        part1 = [sem(f"part1_{w}") for w in range(2)]
        resid = [sem(f"resid{w}") for w in range(2)]
        part2 = [sem(f"part2_{w}") for w in range(2)]
        part3 = [sem(f"part3_{w}") for w in range(2)]
        parts_stored = [sem(f"parts_stored{w}") for w in range(2)]
        stacked = [[sem(f"stacked{p}{h}") for h in range(2)] for p in range(2)]
        s_psum = sem("s_psum")
        s_max = sem("s_max")
        mx_step = [sem(f"max_split_step{h}") for h in range(2)]
        mT_psum = sem("mT_psum")
        mT_ready = sem("mT_ready")
        m_stored = sem("m_stored")
        m_stacked = [[sem(f"m_stacked{p}{h}") for h in range(2)] for p in range(2)]
        st_psum = sem("st_psum")
        st_exp = sem("st_exp")
        pv_done = sem("pv_done")
        ot_ready = sem("ot_ready")
        oT_psum = sem("oT_psum")
        recip = sem("recip")
        o_norm = sem("o_norm")
        v_psum, v_ready = sem("v_psum"), sem("v_ready")
        vT_psum, vT_ready = sem("vT_psum"), sem("vT_ready")
        lepe_mid = sem("lepe_mid")
        tap_ready, tap_added = sem("tap_ready"), sem("tap_added")
        lepeT_psum, y_ready = sem("lepeT_psum"), sem("y_ready")
        stats1, aggr1, eps1, rstd1, shift1, z_ready, x1_ready = (
            sem(s) for s in ("stats1", "aggr1", "eps1", "rstd1", "shift1", "z_ready", "x1_ready"))

        NCONST = 8
        LOADS = 3 * 16 * 2
        MISC = ["xT", "q", "k", "mT1", "O3", "Rq", "Rk", "O0", "lepeT", "mT0", "O1", "vT", "V", "O2"]

        def misc_bank(use):
            return psM[MISC.index(use) % 2]

        READER = {"xT": (2, xT_ready, 1, 1), "mT1": (0, mT_ready, 2, 2), "q": (2, qk_elu[0], 1, 1),
                  "O3": (-1, o_norm, 4, 4), "k": (2, qk_elu[1], 1, 1), "Rq": (2, rot_sin[0], 1, 1),
                  "Rk": (2, rot_sin[1], 1, 1), "O0": (0, o_norm, 4, 1), "lepeT": (-1, y_ready, 1, 1),
                  "mT0": (1, mT_ready, 2, 1), "O1": (0, o_norm, 4, 2), "V": (1, v_ready, 1, 1),
                  "vT": (1, vT_ready, 1, 1), "O2": (0, o_norm, 4, 3)}

        def misc_freed(pe, t, use):
            n = MISC.index(use)
            for back in range(2, 2 * len(MISC), 2):
                turn, m = divmod(n - back, len(MISC))
                of, reader, per, mine = READER[MISC[m]]
                b = t + turn + of
                if b.live:
                    pe.wait_ge(reader, b.done(per, mine))
                    return

        def bank(banks, k):
            return banks[1 if len(banks) == 3 and k == TILES - 1 else k % len(banks)]

        def st_banks(t):
            return psST + psS if isinstance(t.i, int) and t.c == B - 1 else psST

        def tile_before(banks, k):
            if len(banks) == 3 and k in (0, 1, 2, TILES - 1):
                return {0: -4, 1: -1, 2: -2, TILES - 1: TILES - 3}[k]
            return k - len(banks)

        def everywhere(emit):
            def loop(eng):
                for c in range(-3, FIRST):
                    emit(Batch(0, c))
                with eng.Fori(0, (B - 3 - FIRST) // 2) as i:
                    emit(Batch(i, FIRST))
                    emit(Batch(i, FIRST + 1))
                for c in range(B - 3, B + 1):
                    emit(Batch(0, c))
            return loop

        block = es.enter_context(nc.Block())

        @block.sync
        def _(sp):
            def load_x(b):
                if due(before := (b + (-2)).done_par(16)):
                    sp.wait_ge(x_loaded[b.par], before)
                sp.dma_start(X[:, bass.ds(b.number() * QC, QC), :],
                             x_in[bass.ds(b.number() * QC, QC)].rearrange("q p c -> p q c")).then_inc(x_loaded[b.par], 16)

            def iteration(t):
                if (t + 3).live:
                    load_x(t + 3)
                b = t + 1
                if t.live:
                    store_max(t, 1)
                    stack_max(t, 1)
                b2 = t + 2
                if b2.live:
                    for hf in range(2):
                        if due(before := (b2 + (-2)).done_par(LOADS)):
                            sp.wait_ge(stacked[b2.par][hf], before)
                    for a, part in enumerate((part1, part2, part3)):
                        for w in range(2):
                            sp.wait_ge(part[w], b2.done(1, 1))
                            for place in range(a, PARTS if w else QPARTS, PARTS):
                                sp.dma_start(SCR[w][b2.par, :, place], PT[:, w, a, :]).then_inc(parts_stored[w], 16)
                if b.live:
                    store_max(b, 0)
                    stack_max(b, 0)
                if b2.live:
                    stack(t, b2, 0)
                    stack(t, b2, 1)

            def stack(t, b, hf):
                for w in range(2):
                    sp.wait_ge(parts_stored[w], b.done(16 * (PARTS if w else QPARTS), 16 * (PARTS if w else QPARTS)))
                if t.live:
                    sp.wait_ge(st_psum, t.done(64, 32 * (hf + 1)))
                for w, S in enumerate((QS, KS)):
                    for r in range(PARTS):
                        first = 0 if w else r
                        sp.dma_start(S[b.par][24 * r:24 * r + 24, HALF * hf:HALF * hf + HALF, :],
                                     SCR[w][b.par, HALF * hf:HALF * hf + HALF, first:first + PARTS].rearrange(
                                         "h a d n -> (a d) h n")).then_inc(stacked[b.par][hf], 16)

            def store_max(b, hf):
                sp.wait_ge(mT_ready, b.done(2, hf + 1))
                sp.dma_start(SCM[b.par, hf], MT[:, hf, :]).then_inc(m_stored, 16)

            def stack_max(b, hf):
                sp.wait_ge(m_stored, b.done(32, 16 * (hf + 1)))
                sp.dma_start(QS[b.par][ROWS_QK:ROWS_ALL, HALF * hf:HALF * hf + HALF, :],
                             SCM[b.par, hf].rearrange("(a h) n -> a h n", a=PARTS)).then_inc(m_stacked[b.par][hf], 16)

            everywhere(iteration)(sp)

        @block.tensor
        def _(pe):
            pe.wait_ge(consts, 16 * NCONST)
            pe.wait_ge(lead, 2)

            def scores_t(t, h, kc, k):
                if kc == 0 and h % HALF == 0:
                    hf = h // HALF
                    pe.wait_ge(stacked[t.par][hf], t.done_par(LOADS))
                    pe.wait_ge(m_stacked[t.par][hf], t.done_par(16))
                banks = st_banks(t)
                if len(psST) <= k < len(banks):
                    pe.wait_ge(s_max, t.done(TILES, TILES))
                elif due(before := t.done(TILES, tile_before(psST if k < len(psST) else banks, k) + 1)):
                    pe.wait_ge(st_exp, before)
                nc.tensor.matmul(bank(st_banks(t), k)[:], KS[t.par][0:ROWS_ALL, h, kc * P:(kc + 1) * P],
                                 QS[t.par][0:ROWS_ALL, h, :], start=True, stop=True).then_inc(st_psum, 1)

            def scores(b, h, qc, k):
                if qc == 0 and h % HALF == 0:
                    pe.wait_ge(stacked[b.par][h // HALF], b.done_par(LOADS))
                if due(before := b.done(TILES, tile_before(psS, k) + 1)):
                    pe.wait_ge(s_max, before)
                nc.tensor.matmul(bank(psS, k)[:], QS[b.par][0:ROWS_QK, h, qc * P:(qc + 1) * P],
                                 KS[b.par][0:ROWS_QK, h, :], start=True, stop=True).then_inc(s_psum, 1)

            def values(b, s):
                g, kc = divmod(s, QC)
                if s == 0:
                    pe.wait_ge(v_ready, b.done(1, 1))
                if kc == 0:
                    if due(before := b.done(4, g)):
                        pe.wait_ge(ot_ready, before)
                pe.wait_ge(st_exp, b.done(64, 4 * s + 4))
                for j in range(HG):
                    last = nc.tensor.matmul(psPV[VW * j:VW * j + VW, :], V[b.par][:, kc, HG * g + j, :],
                                            PR[:, s % 2, j, :], start=(kc == 0), stop=(kc == QC - 1))
                last.then_inc(pv_done, 1)

            def out_transposes(b, g, use):
                pe.wait_ge(ot_ready, b.done(4, g + 1))
                m = misc_bank(use)
                for qc in range(QC):
                    last = nc.tensor.transpose(m[:, qc * P:(qc + 1) * P], OT[:, g % 2, qc * P:(qc + 1) * P], IDF[:])
                last.then_inc(oT_psum, 1)

            def misc(t, s):
                nxt, prep, prev = t + 1, t + 2, t + (-1)
                if s == 0 and prep.live:
                    misc_freed(pe, t, "xT")
                    pe.wait_ge(xn_ready, prep.done(1, 1))
                    m = misc_bank("xT")
                    for qc in range(QC):
                        last = nc.tensor.transpose(m[:, qc * P:(qc + 1) * P], XN[:, qc, :], IDF[:])
                    last.then_inc(xT_psum, 1)
                if s == 3 and t.live:
                    misc_freed(pe, t, "mT1")
                    max_transposes(t, 1, "mT1")
                if s == 1 and prep.live:
                    misc_freed(pe, t, "q")
                    project(prep, 0, "q")
                if s == 2 and prep.live:
                    misc_freed(pe, t, "k")
                    project(prep, 1, "k")
                if s == 4 and prev.live:
                    misc_freed(pe, t, "O3")
                    out_transposes(prev, 3, "O3")
                if s in (5, 6) and prep.live:
                    w = s - 5
                    use = ("Rq", "Rk")[w]
                    misc_freed(pe, t, use)
                    pe.wait_ge(qk_elu[w], prep.done(1, 1))
                    nc.tensor.matmul(misc_bank(use)[:], PERM[:], EL[:, w, :], start=True, stop=True).then_inc(rot_psum[w], 1)
                if s == 7 and t.live:
                    misc_freed(pe, t, "O0")
                    out_transposes(t, 0, "O0")
                if s == 8 and prev.live:
                    misc_freed(pe, t, "lepeT")
                    pe.wait_ge(tap_added, prev.done(2, 2))
                    m = misc_bank("lepeT")
                    for qc in range(QC):
                        last = nc.tensor.transpose(m[:, qc * P:(qc + 1) * P], LP[:, prev.par, qc * P:(qc + 1) * P], IDF[:])
                    last.then_inc(lepeT_psum, 1)
                if s == 9 and nxt.live:
                    misc_freed(pe, t, "mT0")
                    max_transposes(nxt, 0, "mT0")
                if s == 10 and t.live:
                    misc_freed(pe, t, "O1")
                    out_transposes(t, 1, "O1")
                if s == 11 and nxt.live:
                    misc_freed(pe, t, "vT")
                    pe.wait_ge(xT_ready, nxt.done(1, 1))
                    nc.tensor.matmul(misc_bank("vT")[:], WQKV[:, 2 * C:3 * C], XT[:, nxt.par, :],
                                     start=True, stop=True).then_inc(vT_psum, 1)
                if s == 13 and nxt.live:
                    misc_freed(pe, t, "V")
                    pe.wait_ge(vT_ready, nxt.done(1, 1))
                    m = misc_bank("V")
                    for kc in range(QC):
                        last = nc.tensor.transpose(m[:, kc * P:(kc + 1) * P], VT[:, 1 + kc * P:1 + (kc + 1) * P], IDF[:])
                    last.then_inc(v_psum, 1)
                if s == 14 and t.live:
                    misc_freed(pe, t, "O2")
                    out_transposes(t, 2, "O2")

            def max_transposes(b, hf, use):
                pe.wait_ge(mx_step[hf], b.done(5, 5))
                m = misc_bank(use)[0:PARTS * HALF, 0:N // 2].bitcast(BF16)
                for qc in range(QC):
                    last = nc.tensor.transpose(m[:, qc * P:(qc + 1) * P],
                                               MP[:, hf, qc, :, :].rearrange("p a h -> p (a h)"), IDB[:])
                last.then_inc(mT_psum, 1)

            def project(b, w, use):
                pe.wait_ge(xT_ready, b.done(1, 1))
                nc.tensor.matmul(misc_bank(use)[:], WQKV[:, w * C:(w + 1) * C], XT[:, b.par, :],
                                 start=True, stop=True).then_inc(qk_psum[w], 1)

            def iteration(t):
                nxt, prev = t + 1, t + (-1)
                for s in range(SLOTS):
                    g, kc = divmod(s, QC)
                    for j in range(HG):
                        if t.live:
                            scores_t(t, HG * g + j, kc, 4 * s + j)
                        if nxt.live:
                            scores(nxt, s, j, 4 * s + j)
                        if j == (3 if isinstance(t.i, int) and t.c == B - 1 else 1):
                            if s == 0 and prev.live:
                                values(prev, SLOTS - 1)
                            if s > 0 and t.live:
                                values(t, s - 1)
                    misc(t, s)

            everywhere(iteration)(pe)

        @block.scalar
        def _(act):
            for dst, src in ((IDF[:], ident), (WQKV[:], wqkvT), (CHAN[:], chan), (PERM[:], perm),
                             (COS[:], rope_cos), (SIN[:], rope_sin),
                             *((KS[p][ROWS_QK:ROWS_ALL].rearrange("r h n -> r (h n)").bitcast(U16), ones) for p in range(2))):
                act.dma_start(dst, src).then_inc(consts, 16)
            act.wait_ge(consts, 16 * NCONST)

            def extra(t, s):
                nxt, prep, prev = t + 1, t + 2, t + (-1)
                if s in (0, 4, 8, 12):
                    b, g = (prev, 3) if s == 0 else (t, s // 4 - 1)
                    if b.live:
                        act.wait_ge(pv_done, b.done(16, 4 * g + 4))
                        if due(before := b.done(4, g - 1)):
                            act.wait_ge(oT_psum, before)
                        nc.scalar.activation(OT[:, g % 2, :], psPV[:], ACT.Copy).then_inc(ot_ready, 1)
                if s == 0 and prep.live:
                    act.wait_ge(xT_psum, prep.done(1, 1))
                    if due(before := (prep + (-2)).done(1, 1)):
                        act.wait_ge(vT_psum, before)
                    nc.scalar.activation(XT[:, prep.par, :], misc_bank("xT")[:], ACT.Copy).then_inc(xT_ready, 1)
                if s == 4 and t.live:
                    copy_max(t, 1, "mT1")
                if s in (1, 2) and prep.live:
                    w = s - 1
                    act.wait_ge(qk_psum[w], prep.done(1, 1))
                    if due(before := prep.done(1, 0)):
                        act.wait_ge(qk_elu[w], before)
                    nc.scalar.activation(EXQ[:, w, :], misc_bank("qk"[w])[:], ACT.Exp,
                                         bias=CHAN[:, w:w + 1]).then_inc(qk_exp[w], 1)
                if s in (7, 8) and prep.live:
                    w = s - 7
                    act.wait_ge(rot_sum[w], prep.done(1, 1))
                    if due(before := prep.done(16 * (PARTS if w else QPARTS), 0)):
                        act.wait_ge(parts_stored[w], before)
                    nc.scalar.activation(PT[:, w, 0, :], ROT[:, w, :], ACT.Copy).then_inc(part1[w], 1)
                if s in (9, 10) and prep.live:
                    w = s - 9
                    act.wait_ge(resid[w], prep.done(1, 1))
                    nc.scalar.activation(PT[:, w, 1, :], RES[:, w, :], ACT.Copy).then_inc(part2[w], 1)
                if s == 10 and nxt.live:
                    copy_max(nxt, 0, "mT0")
                if s == 12 and nxt.live:
                    act.wait_ge(vT_psum, nxt.done(1, 1))
                    if due(before := nxt.done(2, 0)):
                        act.wait_ge(tap_added, before)
                    if due(before := nxt.done(1, 0)):
                        act.wait_ge(v_psum, before)
                    nc.scalar.activation(VT[:, 1:N + 1], misc_bank("vT")[:], ACT.Identity,
                                         bias=CHAN[:, 2:3]).then_inc(vT_ready, 1)
                if s == 13 and nxt.live:
                    act.wait_ge(vT_ready, nxt.done(1, 1))
                    if due(before := (nxt + (-2)).done(1, 1)):
                        act.wait_ge(lepeT_psum, before)
                    nc.scalar.activation(LP[:, nxt.par, :], VT[:, 1:N + 1], ACT.Identity,
                                         bias=CHAN[:, 6:7], scale=CHAN[:, 4:5]).then_inc(lepe_mid, 1)

            def copy_max(b, hf, use):
                act.wait_ge(mT_psum, b.done(2, hf + 1))
                if due(before := b.done(32, 16 * (hf + 1) - 32)):
                    act.wait_ge(m_stored, before)
                nc.scalar.activation(MT[:, hf, :], misc_bank(use)[0:PARTS * HALF, 0:N // 2].bitcast(BF16),
                                     ACT.Copy).then_inc(mT_ready, 1)

            def iteration(t):
                if isinstance(t.i, int) and t.c == 0:
                    act.wait_ge(ones_set, 1)
                    load_weights(act)
                for s in range(SLOTS):
                    for j in range(HG):
                        if t.live:
                            k = 4 * s + j
                            act.wait_ge(st_psum, t.done(64, k + 1))
                            if j == 0:
                                if due(before := t.done(16, s - 1)):
                                    act.wait_ge(pv_done, before)
                            nc.scalar.activation(PR[:, s % 2, j, :], bank(st_banks(t), k)[:], ACT.Exp,
                                                 scale=SCALE).then_inc(st_exp, 1)
                    extra(t, s)

            everywhere(iteration)(act)

        @block.vector
        def _(dve):
            nc.vector.memset(VT[:], 0.0).then_inc(lead, 1)
            dve.wait_ge(consts, 16 * NCONST)
            nc.vector.tensor_copy(IDB[:], IDF[:])
            nc.vector.tensor_scalar(BP1[:], CHAN[:, 0:2], 1.0, None, ALU.add).then_inc(lead, 1)
            dve.wait_ge(lead, 2)
            dve.wait_ge(ones_set, 1)

            def elu(b, w, step):
                if step == 0:
                    dve.wait_ge(qk_exp[w], b.done(1, 1))
                    nc.vector.tensor_scalar(EXQ[:, w, :], EXQ[:, w, :], 1.0, None, ALU.min).then_inc(qk_min[w], 1)
                    return
                dve.wait_ge(qk_min[w], b.done(1, 1))
                if due(before := b.done(1, 0)):
                    dve.wait_ge(rot_cos[w], before)
                if due(before := b.done(1, 0)):
                    dve.wait_ge(rot_psum[w], before)
                nc.vector.scalar_tensor_tensor(out=EL[:, w, :], in0=misc_bank("qk"[w])[:], scalar=BP1[:, w:w + 1],
                                               in1=EXQ[:, w, :], op0=ALU.add, op1=ALU.max).then_inc(qk_elu[w], 1)

            def normalise(b, g, use):
                m = misc_bank(use)[:].rearrange("p (q j v) -> p q j v", q=QC, j=HG)
                dve.wait_ge(oT_psum, b.done(4, g + 1))
                if due(before := b.done(4, g)):
                    dve.wait_ge(o_norm, before)
                nc.vector.reciprocal(REC[:], m[:, :, :, D]).then_inc(recip, 1)
                dve.wait_ge(recip, b.done(4, g + 1))
                if g == 0:
                    if due(before := b.done(1, -1)):
                        dve.wait_ge(z_ready, before)
                y = Y[:, b.par, :, g * HG * D:(g + 1) * HG * D].rearrange("p q (j d) -> p q j d", j=HG)
                nc.vector.tensor_tensor(y, m[:, :, :, 0:D], REC[:].unsqueeze(3).to_broadcast([P, QC, HG, D]),
                                        ALU.mult).then_inc(o_norm, 1)

            def extra(t, s, j):
                nxt, prep, prev, far = t + 1, t + 2, t + (-1), t + 3
                if s in (2, 3) and j > 1 and prep.live:
                    elu(prep, s - 2, j - 2)
                if s == 5 and j == 3 and prev.live:
                    normalise(prev, 3, "O3")
                if s in (6, 7) and j == 0 and prep.live:
                    w = s - 6
                    dve.wait_ge(rot_psum[w], prep.done(1, 1))
                    if due(before := prep.done(1, 0)):
                        dve.wait_ge(part3[w], before)
                    nc.vector.tensor_tensor(RES[:, w, :], misc_bank(("Rq", "Rk")[w])[:], SIN[:],
                                            ALU.mult).then_inc(rot_sin[w], 1)
                if s == 8 and j == 1 and t.live:
                    normalise(t, 0, "O0")
                if s == 9 and j == 1 and prev.live:
                    dve.wait_ge(lepeT_psum, prev.done(1, 1))
                    dve.wait_ge(o_norm, prev.done(4, 4))
                    nc.vector.tensor_tensor(Y[:, prev.par], misc_bank("lepeT")[:].rearrange("p (q c) -> p q c", q=QC),
                                            Y[:, prev.par],
                                            ALU.add).then_inc(y_ready, 1)
                if s == 11 and j == 1 and t.live:
                    normalise(t, 1, "O1")
                if s == 14 and j == 1 and nxt.live:
                    dve.wait_ge(v_psum, nxt.done(1, 1))
                    if due(before := (nxt + (-1)).done(16, 0)):
                        dve.wait_ge(pv_done, before)
                    nc.vector.tensor_copy(V[nxt.par][:, :, :, 0:D],
                                          misc_bank("V")[:].rearrange("p (q h d) -> p q h d", q=QC, h=H)).then_inc(v_ready, 1)
                if s == 15 and j == 1 and t.live:
                    normalise(t, 2, "O2")
                if s == 10 and j == 1 and prev.live:
                    dve.wait_ge(y_ready, prev.done(1, 1))
                    for qc in range(QC):
                        last = nc.vector.bn_stats(ST1[:, qc, :], Y[:, prev.par, qc, :])
                    last.then_inc(stats1, 1)
                if s == 11 and j == 3 and prev.live:
                    dve.wait_ge(stats1, prev.done(1, 1))
                    if due(before := prev.done(1, 0)):
                        dve.wait_ge(z_ready, before)
                    dve.sem_inc(passed, 1)
                    for qc in range(QC):
                        last = nc.vector.bn_aggr(MV1[:, qc, :], ST1[:, qc, :])
                    last.then_inc(aggr1, 1)
                if s == 1 and j == 1 and far.live:
                    dve.wait_ge(x_loaded[far.par], far.done_par(16))
                    for qc in range(QC):
                        last = nc.vector.bn_stats(ST0[:, qc, :], X[:, far.number() * QC + qc, :])
                    last.then_inc(stats0, 1)
                if s == 3 and j == 2 and far.live:
                    dve.wait_ge(stats0, far.done(1, 1))
                    dve.sem_inc(passed, 1)
                    for qc in range(QC):
                        last = nc.vector.bn_aggr(MV0[:, qc, :], ST0[:, qc, :])
                    last.then_inc(aggr0, 1)
                if s == 13 and j in (0, 2) and far.live:
                    if j == 0:
                        dve.wait_ge(rstd0, far.done(1, 1))
                        if due(before := far.done(1, 0)):
                            dve.wait_ge(xT_psum, before)
                    for qc in (j, j + 1):
                        last = nc.vector.tensor_scalar(XN[:, qc, :], X[:, far.number() * QC + qc, :], MV0[:, qc, 0:1],
                                                       RS0[:, qc:qc + 1], ALU.subtract, ALU.mult)
                    if j == 2:
                        last.then_inc(xn_ready, 1)

            def iteration(t):
                nxt = t + 1
                for s in range(SLOTS):
                    for j in range(HG):
                        if nxt.live:
                            k = 4 * s + j
                            dve.wait_ge(s_psum, nxt.done(64, k + 1))
                            if s % HALF == 0 and j == 0:
                                if due(before := nxt.done(5, 0)):
                                    dve.wait_ge(mx_step[s // HALF], before)
                            nc.vector.tensor_reduce(out=MX[:, j, s:s + 1], in_=bank(psS, k)[:], axis=AX.X,
                                                    op=ALU.max).then_inc(s_max, 1)
                        extra(t, s, j)

            everywhere(iteration)(dve)

        @block.gpsimd
        def _(pool):
            nc.gpsimd.memset(NHALF[:], -0.5).then_inc(half_set, 1)
            nc.gpsimd.memset(BD[:], 0.0)
            for p in range(2):
                last = nc.gpsimd.memset(V[p][:], 0.0)
            last.then_inc(zeros_set, 1)
            pool.wait_ge(half_set, 1)
            pool.wait_ge(zeros_set, 1)
            for p in range(2):
                last = nc.gpsimd.memset(V[p][:, :, :, D:D + 1], 1.0)
            last.then_inc(ones_set, 1)
            pool.wait_ge(consts, 16 * NCONST)
            pool.wait_ge(lead, 2)

            def split_max(b, hf):
                m = MX[:, :, HALF * hf:HALF * hf + HALF]
                n = [MP[:, hf, :, a, :] for a in range(PARTS)]
                r = MR[:, hf]
                pool.wait_ge(s_max, b.done(64, 32 * (hf + 1)))
                if due(before := b.done(2, hf - 1)):
                    pool.wait_ge(mT_psum, before)
                pool.sem_inc(passed, 1)
                step = mx_step[hf]
                nc.gpsimd.tensor_scalar(n[0], m, -1.0, 0.0, ALU.mult, ALU.add).then_inc(step, 1)
                pool.wait_ge(step, b.done(5, 1))
                nc.gpsimd.tensor_tensor(r, m, n[0], ALU.add).then_inc(step, 1)
                pool.wait_ge(step, b.done(5, 2))
                pool.sem_inc(passed, 1)
                nc.gpsimd.tensor_scalar(n[1], r, -1.0, 0.0, ALU.mult, ALU.add).then_inc(step, 1)
                pool.wait_ge(step, b.done(5, 3))
                nc.gpsimd.tensor_tensor(r, r, n[1], ALU.add).then_inc(step, 1)
                pool.wait_ge(step, b.done(5, 4))
                pool.sem_inc(passed, 1)
                nc.gpsimd.tensor_scalar(n[2], r, -1.0, 0.0, ALU.mult, ALU.add).then_inc(step, 1)

            def rsqrt(b, MV, VE, RS, aggr, eps, rstd, free):
                pool.wait_ge(aggr, b.done(1, 1))
                pool.sem_inc(passed, 1)
                nc.gpsimd.tensor_scalar(VE[:], MV[:, :, 1], 1.0, EPS, ALU.mult, ALU.add).then_inc(eps, 1)
                pool.wait_ge(eps, b.done(1, 1))
                if due(before := b.done(1, 0)):
                    pool.wait_ge(free, before)
                nc.gpsimd.tensor_tensor(RS[:], VE[:], NHALF[:], ALU.pow).then_inc(rstd, 1)

            def lepe(b):
                pool.wait_ge(lepe_mid, b.done(1, 1))
                for tap, (first, w) in enumerate(((0, 3), (2, 5))):
                    if due(before := b.done(2, tap)):
                        pool.wait_ge(tap_added, before)
                    pool.sem_inc(passed, 1)
                    nc.gpsimd.tensor_scalar(TAP[:], VT[:, first:first + N], CHAN[:, w:w + 1], 0.0, ALU.mult,
                                            ALU.add).then_inc(tap_ready, 1)
                    pool.wait_ge(tap_ready, b.done(2, tap + 1))
                    nc.gpsimd.tensor_tensor(LP[:, b.par, :], LP[:, b.par, :], TAP[:], ALU.add).then_inc(tap_added, 1)

            def iteration(t):
                nxt, prep, prev, far = t + 1, t + 2, t + (-1), t + 3
                if t.live:
                    split_max(t, 1)
                if far.live:
                    rsqrt(far, MV0, VE0, RS0, aggr0, eps0, rstd0, xn_ready)
                if t.live:
                    lepe(t)
                if prep.live:
                    for w in range(2):
                        pool.wait_ge(qk_elu[w], prep.done(1, 1))
                        if due(before := prep.done(1, 0)):
                            pool.wait_ge(resid[w], before)
                        nc.gpsimd.tensor_tensor(ROT[:, w, :], EL[:, w, :], COS[:], ALU.mult).then_inc(rot_cos[w], 1)
                    for w in range(2):
                        pool.wait_ge(rot_cos[w], prep.done(1, 1))
                        pool.wait_ge(rot_sin[w], prep.done(1, 1))
                        nc.gpsimd.tensor_tensor(ROT[:, w, :], ROT[:, w, :], RES[:, w, :], ALU.add).then_inc(rot_sum[w], 1)
                if nxt.live:
                    split_max(nxt, 0)
                for w in range(2):
                    if prep.live:
                        pool.wait_ge(part1[w], prep.done(1, 1))
                        nc.gpsimd.tensor_tensor(RES[:, w, :], ROT[:, w, :], PT[:, w, 0, :], ALU.subtract).then_inc(resid[w], 1)
                if prep.live:
                    for w in range(2):
                        pool.wait_ge(part2[w], prep.done(1, 1))
                        nc.gpsimd.tensor_tensor(PT[:, w, 2, :], RES[:, w, :], PT[:, w, 1, :], ALU.subtract).then_inc(part3[w], 1)
                if prev.live:
                    rsqrt(prev, MV1, VE1, RS1, aggr1, eps1, rstd1, z_ready)
                    pool.wait_ge(rstd1, prev.done(1, 1))
                    nc.gpsimd.tensor_tensor(SH1[:], MV1[:, :, 0], RS1[:], ALU.mult).then_inc(shift1, 1)
                    pool.wait_ge(shift1, prev.done(2, 1))
                    pool.sem_inc(passed, 1)
                    nc.gpsimd.tensor_scalar(SH1[:], SH1[:], -1.0, 0.0, ALU.mult, ALU.add).then_inc(shift1, 1)
                    pool.wait_ge(shift1, prev.done(2, 2))
                    if due(before := prev.done(1, 0)):
                        pool.wait_ge(x1_ready, before)
                    pool.wait_ge(y_ready, prev.done(1, 1))
                    pool.sem_inc(passed, 1)
                    for qc in range(QC):
                        last = nc.gpsimd.tensor_scalar(Z[:, qc, :], Y[:, prev.par, qc, :], RS1[:, qc:qc + 1],
                                                       SH1[:, qc:qc + 1], ALU.mult, ALU.add)
                    last.then_inc(z_ready, 1)
                    pool.wait_ge(z_ready, prev.done(1, 1))
                    x = X[:, bass.ds(prev.number() * QC, QC), :]
                    nc.gpsimd.tensor_tensor(x, x, Z[:], ALU.add).then_inc(x1_ready, 1)

            everywhere(iteration)(pool)


def experts(nc, W1, W3, W2, GW, GB, BIAS, BD, weights, X, IDF, out):
    es = ExitStack()
    with es:
        def sb(name, shape, dt):
            return es.enter_context(nc.sbuf_tensor(name, shape, dt))

        def sem(name):
            return es.enter_context(nc.semaphore(name))

        LOW = BIAS_LOW
        LAG = 3
        HA_BUFS = 3
        WH = [sb(f"WH{m}", [P, EXP_ALL, 2, F], F32R) for m in range(2)]
        WL = [sb(f"WL{m}", [P, EXP_ALL, 2, F], F32R) for m in range(2)]
        GHL = sb("GHL", [P, 2, NE], F32R)
        LG = sb("LG", [P, QC, NE], F32)
        IOTA = sb("IOTA", [P, NE], F32)
        NHALF = sb("NHALFB", [P, QC], F32)

        ST2 = sb("ST2", [P, QC, 6], F32)
        MV2 = sb("MV2", [P, QC, 2], F32)
        VE2 = sb("VE2", [P, QC], F32)
        RS2 = sb("RS2", [P, QC], F32)
        ST3 = sb("ST3", [P, QC, 6], F32)
        MV3 = sb("MV3", [P, QC, 2], F32)
        VE3 = sb("VE3", [P, QC], F32)
        RS3 = sb("RS3", [P, QC], F32)
        XN = sb("XNB", [P, QC, C], F32)
        XH = sb("XH", [P, 2, N], F32R)
        XL = sb("XL", [P, 2, N], F32R)
        GM = sb("GM", [P, QC, 1], F32)
        GE = sb("GE", [P, QC, NE], F32)
        GS = sb("GS", [P, QC, 1], F32)
        GR = sb("GR", [P, QC, 1], F32)
        SC = sb("SC", [P, QC, NE], F32)
        BI = sb("BI", [P, QC, NE], F32)
        TOP = sb("TOP", [P, QC, 8], F32)
        IDX = sb("IDX", [P, QC, 8], U32)
        IDXF = sb("IDXF", [P, QC, TOPK], F32)
        PICK = sb("PICK", [P, TOPK, QC, NE], F32)
        CW = sb("CW", [P, 2, QC, EXP_ALL], F32)
        CWX = sb("CWX", [P, 2, QC, LOW + EXP_ALL], F32R)
        CWT = sb("CWT", [LOW + EXP_ALL, 2, N], F32R)
        BX = sb("BX", [LOW + EXP_ALL, C], F32R)
        BHIGH = sb("BHIGH", [LOW + EXP_ALL, C], F32R)
        A1 = sb("A1", [P, 2, 2, N], F32)
        G = sb("G", [P, 2, N], F32)
        L = sb("L", [P, 2, N], F32)
        TH = sb("TH", [P, 2, N], F32)
        GT = sb("GT", [P, 2, N], F32)
        HA = sb("HA", [P, HA_BUFS, N], F32)
        YW = sb("YW", [P, 2, QC, C], F32)
        ACC = sb("ACC", [P, 2, QC, C], F32)
        Z = sb("ZB", [P, QC, C], F32)
        OUT = sb("OUT", [P, 2, QC, C], F32)

        RING = 6
        psH = [es.enter_context(nc.psum_tensor(f"psH{i}", [P, N], F32)) for i in range(RING)]
        psY = es.enter_context(nc.psum_tensor("psY", [P, N], F32))
        psX = es.enter_context(nc.psum_tensor("psX", [P, N], F32))

        ready = sem("gate_split")
        split = sem("weights_split")
        passed = sem("passedB")
        iota_done, wh_ready = sem("iota_done"), sem("weights_high")
        stats2, aggr2, eps2, rstd2, xn_ready = (sem(s) for s in ("stats2", "aggr2", "eps2", "rstd2", "xn2_ready"))
        stats3, aggr3, eps3, rstd3, z_ready = (sem(s) for s in ("stats3", "aggr3", "eps3", "rstd3", "z3_ready"))
        xT_psum, xh_ready, xl_ready = sem("xT2_psum"), sem("xh_ready"), sem("xl_ready")
        logits_psum = sem("logits_psum")
        gate_step = sem("gate_step")
        gate_exp = sem("gate_exp")
        cwT_psum, cwT_ready = sem("cwT_psum"), sem("cwT_ready")
        h1_psum, h3_psum = sem("h1_psum"), sem("h3_psum")
        a1_ready, gl_ready = sem("a1_ready"), sem("gl_ready")
        g_clip, l_clip = sem("g_clipped"), sem("l_clipped")
        tanh_done, l_plus = sem("tanh_done"), sem("l_plus")
        gate_done, ha_ready = sem("gate_done"), sem("ha_ready")
        y_psum, y_read = sem("y_psum"), sem("y_read")
        summed = sem("summed")
        x2_ready = sem("x2_ready")
        stored = [sem(f"stored{i}") for i in range(2)]
        GATE_STEPS = 16
        SUMS = NE - 1
        SPLIT_BEFORE = ((1, 4), (3, 1), (4, 3), (5, 3))
        FIRST_SPLITS = len(SPLIT_BEFORE)

        def everywhere(emit):
            def loop(eng):
                for c in range(-1, FIRST):
                    emit(Batch(0, c))
                with eng.Fori(0, (B - 1 - FIRST) // 2) as i:
                    emit(Batch(i, FIRST))
                    emit(Batch(i, FIRST + 1))
                for c in (B - 1, B):
                    emit(Batch(0, c))
            return loop

        block = es.enter_context(nc.Block())

        @block.sync
        def _(sp):
            def iteration(t):
                b = t + (-1)
                if b.live:
                    sp.wait_ge(x2_ready, b.done(1, 1))
                    sp.dma_start(out[bass.ds(b.number() * QC, QC)].rearrange("q p c -> p q c"),
                                 OUT[:, b.par]).then_inc(stored[b.par], 16)

            everywhere(iteration)(sp)
            for p in range(2):
                sp.wait_ge(stored[p], 16 * (B // 2))

        @block.tensor
        def _(pe):
            pe.wait_ge(ready, 2)

            def hidden(b, e, u):
                m, gl = u % 2, u // 2 % 2
                if isinstance(b.i, int) and b.c == 0 and u % 4 == 0:
                    pe.wait_ge(split, e + 1)
                if u == 0:
                    pe.wait_ge(xh_ready, b.done(1, 1))
                    pe.wait_ge(xl_ready, b.done(1, 1))
                v = u - RING
                if due(before := b.done(2 * EXP_ALL, v // 4 * 2 + v % 4 // 2 + 1)):
                    pe.wait_ge(gl_ready if m else a1_ready, before)
                ps = psH[u % RING]
                nc.tensor.matmul(ps[:], WH[m][:, e, gl, :], XH[:, b.par, :], start=True, stop=False)
                nc.tensor.matmul(ps[:], WH[m][:, e, gl, :], XL[:, b.par, :], start=False, stop=False)
                nc.tensor.matmul(ps[:], WL[m][:, e, gl, :], XH[:, b.par, :], start=False,
                                 stop=True).then_inc(h3_psum if m else h1_psum, 1)

            def down(b, e):
                pe.wait_ge(ha_ready, b.done(EXP_ALL, e + 1))
                if due(before := b.done(EXP_ALL, e)):
                    pe.wait_ge(y_read, before)
                shared = e == NE
                if shared:
                    pe.wait_ge(cwT_ready, b.done(1, 1))
                for qc in range(QC):
                    last = nc.tensor.matmul(psY[:, qc * P:(qc + 1) * P], HA[:, e % HA_BUFS, qc * P:(qc + 1) * P],
                                            W2[:, e, :], start=True, stop=not shared)
                    if shared:
                        last = nc.tensor.matmul(psY[:, qc * P:(qc + 1) * P], CWT[:, b.par, qc * P:(qc + 1) * P],
                                                BX[:], start=False, stop=True)
                last.then_inc(y_psum, 1)

            def prepare(b, s):
                if s == 2:
                    pe.wait_ge(xn_ready, b.done(1, 1))
                    if due(before := b.done(1, 0)):
                        pe.wait_ge(cwT_ready, before)
                    for qc in range(QC):
                        last = nc.tensor.transpose(psX[:, qc * P:(qc + 1) * P], XN[:, qc, :], IDF[:])
                    last.then_inc(xT_psum, 1)
                if s == 4:
                    pe.wait_ge(xh_ready, b.done(1, 1))
                    pe.wait_ge(xl_ready, b.done(1, 1))
                    for qc in range(QC):
                        o = psX[:, qc * 2 * NE:(qc + 1) * 2 * NE]
                        nc.tensor.matmul(o, XH[:, b.par, qc * P:(qc + 1) * P], GHL[:].rearrange("p a e -> p (a e)"),
                                         start=True, stop=False)
                        last = nc.tensor.matmul(o[:, 0:NE], XL[:, b.par, qc * P:(qc + 1) * P], GHL[:, 0],
                                                start=False, stop=True)
                    last.then_inc(logits_psum, 1)
                if s == EXP_ALL:
                    pe.wait_ge(gate_step, b.done(GATE_STEPS, GATE_STEPS))
                    pe.sem_inc(passed, 1)
                    for qc in range(QC):
                        last = nc.tensor.transpose(psX[0:LOW + EXP_ALL, qc * P:(qc + 1) * P], CWX[:, b.par, qc, :].bitcast(F32), IDF[:])
                    last.then_inc(cwT_psum, 1)

            def iteration(t):
                nxt = t + 1
                prev = t + (-1)
                for e in range(EXP_ALL):
                    for u in range(4):
                        if t.live:
                            hidden(t, e, 4 * e + u)
                        if u == 1 and e < LAG and prev.live:
                            down(prev, EXP_ALL - LAG + e)
                        if u == 1 and e >= LAG and t.live:
                            down(t, e - LAG)
                    if e == 0 and t.live:
                        prepare(t, EXP_ALL)
                    if nxt.live:
                        prepare(nxt, e)

            everywhere(iteration)(pe)

        @block.scalar
        def _(act):
            act.wait_ge(weights, 16 * WEIGHTS)
            nc.scalar.activation(BHIGH[:], BD[:], ACT.Copy)
            nc.scalar.activation(GHL[:, 0], GW[:], ACT.Copy).then_inc(wh_ready, 1)

            def prepare(b, s):
                if s == 2:
                    act.wait_ge(xT_psum, b.done(1, 1))
                    if due(before := b.done(2 * EXP_ALL, -2 * EXP_ALL)):
                        act.wait_ge(h3_psum, before)
                    nc.scalar.activation(XH[:, b.par, :], psX[:], ACT.Copy).then_inc(xh_ready, 1)
                if s == 5:
                    act.wait_ge(gate_step, b.done(GATE_STEPS, 3))
                    nc.scalar.activation(GE[:], GE[:], ACT.Exp).then_inc(gate_exp, 1)
                if s == EXP_ALL:
                    act.wait_ge(cwT_psum, b.done(1, 1))
                    if due(before := b.done(EXP_ALL, -EXP_ALL)):
                        act.wait_ge(y_psum, before)
                    nc.scalar.activation(CWT[:, b.par, :], psX[0:LOW + EXP_ALL, :], ACT.Copy).then_inc(cwT_ready, 1)

            def hidden(b, e, gl):
                k = 2 * e + gl
                act.wait_ge(h1_psum, b.done(2 * EXP_ALL, k + 1))
                if due(before := b.done(2 * EXP_ALL, k - 3)):
                    act.wait_ge(gl_ready, before)
                nc.scalar.activation(A1[:, (b.par + e) % 2, gl, :], psH[(4 * e + 2 * gl) % RING][:],
                                     ACT.Identity, bias=BIAS[:, 0, gl, e:e + 1]).then_inc(a1_ready, 1)

            def gates(b, e, gl):
                if gl == 0:
                    act.wait_ge(g_clip, b.done(EXP_ALL, e + 1))
                    if due(before := b.done(EXP_ALL, e - 1)):
                        act.wait_ge(gate_done, before)
                    nc.scalar.activation(TH[:, (b.par + e) % 2, :], G[:, (b.par + e) % 2, :], ACT.Tanh,
                                         scale=ALPHA / 2).then_inc(tanh_done, 1)
                else:
                    act.wait_ge(l_clip, b.done(EXP_ALL, e + 1))
                    nc.scalar.activation(L[:, (b.par + e) % 2, :], L[:, (b.par + e) % 2, :], ACT.Identity,
                                         bias=1.0).then_inc(l_plus, 1)

            def weigh(b, e):
                act.wait_ge(y_psum, b.done(EXP_ALL, e + 1))
                if e == 0:
                    act.wait_ge(gate_step, b.done(GATE_STEPS, GATE_STEPS))
                    if due(before := b.done(1, -1)):
                        act.wait_ge(z_ready, before)
                else:
                    if due(before := b.done(SUMS, max(e - 2, 0))):
                        act.wait_ge(summed, before)
                for qc in range(QC):
                    to = ACC[:, b.par, qc, :] if e == 0 else YW[:, e % 2, qc, :]
                    last = nc.scalar.activation(to, psY[:, qc * C:(qc + 1) * C], ACT.Copy, scale=CW[:, b.par, qc, e:e + 1])
                last.then_inc(y_read, 1)

            def iteration(t):
                nxt, prev = t + 1, t + (-1)
                for e in range(EXP_ALL):
                    if not t.live and nxt.live:
                        for m, W in enumerate((W1, W3)):
                            last = nc.scalar.activation(WH[m][:, e], W[:, e].rearrange("p (f g) -> p g f", g=2), ACT.Copy)
                        last.then_inc(wh_ready, 1)
                    if t.live:
                        hidden(t, e, 0)
                        if e > 0:
                            gates(t, e - 1, 0)
                    if e < LAG - 1 and prev.live:
                        weigh(prev, EXP_ALL - LAG + e)
                    if e >= LAG and t.live:
                        weigh(t, e - LAG)
                    if t.live:
                        hidden(t, e, 1)
                        if e > 0:
                            gates(t, e - 1, 1)
                    if e == 0 and t.live:
                        prepare(t, EXP_ALL)
                    if nxt.live:
                        prepare(nxt, e)
                if t.live:
                    gates(t, NE, 0)
                    gates(t, NE, 1)

            everywhere(iteration)(act)

        @block.vector
        def _(dve):
            nc.vector.memset(NHALF[:], -0.5)
            nc.vector.memset(CWX[:].bitcast(F32), 0.0)
            last = nc.vector.memset(CW[:], 1.0)
            last.then_inc(ready, 1)
            dve.wait_ge(iota_done, 1)
            dve.wait_ge(wh_ready, 1)
            nc.vector.tensor_copy(BX[0:LOW], BD[0:LOW])
            nc.vector.tensor_tensor(BX[LOW:LOW + EXP_ALL], BD[LOW:LOW + EXP_ALL], BHIGH[LOW:LOW + EXP_ALL].bitcast(F32),
                                    ALU.subtract)
            nc.vector.tensor_tensor(GHL[:, 1], GW[:], GHL[:, 0].bitcast(F32), ALU.subtract).then_inc(ready, 1)

            def split_weights(e):
                dve.wait_ge(wh_ready, 2 + e)
                for m, W in enumerate((W1, W3)):
                    nc.vector.tensor_tensor(WL[m][:, e], W[:, e].rearrange("p (f g) -> p g f", g=2),
                                            WH[m][:, e].bitcast(F32), ALU.subtract)
                nc.vector.tensor_scalar(W2[:, e], W2[:, e], 0.5, None, ALU.mult).then_inc(split, 1)

            def prepare(b, s):
                def step(n):
                    dve.wait_ge(gate_step, b.done(GATE_STEPS, n))
                if s == (0, 0):
                    for qc in range(QC):
                        last = nc.vector.bn_stats(ST2[:, qc, :], X[:, b.number() * QC + qc, :])
                    last.then_inc(stats2, 1)
                if s == (0, 2):
                    dve.wait_ge(stats2, b.done(1, 1))
                    dve.sem_inc(passed, 1)
                    for qc in range(QC):
                        last = nc.vector.bn_aggr(MV2[:, qc, :], ST2[:, qc, :])
                    last.then_inc(aggr2, 1)
                if s == (1, 4):
                    dve.wait_ge(rstd2, b.done(1, 1))
                    for qc in range(QC):
                        last = nc.vector.tensor_scalar(XN[:, qc, :], X[:, b.number() * QC + qc, :], MV2[:, qc, 0:1],
                                                       RS2[:, qc:qc + 1], ALU.subtract, ALU.mult)
                    last.then_inc(xn_ready, 1)
                if s == (3, 1):
                    dve.wait_ge(xh_ready, b.done(1, 1))
                    nc.vector.tensor_tensor(XL[:, b.par, :], psX[:], XH[:, b.par, :].bitcast(F32),
                                            ALU.subtract).then_inc(xl_ready, 1)
                if s == (4, 2):
                    dve.wait_ge(logits_psum, b.done(1, 1))
                    nc.vector.tensor_reduce(out=LG[:], in_=psX[:, 0:QC * 2 * NE].rearrange("p (q a e) -> p q e a", q=QC, a=2),
                                            axis=AX.X, op=ALU.add).then_inc(gate_step, 1)
                if s == (4, 3):
                    step(1)
                    nc.vector.tensor_reduce(out=GM[:], in_=LG[:], axis=AX.X, op=ALU.max).then_inc(gate_step, 1)
                if s == (4, 4):
                    step(2)
                    nc.vector.tensor_tensor(GE[:], LG[:], GM[:].to_broadcast([P, QC, NE]), ALU.subtract).then_inc(gate_step, 1)
                if s == (5, 3):
                    dve.wait_ge(gate_exp, b.done(1, 1))
                    nc.vector.tensor_reduce(out=GS[:], in_=GE[:], axis=AX.X, op=ALU.add).then_inc(gate_step, 1)
                if s == (5, 4):
                    step(4)
                    nc.vector.reciprocal(GR[:], GS[:]).then_inc(gate_step, 1)
                if s == (6, 0):
                    step(5)
                    nc.vector.tensor_tensor(SC[:], GE[:], GR[:].to_broadcast([P, QC, NE]), ALU.mult).then_inc(gate_step, 1)
                if s == (6, 1):
                    step(6)
                    nc.vector.tensor_tensor(BI[:], SC[:], GB[:].unsqueeze(1).to_broadcast([P, QC, NE]),
                                            ALU.add).then_inc(gate_step, 1)
                if s == (6, 2):
                    dve.wait_ge(gate_step, b.done(GATE_STEPS, 7))
                    dve.sem_inc(passed, 1)
                    for qc in range(QC):
                        last = nc.vector.max(out=TOP[:, qc, :], in_=BI[:, qc, :])
                    last.then_inc(gate_step, 1)
                if s == (6, 3):
                    dve.wait_ge(gate_step, b.done(GATE_STEPS, 8))
                    dve.sem_inc(passed, 1)
                    for qc in range(QC):
                        last = nc.vector.max_index(out=IDX[:, qc, :], in_max=TOP[:, qc, :], in_values=BI[:, qc, :])
                    last.then_inc(gate_step, 1)
                if s == (6, 4):
                    step(9)
                    nc.vector.tensor_copy(IDXF[:], IDX[:, :, 0:TOPK]).then_inc(gate_step, 1)
                if s == (7, 0):
                    step(10)
                    for k in range(TOPK):
                        last = nc.vector.tensor_tensor(PICK[:, k], IOTA[:].unsqueeze(1).to_broadcast([P, QC, NE]),
                                                       IDXF[:, :, k:k + 1].to_broadcast([P, QC, NE]), ALU.is_equal)
                    last.then_inc(gate_step, 1)
                if s == (7, 1):
                    step(11)
                    nc.vector.tensor_tensor(PICK[:, 0], PICK[:, 0], PICK[:, 1], ALU.add).then_inc(gate_step, 1)
                if s == (7, 2):
                    step(12)
                    if due(before := b.done(EXP_ALL, -EXP_ALL)):
                        dve.wait_ge(y_read, before)
                    nc.vector.tensor_tensor(CW[:, b.par, :, 0:NE], PICK[:, 0], SC[:], ALU.mult).then_inc(gate_step, 1)
                if s == (7, 3):
                    step(13)
                    if due(before := b.done(1, -1)):
                        dve.wait_ge(cwT_psum, before)
                    nc.vector.tensor_copy(CWX[:, b.par, :, 0:EXP_ALL], CW[:, b.par]).then_inc(gate_step, 1)
                if s == (7, 4):
                    step(14)
                    nc.vector.tensor_tensor(CWX[:, b.par, :, EXP_ALL:2 * EXP_ALL], CW[:, b.par],
                                            CWX[:, b.par, :, 0:EXP_ALL].bitcast(F32), ALU.subtract).then_inc(gate_step, 1)
                if s == (7, 5):
                    nc.vector.tensor_copy(CWX[:, b.par, :, LOW:LOW + EXP_ALL], CW[:, b.par]).then_inc(gate_step, 1)

            def products(b, e, gl):
                T = (G, L)[gl]
                k = 2 * e + gl
                dve.wait_ge(h3_psum, b.done(2 * EXP_ALL, k + 1))
                dve.wait_ge(a1_ready, b.done(2 * EXP_ALL, k + 1))
                if due(before := b.done(EXP_ALL, e - 1)):
                    dve.wait_ge(gate_done if gl == 0 else ha_ready, before)
                nc.vector.scalar_tensor_tensor(out=T[:, (b.par + e) % 2, :], in0=psH[(4 * e + 2 * gl + 1) % RING][:],
                                               scalar=BIAS[:, 1, gl, e:e + 1], in1=A1[:, (b.par + e) % 2, gl, :],
                                               op0=ALU.add, op1=ALU.mult).then_inc(gl_ready, 1)

            def clip(b, e, gl):
                dve.wait_ge(gl_ready, b.done(2 * EXP_ALL, 2 * e + gl + 1))
                if gl == 0:
                    nc.vector.tensor_scalar(G[:, (b.par + e) % 2, :], G[:, (b.par + e) % 2, :], LIMIT, None,
                                            ALU.min).then_inc(g_clip, 1)
                else:
                    nc.vector.tensor_scalar(L[:, (b.par + e) % 2, :], L[:, (b.par + e) % 2, :], LIMIT, -LIMIT,
                                            ALU.min, ALU.max).then_inc(l_clip, 1)

            def gated(b, e):
                dve.wait_ge(tanh_done, b.done(EXP_ALL, e + 1))
                if due(before := b.done(EXP_ALL, e - 1)):
                    dve.wait_ge(ha_ready, before)
                nc.vector.scalar_tensor_tensor(out=GT[:, (b.par + e) % 2, :], in0=TH[:, (b.par + e) % 2, :], scalar=1.0, in1=G[:, (b.par + e) % 2, :],
                                               op0=ALU.add, op1=ALU.mult).then_inc(gate_done, 1)

            def complete(b):
                dve.wait_ge(y_psum, b.done(EXP_ALL, EXP_ALL))
                dve.wait_ge(summed, b.done(SUMS, SUMS))
                nc.vector.tensor_tensor(ACC[:, b.par], psY[:].rearrange("p (q c) -> p q c", q=QC), ACC[:, b.par],
                                        ALU.add).then_inc(y_read, 1)

            def finish(b, s):
                if s == (2, 3):
                    dve.wait_ge(y_read, b.done(EXP_ALL, EXP_ALL))
                    for qc in range(QC):
                        last = nc.vector.bn_stats(ST3[:, qc, :], ACC[:, b.par, qc, :])
                    last.then_inc(stats3, 1)
                if s == (3, 0):
                    dve.wait_ge(stats3, b.done(1, 1))
                    dve.sem_inc(passed, 1)
                    for qc in range(QC):
                        last = nc.vector.bn_aggr(MV3[:, qc, :], ST3[:, qc, :])
                    last.then_inc(aggr3, 1)
                if s == (4, 2):
                    dve.wait_ge(rstd3, b.done(1, 1))
                    if due(before := b.done(1, 0)):
                        dve.wait_ge(x2_ready, before)
                    for qc in range(QC):
                        last = nc.vector.tensor_scalar(Z[:, qc, :], ACC[:, b.par, qc, :], MV3[:, qc, 0:1],
                                                       RS3[:, qc:qc + 1], ALU.subtract, ALU.mult)
                    last.then_inc(z_ready, 1)

            def iteration(t):
                nxt, prev = t + 1, t + (-1)
                if not t.live and nxt.live:
                    done = 0
                    for place in ((e, k) for e in range(EXP_ALL) for k in range(6)):
                        if done < FIRST_SPLITS and place in SPLIT_BEFORE:
                            split_weights(done)
                            done += 1
                        prepare(nxt, place)
                    return
                for e in range(EXP_ALL):
                    if isinstance(t.i, int) and t.c == 0 and e + FIRST_SPLITS < EXP_ALL:
                        split_weights(e + FIRST_SPLITS)
                    for k in range(6):
                        if k == 0 and t.live:
                            products(t, e, 0)
                        if k == 1 and e == LAG - 1 and prev.live:
                            complete(prev)
                        if k == 2 and t.live:
                            clip(t, e, 0)
                        if k == 3 and t.live:
                            products(t, e, 1)
                        if k == 4 and e == 0 and prev.live:
                            gated(prev, NE)
                        if k == 4 and t.live and e > 0:
                            gated(t, e - 1)
                        if k == 5 and t.live:
                            clip(t, e, 1)
                        if prev.live:
                            finish(prev, (e, k))
                        if nxt.live:
                            prepare(nxt, (e, k))

            everywhere(iteration)(dve)

        @block.gpsimd
        def _(pool):
            nc.gpsimd.iota(IOTA[:], pattern=[[1, NE]], base=0, channel_multiplier=0,
                           allow_small_or_imprecise_dtypes=True).then_inc(iota_done, 1)
            pool.wait_ge(ready, 1)

            def rsqrt(b, MV, VE, RS, aggr, eps, rstd, free):
                pool.wait_ge(aggr, b.done(1, 1))
                pool.sem_inc(passed, 1)
                nc.gpsimd.tensor_scalar(VE[:], MV[:, :, 1], 1.0, EPS, ALU.mult, ALU.add).then_inc(eps, 1)
                pool.wait_ge(eps, b.done(1, 1))
                if due(before := b.done(1, 0)):
                    pool.wait_ge(free, before)
                nc.gpsimd.tensor_tensor(RS[:], VE[:], NHALF[:], ALU.pow).then_inc(rstd, 1)

            def add(b, e):
                pool.wait_ge(y_read, b.done(EXP_ALL, e + 1))
                if due(before := b.done(SUMS, e - 1)):
                    pool.wait_ge(summed, before)
                nc.gpsimd.tensor_tensor(ACC[:, b.par], ACC[:, b.par], YW[:, e % 2], ALU.add).then_inc(summed, 1)

            def act_out(b, e):
                pool.wait_ge(gate_done, b.done(EXP_ALL, e + 1))
                pool.wait_ge(l_plus, b.done(EXP_ALL, e + 1))
                if due(before := b.done(EXP_ALL, e + 1 - HA_BUFS)):
                    pool.wait_ge(y_psum, before)
                nc.gpsimd.tensor_tensor(HA[:, e % HA_BUFS, :], GT[:, (b.par + e) % 2, :], L[:, (b.par + e) % 2, :], ALU.mult).then_inc(ha_ready, 1)

            def iteration(t):
                nxt, prev = t + 1, t + (-1)
                for e in range(EXP_ALL):
                    if e == 0 and nxt.live:
                        rsqrt(nxt, MV2, VE2, RS2, aggr2, eps2, rstd2, xn_ready)
                    if e == 3 and prev.live:
                        rsqrt(prev, MV3, VE3, RS3, aggr3, eps3, rstd3, z_ready)
                    if e == 0 and prev.live:
                        act_out(prev, NE)
                    if t.live and e > 0:
                        act_out(t, e - 1)
                    if e < LAG - 1 and prev.live:
                        add(prev, EXP_ALL - LAG + e)
                    if e > LAG and t.live:
                        add(t, e - LAG)
                    if e == 5 and prev.live:
                        pool.wait_ge(z_ready, prev.done(1, 1))
                        if due(before := (prev + (-2)).done_par(16)):
                            pool.wait_ge(stored[prev.par], before)
                        nc.gpsimd.tensor_tensor(OUT[:, prev.par], X[:, bass.ds(prev.number() * QC, QC), :], Z[:],
                                                ALU.add).then_inc(x2_ready, 1)

            everywhere(iteration)(pool)


def build(nc, x, wqkvT, chan, ones, cos, sin, perm, ident, gate_wT, gate_b, w1T, w3T, w2T, hb, b2, out):
    ctx = ExitStack()
    with ctx:
        def sb(name, shape):
            return ctx.enter_context(nc.sbuf_tensor(name, shape, F32))

        X = sb("X", [P, B * QC, C])
        W1 = sb("W1", [P, EXP_ALL, 2 * F])
        W3 = sb("W3", [P, EXP_ALL, 2 * F])
        W2 = sb("W2", [P, EXP_ALL, C])
        IDF = sb("IDF", [P, P])
        GW = sb("GW", [P, NE])
        GB = sb("GB", [P, NE])
        BIAS = sb("BIAS", [P, 2, 2, EXP_ALL])
        BD = sb("BD", [BIAS_LOW + EXP_ALL, C])
        weights = ctx.enter_context(nc.semaphore("weights_loaded"))

        def load_weights(eng):
            for dst, src in ((GW, gate_wT), (BIAS, hb), (BD[0:EXP_ALL], b2),
                             (BD[EXP_ALL:2 * EXP_ALL], b2), (BD[BIAS_LOW:], b2), (GB, gate_b.unsqueeze(0).to_broadcast([P, NE])),
                             (W1, w1T), (W3, w3T), (W2, w2T)):
                eng.dma_start(dst[:], src).then_inc(weights, 16)

        attention(nc, x, wqkvT, chan, ones, cos, sin, perm, ident, X, IDF, BD, load_weights)
        experts(nc, W1, W3, W2, GW, GB, BIAS, BD, weights, X, IDF, out)


def host_constants():
    import numpy as np
    div = np.exp(np.arange(0, D, 2, dtype=np.float32) * np.float32(-np.log(10000.0) / D)).astype(np.float32)
    angle = (np.arange(N, dtype=np.float32)[:, None] * div).astype(np.float32)
    freq = (np.arange(C) % D) // 2
    cos = np.cos(angle.astype(np.float64)).astype(np.float32).T[freq]
    sin = np.sin(angle.astype(np.float64)).astype(np.float32).T[freq]
    perm = np.zeros((C, C), np.float32)
    for j in range(0, C, 2):
        perm[j + 1, j] = -1.0
        perm[j, j + 1] = 1.0
    return dict(cos=cos, sin=sin, perm=perm, ident=np.eye(P, dtype=np.float32))


_INPUTS = ("x", "wqkvT", "chan", "ones", "cos", "sin", "perm", "ident", "gate_wT", "gate_b", "w1T", "w3T", "w2T", "hb", "b2")


def kernel(**inputs):
    import numpy as np
    import concourse.bacc as bacc
    from concourse.bass_utils import run_bass_kernel_spmd

    a = {k: np.asarray(v) for k, v in inputs.items()}
    stack = lambda routed, shared: np.concatenate([a["L0_ffn_" + routed], a["L0_ffn_" + shared][None]])
    both = lambda m: stack("b" + m, "sb" + m).reshape(EXP_ALL, F, 2)
    laid = dict(
        x=a["L0_attn_x"].reshape(B * QC, P, C),
        wqkvT=a["L0_attn_w_qkv"].T,
        chan=np.concatenate([a["L0_attn_b_qkv"].reshape(3, C).T, a["L0_attn_w_lepe"][:, 0, :],
                             a["L0_attn_b_lepe"][:, None]], 1),
        ones=np.full((PARTS, H * N), 0x3F80, np.uint16),
        gate_wT=a["L0_ffn_gate_w"].T,
        gate_b=a["L0_ffn_gate_b"],
        w1T=stack("w1", "sw1").transpose(2, 0, 1),
        w3T=stack("w3", "sw3").transpose(2, 0, 1),
        w2T=stack("w2", "sw2").transpose(2, 0, 1),
        hb=np.stack([both("1"), both("3")]).transpose(2, 0, 3, 1),
        b2=stack("b2", "sb2"),
        **host_constants(),
    )
    nc = bacc.Bacc("TRN2", target_bir_lowering=False, num_devices=1)
    arrays, args = {}, []
    for name in _INPUTS:
        v = np.ascontiguousarray(laid[name])
        arrays["in_" + name] = v
        args.append(nc.dram_tensor("in_" + name, v.shape, mybir.dt.from_np(v.dtype), kind="ExternalInput").ap())
    args.append(nc.dram_tensor("out_0", (B * QC, P, C), F32, kind="ExternalOutput").ap())
    build(nc, *args)
    r = run_bass_kernel_spmd(nc, [arrays], core_ids=[0])
    return r.results[0]["out_0"].reshape(B, N, C)
```
